# Optimizing a Trainium2 kernel written in Bass

```python
import numpy as np
import jax
import jax.numpy as jnp

def _softmax(x, axis=-1):
    return jax.nn.softmax(x, axis=axis)
def _gelu(x):
    return jax.nn.gelu(x, approximate=True)
def _silu(x):
    return jax.nn.silu(x)
def _sigmoid(x):
    return jax.nn.sigmoid(x)
def _layernorm(x, axis=-1, eps=1e-5):
    m = jnp.mean(x, axis=axis, keepdims=True)
    v = jnp.var(x, axis=axis, keepdims=True)
    return (x - m) / jnp.sqrt(v + eps)
def _scatter_add(tgt, idx, src, axis=0):
    return tgt.at[idx].add(src)
def _segment_sum(src, seg, n):
    return jax.ops.segment_sum(src, seg, n)

kernel_name = 'mk_conv_seq_d2_conv_nchw64_120fea'

def setup_inputs(seed: int = 0):
    np.random.seed(seed)
    _w = jnp.asarray
    def _rec_inputs():
        import jax
        import jax.numpy as jnp
        _gk = jax.random.key(seed)
        x = 0.000266 + 1 * jax.random.normal(jax.random.fold_in(_gk, 1), (16, 64, 128, 128), jnp.float32)
        return x
    x = _rec_inputs()
    def _L0_conv_setup():
        import jax, jax.numpy as jnp
        import numpy as np
        B, C, IN_SIZE, OUT_SIZE = (16, 64, 128, 128)
        LRELU_UP = 2
        FILTER_SIZE = 6
        UP_FACTOR = int(np.ceil(max(IN_SIZE, OUT_SIZE) * LRELU_UP / IN_SIZE))
        DN_FACTOR = int(np.ceil(max(IN_SIZE, OUT_SIZE) * LRELU_UP / OUT_SIZE))
        GAIN = np.float32(np.sqrt(2.0))
        SLOPE = 0.2

        def _firwin(numtaps, cutoff, width, fs):
            nyq = 0.5 * fs
            cn = cutoff / nyq
            atten = 2.285 * (numtaps - 1) * np.pi * (width / nyq) + 7.95
            if atten > 50:
                beta = 0.1102 * (atten - 8.7)
            elif atten > 21:
                beta = 0.5842 * (atten - 21) ** 0.4 + 0.07886 * (atten - 21)
            else:
                beta = 0.0
            m = np.arange(numtaps) - (numtaps - 1) / 2.0
            h = cn * np.sinc(cn * m) * np.kaiser(numtaps, beta)
            h = h / h.sum()
            return h.astype(np.float64)

        def _make_filter(taps, size):
            h = _firwin(taps, size / 2.0001, size, size)
            return jnp.asarray(np.outer(h, h), dtype=jnp.float32)

        def _conv_same(y, f):
            k = f.shape[0]
            lo = (k - 1) // 2
            hi = k - 1 - lo
            return jax.lax.conv_general_dilated(y, f[None, None, :, :], window_strides=(1, 1), padding=((lo, hi), (lo, hi)), dimension_numbers=('NCHW', 'OIHW', 'NCHW'))
        key = jax.random.key(seed)
        x = jax.random.normal(key, (B, C, IN_SIZE, IN_SIZE), dtype=jnp.float32)
        bias = jnp.zeros((1, C, 1, 1), dtype=jnp.float32)
        up_filter = _make_filter(FILTER_SIZE * UP_FACTOR, IN_SIZE)
        dn_filter = _make_filter(FILTER_SIZE * DN_FACTOR, OUT_SIZE)
        return {'x': x, 'bias': bias, 'up_filter': up_filter, 'dn_filter': dn_filter}
    _L0_conv_all = _L0_conv_setup()
    _L0_conv_in = {k: v for k, v in _L0_conv_all.items() if k in ('bias', 'up_filter', 'dn_filter', )}
    del _L0_conv_all

    def _L1_conv_setup():
        import jax, jax.numpy as jnp
        import numpy as np
        from jax import lax
        C = 64
        EPS = 1e-06

        def ln2d(x, w, b):
            mean = x.mean(axis=(2, 3), keepdims=True)
            var = ((x - mean) ** 2).mean(axis=(2, 3), keepdims=True)
            return (x - mean) / jnp.sqrt(var + EPS) * w + b

        def pw(x, w, b):
            return jnp.einsum('nihw,oi->nohw', x, w) + b[None, :, None, None]

        def dwconv3(x, w, b):
            y = lax.conv_general_dilated(x, w, window_strides=(1, 1), padding='SAME', feature_group_count=x.shape[1], dimension_numbers=('NCHW', 'OIHW', 'NCHW'))
            return y + b[None, :, None, None]

        def simple_gate(x):
            x1, x2 = jnp.split(x, 2, axis=1)
            return x1 * x2
        key = jax.random.key(seed)
        ks = jax.random.split(key, 16)
        s = 0.05
        return {'x': jax.random.normal(ks[0], (8, C, 256, 256), jnp.float32), 'ln1_w': jnp.ones((1, C, 1, 1), jnp.float32), 'ln1_b': jnp.zeros((1, C, 1, 1), jnp.float32), 'pw1_w': jax.random.normal(ks[1], (2 * C, C), jnp.float32) * s, 'pw1_b': jnp.zeros((2 * C,), jnp.float32), 'dw_w': jax.random.normal(ks[2], (2 * C, 1, 3, 3), jnp.float32) * s, 'dw_b': jnp.zeros((2 * C,), jnp.float32), 'sca_w': jax.random.normal(ks[3], (C, C), jnp.float32) * s, 'sca_b': jnp.zeros((C,), jnp.float32), 'pw2_w': jax.random.normal(ks[4], (C, C), jnp.float32) * s, 'pw2_b': jnp.zeros((C,), jnp.float32), 'ln2_w': jnp.ones((1, C, 1, 1), jnp.float32), 'ln2_b': jnp.zeros((1, C, 1, 1), jnp.float32), 'pw3_w': jax.random.normal(ks[5], (2 * C, C), jnp.float32) * s, 'pw3_b': jnp.zeros((2 * C,), jnp.float32), 'pw4_w': jax.random.normal(ks[6], (C, C), jnp.float32) * s, 'pw4_b': jnp.zeros((C,), jnp.float32), 'beta1': jax.random.normal(ks[7], (1, C, 1, 1), jnp.float32) * 0.1, 'beta2': jax.random.normal(ks[8], (1, C, 1, 1), jnp.float32) * 0.1}
    _L1_conv_all = _L1_conv_setup()
    _L1_conv_in = {k: v for k, v in _L1_conv_all.items() if k in ('ln1_w', 'ln1_b', 'pw1_w', 'pw1_b', 'dw_w', 'dw_b', 'sca_w', 'sca_b', 'pw2_w', 'pw2_b', 'ln2_w', 'ln2_b', 'pw3_w', 'pw3_b', 'pw4_w', 'pw4_b', 'beta1', 'beta2', )}
    del _L1_conv_all

    return {
        "x": x,
        "L0_conv_bias": _L0_conv_in["bias"],
        "L0_conv_up_filter": _L0_conv_in["up_filter"],
        "L0_conv_dn_filter": _L0_conv_in["dn_filter"],
        "L1_conv_ln1_w": _L1_conv_in["ln1_w"],
        "L1_conv_ln1_b": _L1_conv_in["ln1_b"],
        "L1_conv_pw1_w": _L1_conv_in["pw1_w"],
        "L1_conv_pw1_b": _L1_conv_in["pw1_b"],
        "L1_conv_dw_w": _L1_conv_in["dw_w"],
        "L1_conv_dw_b": _L1_conv_in["dw_b"],
        "L1_conv_sca_w": _L1_conv_in["sca_w"],
        "L1_conv_sca_b": _L1_conv_in["sca_b"],
        "L1_conv_pw2_w": _L1_conv_in["pw2_w"],
        "L1_conv_pw2_b": _L1_conv_in["pw2_b"],
        "L1_conv_ln2_w": _L1_conv_in["ln2_w"],
        "L1_conv_ln2_b": _L1_conv_in["ln2_b"],
        "L1_conv_pw3_w": _L1_conv_in["pw3_w"],
        "L1_conv_pw3_b": _L1_conv_in["pw3_b"],
        "L1_conv_pw4_w": _L1_conv_in["pw4_w"],
        "L1_conv_pw4_b": _L1_conv_in["pw4_b"],
        "L1_conv_beta1": _L1_conv_in["beta1"],
        "L1_conv_beta2": _L1_conv_in["beta2"],
    }

def reference(x, L0_conv_bias, L0_conv_up_filter, L0_conv_dn_filter, L1_conv_ln1_w, L1_conv_ln1_b, L1_conv_pw1_w, L1_conv_pw1_b, L1_conv_dw_w, L1_conv_dw_b, L1_conv_sca_w, L1_conv_sca_b, L1_conv_pw2_w, L1_conv_pw2_b, L1_conv_ln2_w, L1_conv_ln2_b, L1_conv_pw3_w, L1_conv_pw3_b, L1_conv_pw4_w, L1_conv_pw4_b, L1_conv_beta1, L1_conv_beta2):
    import jax
    import jax.numpy as jnp
    def _L0_conv_ref(x, bias, up_filter, dn_filter):
        import jax, jax.numpy as jnp
        import numpy as np
        B, C, IN_SIZE, OUT_SIZE = (16, 64, 128, 128)
        LRELU_UP = 2
        FILTER_SIZE = 6
        UP_FACTOR = int(np.ceil(max(IN_SIZE, OUT_SIZE) * LRELU_UP / IN_SIZE))
        DN_FACTOR = int(np.ceil(max(IN_SIZE, OUT_SIZE) * LRELU_UP / OUT_SIZE))
        GAIN = np.float32(np.sqrt(2.0))
        SLOPE = 0.2

        def _firwin(numtaps, cutoff, width, fs):
            nyq = 0.5 * fs
            cn = cutoff / nyq
            atten = 2.285 * (numtaps - 1) * np.pi * (width / nyq) + 7.95
            if atten > 50:
                beta = 0.1102 * (atten - 8.7)
            elif atten > 21:
                beta = 0.5842 * (atten - 21) ** 0.4 + 0.07886 * (atten - 21)
            else:
                beta = 0.0
            m = np.arange(numtaps) - (numtaps - 1) / 2.0
            h = cn * np.sinc(cn * m) * np.kaiser(numtaps, beta)
            h = h / h.sum()
            return h.astype(np.float64)

        def _make_filter(taps, size):
            h = _firwin(taps, size / 2.0001, size, size)
            return jnp.asarray(np.outer(h, h), dtype=jnp.float32)

        def _conv_same(y, f):
            k = f.shape[0]
            lo = (k - 1) // 2
            hi = k - 1 - lo
            return jax.lax.conv_general_dilated(y, f[None, None, :, :], window_strides=(1, 1), padding=((lo, hi), (lo, hi)), dimension_numbers=('NCHW', 'OIHW', 'NCHW'))
        b, c, h, w = x.shape
        y = (x + bias).reshape(b * c, 1, h, w)
        y = jnp.repeat(jnp.repeat(y, UP_FACTOR, axis=2), UP_FACTOR, axis=3)
        y = _conv_same(y, up_filter)
        y = jnp.where(y >= 0, y, SLOPE * y) * GAIN
        y = _conv_same(y, dn_filter)
        n, _, hh, ww = y.shape
        y = y.reshape(n, 1, hh // DN_FACTOR, DN_FACTOR, ww // DN_FACTOR, DN_FACTOR).mean(axis=(3, 5))
        return y.reshape(b, c, hh // DN_FACTOR, ww // DN_FACTOR)

    def _L1_conv_ref(x, ln1_w, ln1_b, pw1_w, pw1_b, dw_w, dw_b, sca_w, sca_b, pw2_w, pw2_b, ln2_w, ln2_b, pw3_w, pw3_b, pw4_w, pw4_b, beta1, beta2):
        import jax, jax.numpy as jnp
        import numpy as np
        from jax import lax
        C = 64
        EPS = 1e-06

        def ln2d(x, w, b):
            mean = x.mean(axis=(2, 3), keepdims=True)
            var = ((x - mean) ** 2).mean(axis=(2, 3), keepdims=True)
            return (x - mean) / jnp.sqrt(var + EPS) * w + b

        def pw(x, w, b):
            return jnp.einsum('nihw,oi->nohw', x, w) + b[None, :, None, None]

        def dwconv3(x, w, b):
            y = lax.conv_general_dilated(x, w, window_strides=(1, 1), padding='SAME', feature_group_count=x.shape[1], dimension_numbers=('NCHW', 'OIHW', 'NCHW'))
            return y + b[None, :, None, None]

        def simple_gate(x):
            x1, x2 = jnp.split(x, 2, axis=1)
            return x1 * x2
        y = ln2d(x, ln1_w, ln1_b)
        y = pw(y, pw1_w, pw1_b)
        y = dwconv3(y, dw_w, dw_b)
        y = simple_gate(y)
        s = y.mean(axis=(2, 3), keepdims=True)
        w = jax.nn.sigmoid(pw(s, sca_w, sca_b))
        y = y * w
        y = pw(y, pw2_w, pw2_b)
        x = x + beta1 * y
        y2 = ln2d(x, ln2_w, ln2_b)
        y2 = pw(y2, pw3_w, pw3_b)
        y2 = simple_gate(y2)
        y2 = pw(y2, pw4_w, pw4_b)
        return x + beta2 * y2

    def _gn(v, G=32, eps=1e-5):
        B_, C_, H_, W_ = v.shape
        g = v.reshape(B_, G, C_ // G, H_, W_)
        m = jnp.mean(g, axis=(2, 3, 4), keepdims=True)
        s = jnp.var(g, axis=(2, 3, 4), keepdims=True)
        return ((g - m) / jnp.sqrt(s + eps)).reshape(v.shape)

    def _ln_c(v, eps=1e-6):
        m = jnp.mean(v, axis=1, keepdims=True)
        s = jnp.var(v, axis=1, keepdims=True)
        return (v - m) / jnp.sqrt(s + eps)

    def _ln_t(v, eps=1e-5):
        m = jnp.mean(v, axis=-1, keepdims=True)
        s = jnp.var(v, axis=-1, keepdims=True)
        return (v - m) / jnp.sqrt(s + eps)

    def _to_tokens(v):
        B_, C_, H_, W_ = v.shape
        return v.reshape(B_, C_, H_ * W_).transpose(0, 2, 1)
    def _from_tokens(t, like):
        B_, C_, H_, W_ = like.shape
        return t.transpose(0, 2, 1).reshape(B_, C_, H_, W_)

    x = _L0_conv_ref(x, L0_conv_bias, L0_conv_up_filter, L0_conv_dn_filter)
    x = _L1_conv_ref(x, L1_conv_ln1_w, L1_conv_ln1_b, L1_conv_pw1_w, L1_conv_pw1_b, L1_conv_dw_w, L1_conv_dw_b, L1_conv_sca_w, L1_conv_sca_b, L1_conv_pw2_w, L1_conv_pw2_b, L1_conv_ln2_w, L1_conv_ln2_b, L1_conv_pw3_w, L1_conv_pw3_b, L1_conv_pw4_w, L1_conv_pw4_b, L1_conv_beta1, L1_conv_beta2)
    return x


_drawn_inputs = setup_inputs


def setup_inputs(seed=0):
    import zlib

    import numpy as np

    out = dict(_drawn_inputs(seed))
    spreads = {'L0_conv_bias': (0.0, 0.1),
     'L1_conv_ln1_w': (1.0, 0.6),
     'L1_conv_ln1_b': (0.0, 0.8),
     'L1_conv_pw1_b': (0.0, 0.8),
     'L1_conv_dw_b': (0.0, 0.8),
     'L1_conv_sca_b': (0.0, 0.8),
     'L1_conv_pw2_b': (0.0, 0.641),
     'L1_conv_ln2_w': (1.0, 0.6),
     'L1_conv_ln2_b': (0.0, 0.8),
     'L1_conv_pw3_b': (0.0, 0.8),
     'L1_conv_pw4_b': (0.0, 0.567)}
    factors = {'L1_conv_pw1_w': 8.0,
     'L1_conv_dw_w': 8.0,
     'L1_conv_sca_w': 8.0,
     'L1_conv_pw2_w': 8.0,
     'L1_conv_pw3_w': 5.352,
     'L1_conv_pw4_w': 5.415,
     'L1_conv_beta1': 3.43,
     'L1_conv_beta2': 3.631}
    for name, (base, spread) in spreads.items():
        noise = np.random.default_rng([zlib.crc32(name.encode()), seed]).standard_normal(out[name].shape)
        drawn = base * np.exp(spread * noise) if base else spread * noise
        out[name] = jnp.asarray(drawn.astype(out[name].dtype))
    for name, factor in factors.items():
        out[name] = (out[name] * factor).astype(out[name].dtype)
    return out
```

```python
from contextlib import ExitStack

import concourse.bass as bass
from concourse import mybir

F32 = mybir.dt.float32
F32R = mybir.dt.float32r
I32 = mybir.dt.int32
ALU = mybir.AluOpType
ACT = mybir.ActivationFunctionType
AX = mybir.AxisListType

P = 128
UP = 2 * P
TAPS = 12
PAD_LO = (TAPS - 1) // 2
PAIRS = TAPS + 1
CENTRE = TAPS // 2 - 1
SLOPE = 0.2
GAIN = float(2.0 ** 0.5)
RANK1_TOL = 2.0 ** -21
LN_EPS = 1e-6
NARROW = P // 2 + 3
SECOND = P - NARROW


def build(nc, x, bias, up_filter, dn_filter, ln1_w, ln1_b, pw1_w, pw1_b, dw_w, dw_b, sca_w, sca_b,
          pw2_w, pw2_b, ln2_w, ln2_b, pw3_w, pw3_b, pw4_w, pw4_b, beta1, beta2, out):
    B, C, H, W = x.shape
    assert (C, H, W) == (64, P, P) and tuple(up_filter.shape) == (TAPS, TAPS)
    IMGS = B * C
    STEPS = IMGS // 2
    HW = H * W
    HALF = HW // 2
    CHUNK_ROWS = 16
    CHUNKS = H // CHUNK_ROWS
    BLOCK_ROWS = 4
    BLOCKS = CHUNK_ROWS // BLOCK_ROWS
    N = BLOCK_ROWS * W
    TAIL = HALF // N

    l0_out = nc.dram_tensor("l0_out", [IMGS, H, W], F32, kind="Internal").ap()
    x_rows = x.rearrange("b c h w -> h (b c) w")
    l0_rows = l0_out.rearrange("n h w -> h n w")
    l0_half = l0_out.rearrange("n (s r) w -> s n (r w)", s=2)
    out_half = out.rearrange("b c (s r) w -> s (b c) (r w)", s=2)

    with ExitStack() as ctx:
        def sb(name, shape, dt=F32):
            return ctx.enter_context(nc.sbuf_tensor(name, shape, dt))

        def sem(name):
            return ctx.enter_context(nc.semaphore(name))

        bank = [ctx.enter_context(nc.psum_tensor(f"bank{i}", [P, 512], F32)) for i in range(8)]

        filt = sb("filt", [P, 2, TAPS, TAPS])
        ratio = sb("ratio", [P, 2, TAPS, TAPS])
        resid = sb("resid", [P, 2, TAPS, TAPS])
        recip = sb("recip", [P, 2])
        factor = sb("factor", [P, 4, TAPS + 2])
        pairs = sb("pairs", [P, 4, PAIRS])
        fits = sb("fits", [P, 4])
        is_rank1 = sb("is_rank1", [P, 1], I32)
        BAND = UP + 2 * NARROW
        tap_of = sb("tap_of", [P, BAND], I32)
        band = sb("band", [P, 2, BAND])
        bias_bc = sb("bias_bc", [P, B, C])

        res = sb("res", [P, 2, HALF])
        gate = sb("gate", [P, HALF])

        masked = gate[:, 0:PAIRS * BAND].rearrange("p (t o) -> p t o", t=PAIRS)
        used = [0]

        def work(pattern, **dims):
            n = 1
            for d in dims.values():
                n *= d
            used[0] += n
            assert used[0] <= HALF
            return res[:, 1, used[0] - n:used[0]].rearrange(pattern, **dims)

        raw = work("p (s m w) -> p s m w", s=2, m=4, w=W)
        biased = work("p (s m w) -> p s m w", s=2, m=4, w=W)
        s1 = work("p (s m u) -> p s m u", s=2, m=2, u=UP)
        z = work("p (s m r u) -> p s m r u", s=2, m=2, r=2, u=UP)
        s3 = work("p (s m c r) -> p s m c r", s=2, m=2, c=2, r=P)
        y = work("p (s m w) -> p s m w", s=2, m=4, w=W)

        filt_pad = sb("filt_pad", [P, 2, TAPS + 2, TAPS + 2])
        pairs2 = sb("pairs2", [P, 2, PAIRS, PAIRS])
        pairs1 = sb("pairs1", [P, 2, PAIRS, TAPS + 2])
        tap_full = sb("tap_full", [P, 2 * UP], I32)
        band2 = gate[:, 0:PAIRS * 2 * UP].rearrange("p (s o) -> p s o", s=PAIRS)
        used[0] = 0
        PADW = W + 6
        raw2 = work("p (s m w) -> p s m w", s=2, m=4, w=W)
        x_pad = work("p (s m w) -> p s m w", s=2, m=4, w=PADW)
        z_pad = work("p (s q r m w) -> p s q r m w", s=2, q=2, r=2, m=4, w=PADW)
        y2 = work("p (s m w) -> p s m w", s=2, m=4, w=W)

        rawc = sb("rawc", [P, 2, CHUNK_ROWS + 2, W])
        split = sb("split", [P, 2, CHUNK_ROWS + 2, W + 2], F32R)
        w9_hi = sb("w9_hi", [P, 9, P], F32R)
        w9_lo = sb("w9_lo", [P, 9, P], F32R)
        masked2 = rawc[:, :, :, :].rearrange("p s r w -> p (s r w)")[:, 0:PAIRS * UP].rearrange(
            "p (t o) -> p t o", t=PAIRS)
        t_gate = sb("t_gate", [P, 2, N])
        t_out = sb("t_out", [P, 2, 4, N])
        gate2 = sb("gate2", [P, 2, N])
        ident = sb("ident", [P, P])
        swap = sb("swap", [P, P])
        diag_of = sb("diag_of", [P, P], I32)
        part_of = sb("part_of", [P, P], I32)
        w_nat = sb("w_nat", [P, 5, 2, C])
        w_tap = sb("w_tap", [P, 2, C])
        dwc = sb("dwc", [P, 9])
        colsum = sb("colsum", [P, 8])
        corr_o = sb("corr_o", [P, P])
        corr = sb("corr", [P, P])
        edge_cols = sb("edge_cols", [P, BLOCK_ROWS, 2])
        edge_top = sb("edge_top", [P, W])
        edge_bottom = sb("edge_bottom", [P, W])
        wbd2 = sb("wbd2", [P, P])
        wbd2_b = sb("wbd2_b", [P, P])
        wbd3 = sb("wbd3", [P, 2, P])
        wbd3_b = sb("wbd3_b", [P, 2, P])
        wbd4 = sb("wbd4", [P, P])
        wsca = sb("wsca", [P, P])
        col = sb("col", [P, 16])
        LN1W, LN1B, SCAB, PW2B, LN2W, LN2B, PW3B1, PW3B2, PW4B, BETA1, BETA2, OUTB = range(12)
        col_o = sb("col_o", [P, 4])
        stats = sb("stats", [P, TAIL, 6])
        mv = sb("mv", [P, 2])
        lnt = sb("lnt", [P, 8])
        ln1ab = sb("ln1ab", [P, 2])
        ln2ab = sb("ln2ab", [P, 2])
        bias3 = sb("bias3", [P, 2])
        gsum = sb("gsum", [P, CHUNKS * BLOCKS // 2])
        gtot = sb("gtot", [P, 1])
        attn = sb("attn", [P, 1])

        filt_landed = sem("filt_landed")
        const_landed = sem("const_landed")
        tap_index = sem("tap_index")
        dve_prep = sem("dve_prep")
        taps_ready = sem("taps_ready")
        corr_ready = sem("corr_ready")
        consts_ready = sem("consts_ready")
        bias_spread = sem("bias_spread")
        bands_ready = sem("bands_ready")
        x_landed = [sem(f"x_landed{i}") for i in range(2)]
        x_biased = sem("x_biased")
        s1_done = sem("s1_done")
        s1_out = sem("s1_out")
        s2_done = sem("s2_done")
        z_scaled = sem("z_scaled")
        z_ready = sem("z_ready")
        s3_done = sem("s3_done")
        s3_out = sem("s3_out")
        s4_done = sem("s4_done")
        y_ready = sem("y_ready")
        y_stored = [sem(f"y_stored{i}") for i in range(2)]
        rank_known = sem("rank_known")
        g_bands = sem("g_bands")
        g_chain = sem("g_chain")
        g_landed = [sem(f"g_landed{i}") for i in range(2)]
        g_zeroed = sem("g_zeroed")
        g_biased = sem("g_biased")
        g_up_done = sem("g_up_done")
        g_scaled = sem("g_scaled")
        g_z_ready = sem("g_z_ready")
        g_down_done = sem("g_down_done")
        g_y_ready = sem("g_y_ready")
        g_stored = [sem(f"g_stored{i}") for i in range(2)]
        pe_prep = sem("pe_prep")
        w1_ready = sem("w1_ready")
        res_landed = [sem(f"res_landed{i}") for i in range(2)]
        chunk_landed = [sem(f"chunk_landed{i}") for i in range(2)]
        chunk_normed = sem("chunk_normed")
        split_hi = sem("split_hi")
        split_done = sem("split_done")
        conv_done = sem("conv_done")
        tgate_ready = sem("tgate_ready")
        gate_done = sem("gate_done")
        bn1_done = sem("bn1_done")
        ln_chain = sem("ln_chain")
        stats_made = sem("stats_made")
        store_begun = sem("store_begun")
        mv_ready = sem("mv_ready")
        mv_swapped = sem("mv_swapped")
        var_ready = sem("var_ready")
        std_ready = sem("std_ready")
        ln1_ready = sem("ln1_ready")
        ln2_ready = sem("ln2_ready")
        gtot_ready = sem("gtot_ready")
        sca_done = sem("sca_done")
        attn_ready = sem("attn_ready")
        w2_ready = sem("w2_ready")
        pw2_done = sem("pw2_done")
        x2_ready = sem("x2_ready")
        bn2_done = sem("bn2_done")
        b3_done = sem("b3_done")
        w3_ready = sem("w3_ready")
        u2_done = sem("u2_done")
        u1_done = sem("u1_done")
        tgate2_ready = sem("tgate2_ready")
        gate2_ready = sem("gate2_ready")
        pw4_done = sem("pw4_done")
        sum_ready = sem("sum_ready")
        outb_ready = sem("outb_ready")
        out_stored = [sem(f"out_stored{i}") for i in range(2)]

        block = ctx.enter_context(nc.Block())

        def each_step(eng, step, lags):
            def live(g):
                return [0 <= g - lag < STEPS for lag in range(lags)]
            for g in range(8):
                step(g, g // 2, g % 4, live(g))
            with eng.Fori(2, STEPS // 4) as i:
                for k in range(4):
                    step(i * 4 + k, i * 2 + k // 2, k, [True] * lags)
            for g in range(STEPS, STEPS + lags - 1):
                step(g, g // 2, g % 4, live(g))

        UNITS = IMGS // 4

        def each_unit(eng, unit, lag):
            for u in range(4):
                unit(u, u % 2, True, u >= 1)
            with eng.Fori(2, UNITS // 2) as i:
                for k in range(2):
                    unit(i * 2 + k, k, True, True)
            if lag:
                unit(UNITS, 0, False, True)

        def by_rank(eng, separable, general):
            eng.wait_ge(rank_known, 1)
            flag = eng.value_load(is_rank1[0:1, 0:1], min_val=0, max_val=1)
            with eng.If(flag > 0):
                separable()
            with eng.Else():
                general()

        def each_batch(eng, batch):
            batch(0, 0, True, B == 1)
            if B > 1:
                if B > 2:
                    with eng.Fori(0, (B - 2) // 2) as i:
                        batch(i * 2 + 1, 1, False, False)
                        batch(i * 2 + 2, 0, False, False)
                batch(B - 1, 1, False, True)

        @block.sync
        def _(sp):
            for f, src in enumerate((up_filter, dn_filter)):
                sp.dma_start(filt[:, f, :, :].rearrange("p a b -> p (a b)"),
                             src.rearrange("a b -> (a b)").partition_broadcast(P)).then_inc(filt_landed, 16)
            sp.dma_start(bias_bc[:, 0, :],
                         bias.rearrange("a c h w -> (a c h w)").partition_broadcast(P)).then_inc(filt_landed, 16)

            def load(u, slot, wait):
                if wait:
                    sp.wait_ge(x_biased, u - 1)
                sp.dma_start(raw[:, slot, :, :], x_rows[:, bass.ds(u * 4, 4), :]).then_inc(x_landed[slot], 16)

            def store(u, slot):
                sp.wait_ge(y_ready, u * 2 + 2)
                sp.dma_start(l0_rows[:, bass.ds(u * 4, 4), :], y[:, slot, :, :]).then_inc(y_stored[slot], 16)

            def separable():
                for u in range(4):
                    load(u, u % 2, u >= 2)
                for u in range(2):
                    store(u, u)
                with sp.Fori(2, UNITS // 2) as i:
                    for k in range(2):
                        load(i * 2 + k, k, True)
                        store(i * 2 + k - 2, k)
                for u in (UNITS - 2, UNITS - 1):
                    store(u, u % 2)
                for slot in range(2):
                    sp.wait_ge(y_stored[slot], 16 * (UNITS // 2))

            def general():
                def unit(u, slot, now, before):
                    if now:
                        if not (isinstance(u, int) and u < 2):
                            sp.wait_ge(g_biased, u - 1)
                        sp.dma_start(raw2[:, slot, :, :], x_rows[:, bass.ds(u * 4, 4), :]
                                     ).then_inc(g_landed[slot], 16)
                    if before:
                        sp.wait_ge(g_y_ready, u)
                        sp.dma_start(l0_rows[:, bass.ds(u * 4 - 4, 4), :], y2[:, 1 - slot, :, :]
                                     ).then_inc(g_stored[1 - slot], 16)
                each_unit(sp, unit, True)
                for slot in range(2):
                    sp.wait_ge(g_stored[slot], 16 * (UNITS // 2))

            by_rank(sp, separable, general)

            def load_res(b, par, wait):
                if wait:
                    sp.wait_ge(sum_ready, (b - 1) * TAIL)
                for s in range(2):
                    sp.dma_start(res[64 * s:64 * s + 64, par, :],
                                 l0_half[s, bass.ds(b * C, C), :]).then_inc(res_landed[par], 16)

            def load_chunk(b, c, slot, first, last, wait):
                q = b * CHUNKS + c
                if wait:
                    sp.wait_ge(split_done, q - 1)
                lo = 1 if first else 0
                n = CHUNK_ROWS + 2 - lo - (1 if last else 0)
                row = 0 if first else c * CHUNK_ROWS - 1
                for s in range(2):
                    sp.dma_start(rawc[64 * s:64 * s + 64, slot, lo:lo + n, :],
                                 l0_out[bass.ds(b * C, C), bass.ds(row, n), :]).then_inc(chunk_landed[slot], 16)

            def store_out(b, quarter):
                slot = quarter % 2
                sp.wait_ge(outb_ready, b * TAIL + quarter * 4 + 4)
                sp.sem_inc(store_begun, 1)
                for s in range(2):
                    sp.dma_start(out_half[s, bass.ds(b * C, C), quarter * 4 * N:(quarter + 1) * 4 * N],
                                 t_out[64 * s:64 * s + 64, slot, :, :].rearrange("p a n -> p (a n)")
                                 ).then_inc(out_stored[slot], 16)

            def batch(b, par, first, last):
                load_chunk(b, 2, 0, False, False, True)
                if not last:
                    load_res(b + 1, 1 - par, not first)
                with sp.Fori(0, (CHUNKS - 4) // 2) as i:
                    load_chunk(b, i * 2 + 3, 1, False, False, True)
                    load_chunk(b, i * 2 + 4, 0, False, False, True)
                load_chunk(b, CHUNKS - 1, 1, False, True, True)
                if not last:
                    load_chunk(b + 1, 0, 0, True, False, True)
                    load_chunk(b + 1, 1, 1, False, False, True)
                for quarter in range(TAIL // 4):
                    store_out(b, quarter)

            load_res(0, 0, False)
            load_chunk(0, 0, 0, True, False, False)
            load_chunk(0, 1, 1, False, False, False)
            each_batch(sp, batch)
            for slot in range(2):
                sp.wait_ge(out_stored[slot], 32 * B * (TAIL // 8))

        @block.gpsimd
        def _(pool):
            for lo, n, base, step, per_row in (
                    (0, UP, PAD_LO + 1, -1, 2),
                    (UP, NARROW, PAD_LO, -2, 1),
                    (UP + NARROW, NARROW, P - 2 * SECOND + PAD_LO, -2, 1)):
                pool.iota(tap_of[:, lo:lo + n], [[step, n]], base=base,
                          channel_multiplier=per_row).then_inc(tap_index, 1)
            for lo, n, base, step, per_row in ((0, UP, PAD_LO + 1, -1, 2), (UP, P, PAD_LO, -2, 1),
                                               (UP + P, P, P + PAD_LO, -2, 1)):
                pool.iota(tap_full[:, lo:lo + n], [[step, n]], base=base,
                          channel_multiplier=per_row).then_inc(tap_index, 1)
            pool.iota(diag_of[:, :], [[-1, P]], base=0, channel_multiplier=1).then_inc(tap_index, 1)
            pool.iota(part_of[:, :], [[0, P]], base=0, channel_multiplier=1).then_inc(tap_index, 1)
            pool.memset(corr_o[:, :], 0.0).then_inc(tap_index, 1)
            pool.memset(wbd2[:, :], 0.0).then_inc(tap_index, 1)
            pool.memset(wbd3[:, :, :], 0.0).then_inc(tap_index, 1)
            pool.memset(wbd4[:, :], 0.0).then_inc(tap_index, 1)
            pool.memset(split[:, :, :, :].bitcast(F32), 0.0).then_inc(tap_index, 1)
            pool.wait_ge(filt_landed, 48)
            for b in range(1, B):
                pool.tensor_copy(bias_bc[:, b, :], bias_bc[:, 0, :]).then_inc(bias_spread, 1)
            if B > 1:
                pool.wait_ge(bias_spread, B - 1)
            bias_flat = bias_bc[:, :, :].rearrange("p b c -> p (b c)")

            def add_bias(u, slot, j, wait):
                pool.wait_ge(x_landed[slot], 16 * j + 16)
                if wait:
                    pool.wait_ge(s1_done, u * 2 - 2)
                pool.tensor_tensor(biased[:, slot, :, :], raw[:, slot, :, :],
                                   bias_flat[:, bass.ds(u * 4, 4)].unsqueeze(2).to_broadcast([P, 4, W]),
                                   ALU.add).then_inc(x_biased, 1)
            def separable():
                for u in range(2):
                    add_bias(u, u, 0, False)
                with pool.Fori(1, IMGS // 8) as i:
                    for k in range(2):
                        add_bias(i * 2 + k, k, i, True)

            def general():
                pool.memset(x_pad[:, :, :, :], 0.0).then_inc(g_zeroed, 1)
                pool.memset(z_pad[:, :, :, :, :, :], 0.0).then_inc(g_zeroed, 1)
                pool.wait_ge(g_zeroed, 2)

                def unit(u, slot, now, before):
                    pool.wait_ge(g_landed[slot], (u - slot) * 8 + 16)
                    if not (isinstance(u, int) and u < 2):
                        pool.wait_ge(g_up_done, u * 4 - 4)
                    pool.tensor_tensor(x_pad[:, slot, :, 3:3 + W], raw2[:, slot, :, :],
                                       bias_flat[:, bass.ds(u * 4, 4)].unsqueeze(2).to_broadcast([P, 4, W]),
                                       ALU.add).then_inc(g_biased, 1)
                each_unit(pool, unit, False)

            by_rank(pool, separable, general)

        @block.tensor
        def _(pe):
            up = [band[:, a, 0:UP] for a in range(2)]
            down = [[band[:, a, UP + h * NARROW:UP + (h + 1) * NARROW] for h in range(2)] for a in range(2)]

            def step(g, u, k, live):
                if live[0]:
                    slot, pos = (k // 2) % 2, 2 * (k % 2)
                    if k % 2 == 0:
                        pe.wait_ge(x_biased, u + 1)
                    if not (isinstance(g, int) and g < 1):
                        pe.wait_ge(s1_out, g)
                    for m in range(2):
                        mm = nc.tensor.matmul(bank[0][:, m * UP:(m + 1) * UP], biased[:, slot, pos + m, :],
                                              up[0], start=(m == 0), stop=True, skip_group_check=True)
                    mm.then_inc(s1_done, 1)
                if live[1]:
                    h, par = g - 1, (k - 1) % 2
                    pe.wait_ge(s1_out, h + 1)
                    for m in range(2):
                        if not (isinstance(h, int) and h < 1):
                            pe.wait_ge(z_ready, h * 2 - 1 + m)
                        for r in range(2):
                            mm = nc.tensor.matmul(bank[1 + m][:, r * UP:(r + 1) * UP],
                                                  s1[:, par, m, r * P:(r + 1) * P], up[1],
                                                  start=(r == 0), stop=True, skip_group_check=True)
                        mm.then_inc(s2_done, 1)
                if live[2]:
                    h, par = g - 2, k % 2
                    pe.wait_ge(z_ready, h * 2 + 2)
                    if not (isinstance(h, int) and h < 1):
                        pe.wait_ge(s3_out, h)
                    acc = bank[3][:, :].rearrange("p (m c r) -> p m c r", m=2, c=2)
                    for n in range(8):
                        m, c, r = n // 4, n // 2 % 2, n % 2
                        mm = nc.tensor.matmul(acc[:, m, c, r * SECOND:r * SECOND + NARROW],
                                              z[:, par, m, r, c * P:(c + 1) * P], down[0][r],
                                              start=(n == 0), stop=True, skip_group_check=True)
                    mm.then_inc(s3_done, 1)
                if live[3]:
                    h, par = g - 3, (k - 3) % 2
                    pe.wait_ge(s3_out, h + 1)
                    if not (isinstance(h, int) and h < 1):
                        pe.wait_ge(y_ready, h)
                    for n in range(4):
                        m, c = n // 2, n % 2
                        mm = nc.tensor.matmul(bank[4][:, m * P + c * SECOND:m * P + c * SECOND + NARROW],
                                              s3[:, par, m, c, :], down[1][c],
                                              start=(n == 0), stop=True, skip_group_check=True)
                    mm.then_inc(s4_done, 1)

            for t in range(9):
                pe.wait_ge(taps_ready, t + 1)
                if t >= 1:
                    pe.wait_ge(w1_ready, t)
                nc.tensor.matmul(bank[5][:, 0:P], masked[:, t, 0:P], ident[:, :],
                                 start=True, stop=True).then_inc(pe_prep, 1)
            pe.wait_ge(corr_ready, 1)
            nc.tensor.matmul(bank[6][:, 0:P], corr_o[:, :], ident[:, :], start=True, stop=True)
            nc.tensor.matmul(bank[6][:, P:2 * P], w_nat[:, 1, :, :].rearrange("p a c -> p (a c)"),
                             ident[:, :], start=True, stop=True)
            for n, at in ((2, 2 * P), (3, 2 * P + C), (4, 3 * P)):
                mm = nc.tensor.matmul(bank[6][:, at:at + C], w_nat[0:C, n, :, :].rearrange("p a c -> p (a c)"),
                                      ident[0:C, 0:C], start=True, stop=True)
            mm.then_inc(pe_prep, 1)

            def separable():
                pe.wait_ge(bands_ready, 1)
                each_step(pe, step, 4)

            def general():
                pe.wait_ge(g_bands, 1)
                pe.wait_ge(g_zeroed, 2)

                def unit(u, slot, now, before):
                    if now:
                        pe.wait_ge(g_biased, u + 1)
                        for q in range(2):
                            for h in range(2):
                                acc = bank[2 * q + h]
                                if not (isinstance(u, int) and u < 1):
                                    pe.wait_ge(g_z_ready, u * 4 - 3 + 2 * q + h)
                                taps = range(q, PAIRS, 2)
                                for t in taps:
                                    at = 3 + (t + q - 6) // 2
                                    mm = nc.tensor.matmul(acc[:, :], band2[:, t, h * P:(h + 1) * P],
                                                          x_pad[:, slot, :, at:at + W],
                                                          start=(t == q), stop=(t == taps[-1]))
                                mm.then_inc(g_up_done, 1)
                    if before:
                        pe.wait_ge(g_z_ready, u * 4)
                        if not (isinstance(u, int) and u < 2):
                            pe.wait_ge(g_y_ready, u - 1)
                        n = 0
                        for t in range(PAIRS):
                            q = (t + 1) % 2
                            at = 3 + (t - 5 - q) // 2
                            for h in range(2):
                                mm = nc.tensor.matmul(bank[4][:, :], band2[:, t, UP + h * P:UP + (h + 1) * P],
                                                      z_pad[:, 1 - slot, q, h, :, at:at + W],
                                                      start=(n == 0), stop=(n == 2 * PAIRS - 1))
                                n += 1
                        mm.then_inc(g_down_done, 1)
                each_unit(pe, unit, True)

            by_rank(pe, separable, general)

            pe.wait_ge(consts_ready, 1)

            def conv_chunk(b, c, slot, first, last):
                q = b * CHUNKS + c
                for j in range(BLOCKS):
                    n = q * BLOCKS + j
                    if j == 0:
                        pe.wait_ge(split_done, q + 1)
                    if not (isinstance(n, int) and n < 2):
                        pe.wait_ge(gate_done, n - 1)
                    acc = bank[j % 2]
                    for t in range(9):
                        win = split[:, slot, BLOCK_ROWS * j + t // 3:BLOCK_ROWS * j + t // 3 + BLOCK_ROWS,
                                    t % 3:t % 3 + W]
                        if t == 8:
                            nc.tensor.matmul(acc[:, :].rearrange("p (r w) -> p r w", w=W)[:, :, 0:W:W - 1],
                                             corr[:, :], edge_cols[:, :, :], start=False, stop=False,
                                             skip_group_check=True)
                            if first and j == 0:
                                nc.tensor.matmul(acc[:, 0:W], corr[:, :], edge_top[:, :], start=False,
                                                 stop=False, skip_group_check=True)
                            if last and j == BLOCKS - 1:
                                nc.tensor.matmul(acc[:, N - W:N], corr[:, :], edge_bottom[:, :],
                                                 start=False, stop=False, skip_group_check=True)
                        nc.tensor.matmul(acc[:, :], w9_lo[:, t, :], win, start=(t == 0), stop=False,
                                         skip_group_check=True)
                        mm = nc.tensor.matmul(acc[:, :], w9_hi[:, t, :], win, start=False, stop=(t == 8),
                                              skip_group_check=True)
                    mm.then_inc(conv_done, 1)

            def swap_stats(n):
                pe.wait_ge(mv_ready, n + 1)
                nc.tensor.matmul(bank[6][:, 0:2], swap[:, :], mv[:, :], start=True,
                                 stop=True).then_inc(mv_swapped, 1)

            swap_stats(0)

            def batch(b, par, first, last):
                conv_chunk(b, 0, 0, True, False)
                with pe.Fori(0, (CHUNKS - 2) // 2) as i:
                    conv_chunk(b, i * 2 + 1, 1, False, False)
                    conv_chunk(b, i * 2 + 2, 0, False, False)
                conv_chunk(b, CHUNKS - 1, 1, False, True)
                pe.wait_ge(gtot_ready, b + 1)
                nc.tensor.matmul(bank[6][:, 4:5], wsca[:, :], gtot[:, :], start=True,
                                 stop=True).then_inc(sca_done, 1)
                if not last:
                    swap_stats(b * 2 + 1)
                pe.wait_ge(w2_ready, b + 1)
                for j in range(TAIL):
                    if j >= 2:
                        pe.wait_ge(x2_ready, b * TAIL + j - 1)
                    elif not first:
                        pe.wait_ge(sum_ready, b * TAIL - 1 + j)
                    nc.tensor.matmul(bank[2 + j % 2][:, :], wbd2_b[:, :], gate[:, j * N:(j + 1) * N],
                                     start=True, stop=True).then_inc(pw2_done, 1)
                swap_stats(b * 2 + (1 if last else 2))
                pe.wait_ge(ln2_ready, b + 1)
                for o in range(2):
                    mm = nc.tensor.matmul(bank[6][:, 8 + o:9 + o], wbd3[:, o, :], ln2ab[:, 1:2],
                                          start=True, stop=True)
                mm.then_inc(b3_done, 1)
                pe.wait_ge(w3_ready, b + 1)
                for j in range(TAIL + 1):
                    if j < TAIL:
                        n = b * TAIL + j
                        x2 = res[:, par, j * N:(j + 1) * N]
                        if not (first and j < 1):
                            pe.wait_ge(tgate2_ready, n)
                        nc.tensor.matmul(bank[5][:, :], wbd3_b[:, 1, :], x2, start=True,
                                         stop=True).then_inc(u2_done, 1)
                        if not (first and j < 2):
                            pe.wait_ge(gate2_ready, n - 1)
                        nc.tensor.matmul(bank[(4, 7)[j % 2]][:, :], wbd3_b[:, 0, :], x2, start=True,
                                         stop=True).then_inc(u1_done, 1)
                    if j >= 1:
                        n = b * TAIL + j - 1
                        pe.wait_ge(gate2_ready, n + 1)
                        if j >= 3:
                            pe.wait_ge(sum_ready, n - 1)
                        nc.tensor.matmul(bank[2 + (j - 1) % 2][:, :], wbd4[:, :], gate2[:, (j - 1) % 2, :],
                                         start=True, stop=True).then_inc(pw4_done, 1)

            each_batch(pe, batch)

        @block.scalar
        def _(act):
            def col_load(n, src, lo=0):
                for s in range(2):
                    act.dma_start(col[64 * s:64 * s + 64, n:n + 1], src[lo:lo + C, :]).then_inc(const_landed, 16)

            vec4 = "a c h w -> c (a h w)"
            col_load(LN1W, ln1_w.rearrange(vec4))
            col_load(LN1B, ln1_b.rearrange(vec4))
            col_load(SCAB, sca_b.rearrange("(c a) -> c a", a=1))
            col_load(PW2B, pw2_b.rearrange("(c a) -> c a", a=1))
            col_load(LN2W, ln2_w.rearrange(vec4))
            col_load(LN2B, ln2_b.rearrange(vec4))
            col_load(PW3B1, pw3_b.rearrange("(c a) -> c a", a=1))
            col_load(PW3B2, pw3_b.rearrange("(c a) -> c a", a=1), C)
            col_load(PW4B, pw4_b.rearrange("(c a) -> c a", a=1))
            col_load(BETA1, beta1.rearrange(vec4))
            col_load(BETA2, beta2.rearrange(vec4))
            act.dma_start(col_o[:, 0:1], dw_b.rearrange("(c a) -> c a", a=1)).then_inc(const_landed, 16)
            act.dma_start(col_o[:, 1:2], pw1_b.rearrange("(c a) -> c a", a=1)).then_inc(const_landed, 16)
            act.dma_start(dwc[:, :], dw_w.rearrange("o a h w -> o (a h w)")).then_inc(const_landed, 16)
            for n, (src, rows) in enumerate(((pw1_w, P), (pw3_w, P), (pw2_w, C), (pw4_w, C), (sca_w, C))):
                for s in range(2):
                    act.dma_start(w_nat[0:rows, n, s, :], src[:, :]).then_inc(const_landed, 16)

            def step(g, u, k, live):
                if live[0]:
                    par = k % 2
                    act.wait_ge(s1_done, g + 1)
                    if not (isinstance(g, int) and g < 2):
                        act.wait_ge(s2_done, g * 2 - 2)
                    nc.scalar.activation(s1[:, par, :, :].rearrange("p m u -> p (m u)"), bank[0][:, :],
                                         ACT.Copy).then_inc(s1_out, 1)
                if live[1]:
                    h, par = g - 1, (k - 1) % 2
                    for m in range(2):
                        act.wait_ge(s2_done, h * 2 + 1 + m)
                        if m == 0 and not (isinstance(h, int) and h < 2):
                            act.wait_ge(s3_done, h - 1)
                        nc.scalar.activation(z[:, par, m, :, :].rearrange("p r u -> p (r u)"),
                                             bank[1 + m][:, :], ACT.Copy, scale=SLOPE).then_inc(z_scaled, 1)

            def general():
                act.wait_ge(g_zeroed, 2)

                def unit(u, slot, now, before):
                    for n in range(4):
                        q, h = n // 2, n % 2
                        act.wait_ge(g_up_done, u * 4 + n + 1)
                        if n == 0 and not (isinstance(u, int) and u < 2):
                            act.wait_ge(g_down_done, u - 1)
                        nc.scalar.activation(z_pad[:, slot, q, h, :, 3:3 + W],
                                             bank[n][:, :].rearrange("p (m w) -> p m w", w=W),
                                             ACT.Copy, scale=SLOPE).then_inc(g_scaled, 1)
                each_unit(act, unit, False)

            by_rank(act, lambda: each_step(act, step, 2), general)

            act.wait_ge(consts_ready, 1)

            def norm(b, c, slot, lo, hi):
                q = b * CHUNKS + c
                act.wait_ge(chunk_landed[slot], b * (16 * CHUNKS) + slot_count(c, slot))
                flat = rawc[:, slot, lo:hi, :].rearrange("p r w -> p (r w)")
                nc.scalar.activation(flat, flat, ACT.Identity, bias=ln1ab[:, 1:2],
                                     scale=ln1ab[:, 0:1]).then_inc(chunk_normed, 1)

            def slot_count(c, slot):
                return (c - slot) * 16 + 32

            def gate_blocks(b, c, half):
                for j in range(BLOCKS):
                    n = (b * CHUNKS + c) * BLOCKS + j
                    act.wait_ge(conv_done, n + 1)
                    if not (isinstance(n, int) and n < 2):
                        act.wait_ge(gate_done, n - 1)
                    nc.scalar.activation(t_gate[0:C, j % 2, :], bank[j % 2][C:P, :], ACT.Identity,
                                         bias=col_o[C:P, 2:3]).then_inc(tgate_ready, 1)

            def sqrt_var(n):
                act.wait_ge(var_ready, n + 1)
                nc.scalar.activation(lnt[:, 4:5], lnt[:, 3:4], ACT.Sqrt).then_inc(std_ready, 1)

            sqrt_var(0)
            act.wait_ge(ln1_ready, 1)
            norm(0, 0, 0, 1, CHUNK_ROWS + 2)

            def batch(b, par, first, last):
                norm(b, 1, 1, 0, CHUNK_ROWS + 2)
                gate_blocks(b, 0, 0)
                with act.Fori(0, (CHUNKS - 4) // 2) as i:
                    norm(b, i * 2 + 2, 0, 0, CHUNK_ROWS + 2)
                    gate_blocks(b, i * 2 + 1, 0)
                    norm(b, i * 2 + 3, 1, 0, CHUNK_ROWS + 2)
                    gate_blocks(b, i * 2 + 2, 0)
                norm(b, CHUNKS - 2, 0, 0, CHUNK_ROWS + 2)
                gate_blocks(b, CHUNKS - 3, 1)
                norm(b, CHUNKS - 1, 1, 0, CHUNK_ROWS + 1)
                gate_blocks(b, CHUNKS - 2, 1)
                gate_blocks(b, CHUNKS - 1, 1)
                act.wait_ge(sca_done, b + 1)
                nc.scalar.activation(attn[:, :], bank[6][:, 4:5], ACT.Sigmoid,
                                     bias=col[:, SCAB:SCAB + 1]).then_inc(attn_ready, 1)
                if not last:
                    sqrt_var(b * 2 + 1)
                    act.wait_ge(ln1_ready, b + 2)
                    norm(b + 1, 0, 0, 1, CHUNK_ROWS + 2)
                sqrt_var(b * 2 + (1 if last else 2))
                act.wait_ge(w3_ready, b + 1)
                for j in range(TAIL + 1):
                    if j < TAIL:
                        n = b * TAIL + j
                        act.wait_ge(u2_done, n + 1)
                        if not (first and j < 2):
                            act.wait_ge(gate2_ready, n - 1)
                        nc.scalar.activation(t_gate[:, j % 2, :], bank[5][:, :], ACT.Identity,
                                             bias=bias3[:, 1:2]).then_inc(tgate2_ready, 1)
                    if j >= 1:
                        n = b * TAIL + j - 1
                        act.wait_ge(sum_ready, n + 1)
                        slot = (j - 1) // 4 % 2
                        o = t_out[:, slot, (j - 1) % 4, :]
                        nc.scalar.activation(o, o, ACT.Identity,
                                             bias=col[:, OUTB:OUTB + 1]).then_inc(outb_ready, 1)

            each_batch(act, batch)

        @block.vector
        def _(dve):
            made = [0]

            def prep(ins):
                made[0] += 1
                ins.then_inc(dve_prep, 1)
                dve.wait_ge(dve_prep, made[0])

            dve.wait_ge(filt_landed, 48)
            prep(nc.vector.memset(factor[:, :, :], 0.0))
            for f in range(2):
                c0 = filt[:, f, CENTRE, CENTRE:CENTRE + 1]
                prep(nc.vector.reciprocal(recip[:, f:f + 1], c0))
                prep(nc.vector.tensor_scalar(ratio[:, f, :, :], filt[:, f, :, :], recip[:, f:f + 1], None, ALU.mult))
                prep(nc.vector.tensor_tensor(
                    resid[:, f, :, :], ratio[:, f, :, CENTRE:CENTRE + 1].to_broadcast([P, TAPS, TAPS]),
                    ratio[:, f, CENTRE:CENTRE + 1, :].to_broadcast([P, TAPS, TAPS]), ALU.mult))
                prep(nc.vector.tensor_copy(factor[:, 2 * f, 1:TAPS + 1], filt[:, f, :, CENTRE]))
                prep(nc.vector.tensor_copy(factor[:, 2 * f + 1, 1:TAPS + 1], ratio[:, f, CENTRE, :]))
            prep(nc.vector.tensor_scalar(factor[:, 2, :], factor[:, 2, :], 0.5, None, ALU.mult))
            prep(nc.vector.tensor_scalar(factor[:, 3, :], factor[:, 3, :], 0.5 * GAIN, None, ALU.mult))
            prep(nc.vector.tensor_tensor(pairs[:, :, :], factor[:, :, 0:PAIRS], factor[:, :, 1:PAIRS + 1], ALU.add))
            prep(nc.vector.tensor_tensor(resid[:, :, :, :], ratio[:, :, :, :], resid[:, :, :, :], ALU.subtract))
            for t in (resid, ratio):
                prep(nc.vector.scalar_tensor_tensor(
                    out=t[:, :, :, :].rearrange("p f a b -> p (f a b)"),
                    in0=t[:, :, :, :].rearrange("p f a b -> p (f a b)"), scalar=-1.0,
                    in1=t[:, :, :, :].rearrange("p f a b -> p (f a b)"), op0=ALU.mult, op1=ALU.max))
            prep(nc.vector.scalar_tensor_tensor(
                out=resid[:, :, :, :].rearrange("p f a b -> p (f a b)"),
                in0=ratio[:, :, :, :].rearrange("p f a b -> p (f a b)"), scalar=RANK1_TOL,
                in1=resid[:, :, :, :].rearrange("p f a b -> p (f a b)"), op0=ALU.mult, op1=ALU.is_ge))
            prep(nc.vector.tensor_reduce(fits[:, 0:1], resid[:, :, :, :].rearrange("p f a b -> p (f a b)"),
                                         AX.X, ALU.min))
            prep(nc.vector.tensor_copy(is_rank1[:, :], fits[:, 0:1]))
            dve.sem_inc(rank_known, 1)
            dve.wait_ge(tap_index, 13)
            for a in range(2):
                for lo, hi, f in ((0, UP, 0), (UP, BAND, 1)):
                    for t in range(PAIRS):
                        ins = nc.vector.tensor_scalar(masked[:, t, lo:hi], tap_of[:, lo:hi], float(t),
                                                      pairs[:, 2 * f + a, t:t + 1], ALU.is_equal, ALU.mult)
                    prep(ins)
                prep(nc.vector.tensor_reduce(band[:, a, :], masked[:, :, :].rearrange("p t o -> p o t"),
                                             AX.X, ALU.add))
            dve.sem_inc(bands_ready, 1)

            prep(nc.vector.tensor_scalar(ident[:, :], diag_of[:, :], 0.0, None, ALU.is_equal))
            prep(nc.vector.tensor_scalar(swap[:, :], diag_of[:, :], float(C), None, ALU.is_equal))
            prep(nc.vector.tensor_scalar(corr[:, :], diag_of[:, :], float(-C), None, ALU.is_equal))
            prep(nc.vector.tensor_tensor(swap[:, :], swap[:, :], corr[:, :], ALU.add))
            dve.wait_ge(const_landed, 16 * 35)
            for t in range(9):
                prep(nc.vector.tensor_scalar(masked[:, t, 0:P], w_nat[:, 0, :, :].rearrange("p a c -> p (a c)"),
                                             dwc[:, t:t + 1], None, ALU.mult))
                dve.sem_inc(taps_ready, 1)
            def tap_sum(n, view, negate=False):
                prep(nc.vector.tensor_reduce(colsum[:, 0:1], view, AX.X, ALU.add, negate=negate))
                prep(nc.vector.tensor_tensor(corr_o[:, n:n + 1], colsum[:, 0:1], col_o[:, 1:2], ALU.mult))

            for n, view in enumerate((dwc[:, 0:3], dwc[:, 6:9], dwc[:, 0:9:3], dwc[:, 2:9:3])):
                tap_sum(n, view)
                prep(nc.vector.tensor_scalar(corr_o[:, n:n + 1], corr_o[:, n:n + 1], -1.0, None, ALU.mult))
            for n, t in enumerate((0, 2, 6, 8)):
                tap_sum(4 + n, dwc[:, t:t + 1])
            prep(nc.vector.tensor_reduce(colsum[:, 0:1], dwc[:, :], AX.X, ALU.add))
            prep(nc.vector.scalar_tensor_tensor(out=col_o[:, 2:3], in0=colsum[:, 0:1], scalar=col_o[:, 1:2],
                                                in1=col_o[:, 0:1], op0=ALU.mult, op1=ALU.add))
            dve.sem_inc(corr_ready, 1)
            def where(dst, n):
                return nc.vector.tensor_scalar(dst, part_of[:, 0:1] if dst.shape[-1] == 1 else part_of[:, :],
                                               float(n), None, ALU.is_equal)
            prep(where(edge_top[:, :], 0))
            prep(where(edge_bottom[:, :], 1))
            for dst, corners in ((edge_top, (4, 5)), (edge_bottom, (6, 7))):
                for at, n in zip((0, W - 1), corners):
                    prep(where(colsum[:, 0:1], n))
                    prep(nc.vector.tensor_tensor(dst[:, at:at + 1], dst[:, at:at + 1], colsum[:, 0:1], ALU.add))
            for r in range(BLOCK_ROWS):
                for s in range(2):
                    prep(where(edge_cols[:, r, s:s + 1], 2 + s))
            for t in range(9):
                dve.wait_ge(pe_prep, t + 1)
                prep(nc.vector.tensor_copy(w9_hi[:, t, :], bank[5][:, 0:P]))
                nc.vector.tensor_tensor(w9_lo[:, t, :], bank[5][:, 0:P], w9_hi[:, t, :],
                                        ALU.subtract).then_inc(w1_ready, 1)
            dve.wait_ge(pe_prep, 10)
            prep(nc.vector.tensor_copy(corr[:, :], bank[6][:, 0:P]))
            for s in range(2):
                lanes, own = slice(64 * s, 64 * s + 64), slice(64 * s, 64 * s + 64)
                for o in range(2):
                    prep(nc.vector.tensor_copy(wbd3[lanes, o, own], bank[6][lanes, P + C * o:P + C * o + C]))
                prep(nc.vector.tensor_copy(wbd2[lanes, own], bank[6][lanes, 2 * P:2 * P + C]))
                prep(nc.vector.tensor_copy(wbd4[lanes, own], bank[6][lanes, 2 * P + C:3 * P]))
                prep(nc.vector.tensor_scalar(wsca[:, own], bank[6][:, 3 * P:3 * P + C], 1.0 / HW, None, ALU.mult))
            prep(nc.vector.tensor_tensor(colsum[:, 1:2], col[:, PW2B:PW2B + 1], col[:, BETA1:BETA1 + 1], ALU.mult))
            prep(nc.vector.scalar_tensor_tensor(out=col[:, OUTB:OUTB + 1], in0=col[:, PW4B:PW4B + 1],
                                                scalar=col[:, BETA2:BETA2 + 1], in1=colsum[:, 1:2],
                                                op0=ALU.mult, op1=ALU.add))
            dve.sem_inc(consts_ready, 1)

            def step(g, u, k, live):
                if live[1]:
                    h, par = g - 1, (k - 1) % 2
                    for m in range(2):
                        dve.wait_ge(z_scaled, h * 2 + 1 + m)
                        zm = z[:, par, m, :, :].rearrange("p r u -> p (r u)")
                        nc.vector.tensor_tensor(zm, zm, bank[1 + m][:, :], ALU.max).then_inc(z_ready, 1)
                if live[2]:
                    h, par = g - 2, k % 2
                    dve.wait_ge(s3_done, h + 1)
                    if not (isinstance(h, int) and h < 2):
                        dve.wait_ge(s4_done, h - 1)
                    nc.vector.tensor_copy(s3[:, par, :, :, :].rearrange("p m c r -> p (m c r)"),
                                          bank[3][:, :]).then_inc(s3_out, 1)
                if live[3]:
                    h, kk = g - 3, (k - 3) % 4
                    slot, pos = kk // 2, 2 * (kk % 2)
                    dve.wait_ge(s4_done, h + 1)
                    if kk % 2 == 0 and not (isinstance(h, int) and h < 4):
                        dve.wait_ge(y_stored[slot], (h - kk) * 4)
                    nc.vector.tensor_copy(y[:, slot, pos:pos + 2, :].rearrange("p m w -> p (m w)"),
                                          bank[4][:, 0:2 * P]).then_inc(y_ready, 1)

            def general():
                made2 = [0]

                def link(ins):
                    made2[0] += 1
                    ins.then_inc(g_chain, 1)
                    dve.wait_ge(g_chain, made2[0])

                link(nc.vector.memset(filt_pad[:, :, :, :], 0.0))
                for f in range(2):
                    link(nc.vector.tensor_copy(filt_pad[:, f, 1:TAPS + 1, 1:TAPS + 1], filt[:, f, :, :]))
                    link(nc.vector.tensor_tensor(pairs1[:, f, :, :], filt_pad[:, f, 0:PAIRS, :],
                                                 filt_pad[:, f, 1:PAIRS + 1, :], ALU.add))
                    link(nc.vector.tensor_tensor(pairs2[:, f, :, :], pairs1[:, f, :, 0:PAIRS],
                                                 pairs1[:, f, :, 1:PAIRS + 1], ALU.add))
                link(nc.vector.tensor_scalar(pairs2[:, 1, :, :], pairs2[:, 1, :, :], 0.25 * GAIN, None, ALU.mult))
                for f in range(2):
                    for s in range(PAIRS):
                        for t in range(PAIRS):
                            ins = nc.vector.tensor_scalar(masked2[:, t, :], tap_full[:, f * UP:(f + 1) * UP],
                                                          float(t), pairs2[:, f, t, s:s + 1],
                                                          ALU.is_equal, ALU.mult)
                        link(ins)
                        link(nc.vector.tensor_reduce(band2[:, s, f * UP:(f + 1) * UP],
                                                     masked2[:, :, :].rearrange("p t o -> p o t"), AX.X, ALU.add))
                dve.sem_inc(g_bands, 1)

                def unit(u, slot, now, before):
                    if now:
                        for n in range(4):
                            q, h = n // 2, n % 2
                            dve.wait_ge(g_scaled, u * 4 + n + 1)
                            zz = z_pad[:, slot, q, h, :, 3:3 + W]
                            nc.vector.tensor_tensor(zz, zz, bank[n][:, :].rearrange("p (m w) -> p m w", w=W),
                                                    ALU.max).then_inc(g_z_ready, 1)
                    if before:
                        dve.wait_ge(g_down_done, u)
                        if not (isinstance(u, int) and u < 3):
                            dve.wait_ge(g_stored[1 - slot], (u + slot) * 8 - 16)
                        nc.vector.tensor_copy(y2[:, 1 - slot, :, :].rearrange("p m w -> p (m w)"),
                                              bank[4][:, :]).then_inc(g_y_ready, 1)
                each_unit(dve, unit, True)

            by_rank(dve, lambda: each_step(dve, step, 4), general)

            CHAIN = 9

            def norm_coefs(n, w, b_, ab, ready):
                count = [0]

                def link(ins):
                    count[0] += 1
                    ins.then_inc(ln_chain, 1)
                    dve.wait_ge(ln_chain, n * CHAIN + count[0])

                dve.sem_inc(stats_made, 1)
                nc.vector.bn_aggr(mv[:, :], stats[:, :, :].rearrange("p a b -> p (a b)")).then_inc(mv_ready, 1)
                dve.wait_ge(mv_ready, n + 1)
                dve.wait_ge(mv_swapped, n + 1)
                link(nc.vector.tensor_tensor(lnt[:, 0:2], mv[:, :], bank[6][:, 0:2], ALU.add))
                link(nc.vector.tensor_tensor(lnt[:, 2:3], mv[:, 0:1], bank[6][:, 0:1], ALU.subtract))
                link(nc.vector.tensor_scalar(lnt[:, 2:3], lnt[:, 2:3], lnt[:, 2:3], 0.25, ALU.mult, ALU.mult))
                link(nc.vector.tensor_scalar(lnt[:, 1:2], lnt[:, 1:2], 0.5, LN_EPS, ALU.mult, ALU.add))
                nc.vector.tensor_tensor(lnt[:, 3:4], lnt[:, 1:2], lnt[:, 2:3], ALU.add).then_inc(var_ready, 1)
                dve.wait_ge(std_ready, n + 1)
                link(nc.vector.reciprocal(lnt[:, 5:6], lnt[:, 4:5]))
                link(nc.vector.tensor_tensor(ab[:, 0:1], lnt[:, 5:6], col[:, w:w + 1], ALU.mult))
                link(nc.vector.tensor_scalar(lnt[:, 6:7], lnt[:, 0:1], -0.5, None, ALU.mult))
                link(nc.vector.tensor_tensor(lnt[:, 6:7], lnt[:, 6:7], ab[:, 0:1], ALU.mult))
                link(nc.vector.tensor_tensor(ab[:, 1:2], lnt[:, 6:7], col[:, b_:b_ + 1], ALU.add))
                dve.sem_inc(ready, 1)

            def bn1(b, par, j):
                nc.vector.bn_stats(stats[:, j, :], res[:, par, j * N:(j + 1) * N]).then_inc(bn1_done, 1)

            def split_chunk(b, c, slot, lo, hi, wait=True):
                q = b * CHUNKS + c
                if wait:
                    dve.wait_ge(conv_done, (q - 1) * BLOCKS)
                if lo:
                    nc.vector.memset(split[:, slot, 0, :].bitcast(F32), 0.0)
                if hi < CHUNK_ROWS + 2:
                    nc.vector.memset(split[:, slot, CHUNK_ROWS + 1, :].bitcast(F32), 0.0)
                dve.wait_ge(chunk_normed, q + 1)
                nc.vector.tensor_copy(split[:, slot, lo:hi, 1:W + 1], rawc[:, slot, lo:hi, :]).then_inc(split_hi, 1)
                dve.wait_ge(split_hi, q + 1)
                nc.vector.tensor_tensor(split[C:P, slot, lo:hi, 1:W + 1], rawc[C:P, slot, lo:hi, :],
                                        split[C:P, slot, lo:hi, 1:W + 1], ALU.subtract).then_inc(split_done, 1)

            def gate_blocks(b, c, half, first):
                for j in range(BLOCKS):
                    n = (b * CHUNKS + c) * BLOCKS + j
                    dve.wait_ge(tgate_ready, n + 1)
                    if not first:
                        dve.wait_ge(pw2_done, b * TAIL)
                    at = (c * BLOCKS + j) - half * TAIL
                    lanes = slice(64 * half, 64 * half + 64)
                    nc.vector.scalar_tensor_tensor(
                        out=gate[lanes, bass.ds(at * N, N)], in0=bank[j % 2][0:C, :], scalar=col_o[0:C, 2:3],
                        in1=t_gate[0:C, j % 2, :], op0=ALU.add, op1=ALU.mult,
                        accum_out=gsum[lanes, bass.ds(at, 1)]).then_inc(gate_done, 1)

            dve.wait_ge(res_landed[0], 32)
            for j in range(TAIL):
                bn1(0, 0, j)
            dve.wait_ge(bn1_done, TAIL)
            norm_coefs(0, LN1W, LN1B, ln1ab, ln1_ready)
            split_chunk(0, 0, 0, 1, CHUNK_ROWS + 2, wait=False)

            def batch(b, par, first, last):
                def chunk(c, half, stats_lo, split_next, slot, hi):
                    if split_next:
                        split_chunk(b, c + 1, slot, 0, hi, wait=not (first and isinstance(c, int) and c == 0))
                    if not last and stats_lo is not None:
                        for j in stats_lo:
                            bn1(b + 1, 1 - par, j)
                    gate_blocks(b, c, half, first)

                chunk(0, 0, None, True, 1, CHUNK_ROWS + 2)
                chunk(1, 0, None, True, 0, CHUNK_ROWS + 2)
                chunk(2, 0, None, True, 1, CHUNK_ROWS + 2)
                chunk(CHUNKS // 2 - 1, 0, None, True, 0, CHUNK_ROWS + 2)
                if not last:
                    dve.wait_ge(res_landed[1 - par], (b + 1 - (1 - par)) * 16 + 32)
                chunk(4, 1, range(0, 4), True, 1, CHUNK_ROWS + 2)
                chunk(5, 1, range(4, 8), True, 0, CHUNK_ROWS + 2)
                chunk(6, 1, range(8, 12), True, 1, CHUNK_ROWS + 1)
                chunk(7, 1, range(12, 16), False, 0, 0)
                dve.wait_ge(gate_done, (b + 1) * CHUNKS * BLOCKS)
                nc.vector.tensor_reduce(gtot[:, :], gsum[:, :], AX.X, ALU.add).then_inc(gtot_ready, 1)
                dve.wait_ge(attn_ready, b + 1)
                nc.vector.tensor_scalar(wbd2_b[:, :], wbd2[:, :], attn[:, :], None, ALU.mult).then_inc(w2_ready, 1)
                if not last:
                    dve.wait_ge(bn1_done, (b + 2) * TAIL)
                    norm_coefs(b * 2 + 1, LN1W, LN1B, ln1ab, ln1_ready)
                    split_chunk(b + 1, 0, 0, 1, CHUNK_ROWS + 2)
                for j in range(TAIL):
                    n = b * TAIL + j
                    dve.wait_ge(pw2_done, n + 1)
                    xb = res[:, par, j * N:(j + 1) * N]
                    nc.vector.scalar_tensor_tensor(out=xb, in0=bank[2 + j % 2][:, :],
                                                   scalar=col[:, BETA1:BETA1 + 1], in1=xb,
                                                   op0=ALU.mult, op1=ALU.add).then_inc(x2_ready, 1)
                    if j >= 1:
                        dve.wait_ge(x2_ready, n)
                        nc.vector.bn_stats(stats[:, j - 1, :],
                                           res[:, par, (j - 1) * N:j * N]).then_inc(bn2_done, 1)
                dve.wait_ge(x2_ready, b * TAIL + TAIL)
                nc.vector.bn_stats(stats[:, TAIL - 1, :], res[:, par, HALF - N:HALF]).then_inc(bn2_done, 1)
                dve.wait_ge(bn2_done, b * TAIL + TAIL)
                norm_coefs(b * 2 + (1 if last else 2), LN2W, LN2B, ln2ab, ln2_ready)
                for o in range(2):
                    nc.vector.tensor_scalar(wbd3_b[:, o, :], wbd3[:, o, :], ln2ab[:, 0:1], None, ALU.mult)
                dve.wait_ge(b3_done, b + 1)
                nc.vector.tensor_tensor(bias3[:, :], bank[6][:, 8:10], col[:, PW3B1:PW3B2 + 1],
                                        ALU.add).then_inc(w3_ready, 1)
                dve.wait_ge(w3_ready, b + 1)
                for j in range(TAIL + 1):
                    if j < TAIL:
                        n = b * TAIL + j
                        dve.wait_ge(tgate2_ready, n + 1)
                        dve.wait_ge(u1_done, n + 1)
                        if not (first and j < 2):
                            dve.wait_ge(pw4_done, n - 1)
                        nc.vector.scalar_tensor_tensor(out=gate2[:, j % 2, :], in0=bank[(4, 7)[j % 2]][:, :],
                                                       scalar=bias3[:, 0:1], in1=t_gate[:, j % 2, :],
                                                       op0=ALU.add, op1=ALU.mult).then_inc(gate2_ready, 1)
                    if j >= 1:
                        n = b * TAIL + j - 1
                        dve.wait_ge(pw4_done, n + 1)
                        slot = (j - 1) // 4 % 2
                        if (j - 1) % 4 == 0 and not (first and j - 1 < 8):
                            dve.wait_ge(out_stored[slot], b * (32 * (TAIL // 8)) + (j - 1) // 8 * 32)
                        nc.vector.scalar_tensor_tensor(out=t_out[:, slot, (j - 1) % 4, :],
                                                       in0=bank[2 + (j - 1) % 2][:, :],
                                                       scalar=col[:, BETA2:BETA2 + 1],
                                                       in1=res[:, par, (j - 1) * N:j * N],
                                                       op0=ALU.mult, op1=ALU.add).then_inc(sum_ready, 1)

            each_batch(dve, batch)



NAMES = ["x", "L0_conv_bias", "L0_conv_up_filter", "L0_conv_dn_filter", "L1_conv_ln1_w", "L1_conv_ln1_b",
         "L1_conv_pw1_w", "L1_conv_pw1_b", "L1_conv_dw_w", "L1_conv_dw_b", "L1_conv_sca_w", "L1_conv_sca_b",
         "L1_conv_pw2_w", "L1_conv_pw2_b", "L1_conv_ln2_w", "L1_conv_ln2_b", "L1_conv_pw3_w",
         "L1_conv_pw3_b", "L1_conv_pw4_w", "L1_conv_pw4_b", "L1_conv_beta1", "L1_conv_beta2"]


def kernel(**inputs):
    import numpy as np
    import concourse.bacc as bacc
    from concourse.bass_utils import run_bass_kernel_spmd

    nc = bacc.Bacc("TRN2", target_bir_lowering=False, num_devices=1)
    arrays, args = {}, []
    for name in NAMES:
        a = np.ascontiguousarray(inputs[name])
        arrays[f"in_{name}"] = a
        args.append(nc.dram_tensor(f"in_{name}", a.shape, mybir.dt.from_np(a.dtype), kind="ExternalInput").ap())
    shape = inputs["x"].shape
    args.append(nc.dram_tensor("out_y", shape, F32, kind="ExternalOutput").ap())
    build(nc, *args)
    results = run_bass_kernel_spmd(nc, [arrays], core_ids=[0])
    return results.results[0]["out_y"]
```

```python
from contextlib import ExitStack

import concourse.bass as bass
from concourse import mybir

F32 = mybir.dt.float32
F32R = mybir.dt.float32r
I32 = mybir.dt.int32
ALU = mybir.AluOpType
ACT = mybir.ActivationFunctionType
AX = mybir.AxisListType

P = 128
UP = 2 * P
TAPS = 12
PAD_LO = (TAPS - 1) // 2
PAIRS = TAPS + 1
CENTRE = TAPS // 2 - 1
SLOPE = 0.2
GAIN = float(2.0 ** 0.5)
RANK1_TOL = 2.0 ** -21
LN_EPS = 1e-6


def build(nc, x, bias, up_filter, dn_filter, ln1_w, ln1_b, pw1_w, pw1_b, dw_w, dw_b, sca_w, sca_b,
          pw2_w, pw2_b, ln2_w, ln2_b, pw3_w, pw3_b, pw4_w, pw4_b, beta1, beta2, out):
    B, C, H, W = x.shape
    assert (C, H, W) == (64, P, P) and tuple(up_filter.shape) == (TAPS, TAPS)
    IMGS = B * C
    STEPS = IMGS // 2
    HW = H * W
    HALF = HW // 2
    CHUNK_ROWS = 16
    CHUNKS = H // CHUNK_ROWS
    BLOCK_ROWS = 4
    BLOCKS = CHUNK_ROWS // BLOCK_ROWS
    N = BLOCK_ROWS * W
    TAIL = HALF // N

    l0_out = nc.dram_tensor("l0_out", [IMGS, H, W], F32, kind="Internal").ap()
    x_rows = x.rearrange("b c h w -> h (b c) w")
    l0_rows = l0_out.rearrange("n h w -> h n w")
    l0_half = l0_out.rearrange("n (s r) w -> s n (r w)", s=2)
    out_half = out.rearrange("b c (s r) w -> s (b c) (r w)", s=2)

    with ExitStack() as ctx:
        def sb(name, shape, dt=F32):
            return ctx.enter_context(nc.sbuf_tensor(name, shape, dt))

        def sem(name):
            return ctx.enter_context(nc.semaphore(name))

        bank = [ctx.enter_context(nc.psum_tensor(f"bank{i}", [P, 512], F32)) for i in range(8)]

        filt = sb("filt", [P, 2, TAPS, TAPS])
        ratio = sb("ratio", [P, 2, TAPS, TAPS])
        resid = sb("resid", [P, 2, TAPS, TAPS])
        recip = sb("recip", [P, 2])
        factor = sb("factor", [P, 4, TAPS + 2])
        pairs = sb("pairs", [P, 4, PAIRS])
        fits = sb("fits", [P, 4])
        is_rank1 = sb("is_rank1", [P, 1], I32)
        BAND = 2 * UP
        tap_of = sb("tap_of", [P, BAND], I32)

        res = sb("res", [P, HALF])
        gate = sb("gate", [P, HALF])
        split = sb("split", [P, 2, CHUNK_ROWS + 2, W + 2], F32R)
        paired = sb("paired", [P, 2, CHUNK_ROWS + 2, W + 2], F32R)
        masked = gate[:, 0:PAIRS * BAND].rearrange("p (t o) -> p t o", t=PAIRS)

        t_out = sb("t_out", [P, 2, 2, N])
        part = sb("part", [P, 4, 2, N], F32R)

        band = t_out[:, :, :, :].rearrange("p a b n -> p (a b n)")[:, 0:2 * BAND].rearrange(
            "p (a o) -> p a o", a=2)
        band_hi, band_lo = (part[:, s, :, :].rearrange("p h n -> p (h n)").rearrange("p (a o) -> p a o", a=2)
                            for s in range(2))
        used = {}

        def work(home, pattern, **dims):
            n = 1
            for d in dims.values():
                n *= d
            at = used.get(id(home), 0)
            used[id(home)] = at + n
            assert at + n <= home.shape[-1]
            return home[:, at:at + n].rearrange(pattern, **dims)

        res_home = res[:, :]
        split_home = split[:, :, :, :].rearrange("p s r w -> p (s r w)")
        paired_home = paired[:, :, :, :].rearrange("p s r w -> p (s r w)")
        raw = work(res_home, "p (s m w) -> p s m w", s=2, m=4, w=W)
        biased = work(res_home, "p (s m w) -> p s m w", s=2, m=4, w=W)
        z = work(res_home, "p (s c m u) -> p s c m u", s=2, c=2, m=2, u=UP)
        y = work(res_home, "p (s m w) -> p s m w", s=2, m=4, w=W)
        x_hi, x_lo = (work(split_home, "p (s m w) -> p s m w", s=2, m=4, w=W) for _ in range(2))
        s1_hi, s1_lo = (work(split_home, "p (s m u) -> p s m u", s=2, m=2, u=UP) for _ in range(2))
        s3_hi, s3_lo = (work(paired_home, "p (s r n) -> p s r n", s=2, r=2, n=2 * W) for _ in range(2))

        filt_pad = sb("filt_pad", [P, 2, TAPS + 2, TAPS + 2])
        pairs2 = sb("pairs2", [P, 2, PAIRS, PAIRS])
        pairs1 = sb("pairs1", [P, 2, PAIRS, TAPS + 2])
        band2 = gate[:, 0:PAIRS * 2 * UP].rearrange("p (s o) -> p s o", s=PAIRS)
        used.clear()
        PADW = W + 6
        raw2 = work(res_home, "p (s m w) -> p s m w", s=2, m=4, w=W)
        x_pad = work(res_home, "p (s m w) -> p s m w", s=2, m=4, w=PADW)
        z_pad = work(res_home, "p (s q r m w) -> p s q r m w", s=2, q=2, r=2, m=4, w=PADW)
        y2 = work(res_home, "p (s m w) -> p s m w", s=2, m=4, w=W)

        rawc = sb("rawc", [P, 2, CHUNK_ROWS + 2, W])
        masked2 = rawc[:, :, :, :].rearrange("p s r w -> p (s r w)")[:, 0:PAIRS * UP].rearrange(
            "p (t o) -> p t o", t=PAIRS)
        bias_bc = rawc[:, :, :, :].rearrange("p s r w -> p (s r w)")[:, PAIRS * UP:PAIRS * UP + IMGS].rearrange(
            "p (b c) -> p b c", b=B)
        stage = sb("stage", [P, 2, 2 * N])
        w_hi = sb("w_hi", [P, 9, P], F32R)
        w_lo_pair = sb("w_lo_pair", [P, 3, P], F32R)
        w_lo_last = sb("w_lo_last", [P, 3, P], F32R)
        t_gate = sb("t_gate", [C, 2, N])
        t_gate2 = sb("t_gate2", [P, 2, N])
        gate2 = sb("gate2", [P, 2, N])
        ident = sb("ident", [P, P])
        swap = sb("swap", [P, P])
        diag_of = sb("diag_of", [P, P], I32)
        part_of = sb("part_of", [P, P], I32)
        w_nat = sb("w_nat", [P, 5, 2, C])
        w_tap = sb("w_tap", [P, 2, C])
        dwc = sb("dwc", [P, 9])
        colsum = sb("colsum", [P, 8])
        corr_o = sb("corr_o", [P, P])
        corr = sb("corr", [P, P])
        edge_cols = sb("edge_cols", [P, BLOCK_ROWS, 2])
        edge_top = sb("edge_top", [P, W])
        edge_bottom = sb("edge_bottom", [P, W])
        wbd2 = sb("wbd2", [P, P])
        wbd2_b = sb("wbd2_b", [P, P])
        wbd3 = sb("wbd3", [P, 2, P])
        wbd3_b = sb("wbd3_b", [P, 2, P])
        wbd4 = sb("wbd4", [P, P])
        wsca = sb("wsca", [P, P])
        w2_part = sb("w2_part", [P, 2, P], F32R)
        w3_part = sb("w3_part", [P, 2, 2, P], F32R)
        w4_part = sb("w4_part", [P, 2, P], F32R)
        col = sb("col", [P, 16])
        LN1W, LN1B, SCAB, PW2B, LN2W, LN2B, PW3B1, PW3B2, PW4B, BETA1, BETA2, OUTB = range(12)
        col_o = sb("col_o", [P, 4])
        stats1 = sb("stats1", [P, TAIL, 6])
        stats2 = sb("stats2", [P, TAIL, 6])
        mv = sb("mv", [P, 2])
        lnt = sb("lnt", [P, 8])
        ln1ab = sb("ln1ab", [P, 2])
        ln2ab = sb("ln2ab", [P, 2])
        bias3 = sb("bias3", [P, 2])
        gsum = sb("gsum", [P, CHUNKS * BLOCKS // 2])
        gtot = sb("gtot", [P, 1])
        attn = sb("attn", [P, 1])

        filt_landed = sem("filt_landed")
        const_landed = sem("const_landed")
        tap_index = sem("tap_index")
        dve_prep = sem("dve_prep")
        taps_ready = sem("taps_ready")
        corr_ready = sem("corr_ready")
        consts_ready = sem("consts_ready")
        bias_spread = sem("bias_spread")
        bands_ready = sem("bands_ready")
        x_landed = [sem(f"x_landed{i}") for i in range(2)]
        x_biased = sem("x_biased")
        x_hi_ready = sem("x_hi_ready")
        x_split = sem("x_split")
        s1_done = sem("s1_done")
        s1_hi_ready = sem("s1_hi_ready")
        s1_out = sem("s1_out")
        s2_done = sem("s2_done")
        z_scaled = sem("z_scaled")
        z_ready = sem("z_ready")
        s3_done = sem("s3_done")
        s3_hi_ready = sem("s3_hi_ready")
        s3_out = sem("s3_out")
        s4_done = sem("s4_done")
        y_ready = sem("y_ready")
        y_stored = [sem(f"y_stored{i}") for i in range(2)]
        rank_known = sem("rank_known")
        g_bands = sem("g_bands")
        g_chain = sem("g_chain")
        g_landed = [sem(f"g_landed{i}") for i in range(2)]
        g_zeroed = sem("g_zeroed")
        g_biased = sem("g_biased")
        g_up_done = sem("g_up_done")
        g_scaled = sem("g_scaled")
        g_z_ready = sem("g_z_ready")
        g_down_done = sem("g_down_done")
        g_y_ready = sem("g_y_ready")
        g_stored = [sem(f"g_stored{i}") for i in range(2)]
        pe_prep = sem("pe_prep")
        w1_ready = sem("w1_ready")
        res_landed = [sem(f"res_landed{i}") for i in range(4)]
        stage_landed = [sem(f"stage_landed{i}") for i in range(2)]
        pads_zeroed = sem("pads_zeroed")
        pair_top = sem("pair_top")
        pair_bottom = sem("pair_bottom")
        chunk_landed = [sem(f"chunk_landed{i}") for i in range(2)]
        chunk_normed = sem("chunk_normed")
        split_hi = sem("split_hi")
        split_done = sem("split_done")
        conv_done = sem("conv_done")
        tgate_ready = sem("tgate_ready")
        gate_done = sem("gate_done")
        bn1_done = sem("bn1_done")
        ln_chain = sem("ln_chain")
        stats_made = sem("stats_made")
        sp_waited = sem("sp_waited")
        mv_ready = sem("mv_ready")
        mv_swapped = sem("mv_swapped")
        var_ready = sem("var_ready")
        std_ready = sem("std_ready")
        ln1_ready = sem("ln1_ready")
        ln2_ready = sem("ln2_ready")
        gtot_ready = sem("gtot_ready")
        sca_done = sem("sca_done")
        attn_ready = sem("attn_ready")
        w2_ready = sem("w2_ready")
        gate_hi_ready = sem("gate_hi_ready")
        gate_parts = sem("gate_parts")
        x2_hi_ready = sem("x2_hi_ready")
        x2_parts = sem("x2_parts")
        gate2_hi_ready = sem("gate2_hi_ready")
        gate2_parts = sem("gate2_parts")
        pw2_done = sem("pw2_done")
        x2_ready = sem("x2_ready")
        bn2_done = sem("bn2_done")
        b3_done = sem("b3_done")
        w3_ready = sem("w3_ready")
        u2_done = sem("u2_done")
        u1_done = sem("u1_done")
        tgate2_ready = sem("tgate2_ready")
        gate2_ready = sem("gate2_ready")
        pw4_done = sem("pw4_done")
        sum_ready = sem("sum_ready")
        outb_ready = sem("outb_ready")
        out_stored = [sem(f"out_stored{i}") for i in range(2)]

        block = ctx.enter_context(nc.Block())

        def each_step(eng, step, lags):
            def live(g):
                return [0 <= g - lag < STEPS for lag in range(lags)]
            for g in range(8):
                step(g, g // 2, g % 4, live(g))
            with eng.Fori(2, STEPS // 4) as i:
                for k in range(4):
                    step(i * 4 + k, i * 2 + k // 2, k, [True] * lags)
            for g in range(STEPS, STEPS + lags - 1):
                step(g, g // 2, g % 4, live(g))

        UNITS = IMGS // 4

        def each_unit(eng, unit, lag):
            for u in range(4):
                unit(u, u % 2, True, u >= 1)
            with eng.Fori(2, UNITS // 2) as i:
                for k in range(2):
                    unit(i * 2 + k, k, True, True)
            if lag:
                unit(UNITS, 0, False, True)

        def by_rank(eng, separable, general):
            eng.wait_ge(rank_known, 1)
            flag = eng.value_load(is_rank1[0:1, 0:1], min_val=0, max_val=1)
            with eng.If(flag > 0):
                separable()
            with eng.Else():
                general()

        def each_batch(eng, batch):
            batch(0, True, False, B > 1)
            if B > 2:
                batch(1, True, True, True)
            if B > 3:
                with eng.Fori(0, B - 3) as i:
                    batch(i + 2, True, True, True)
            if B > 1:
                batch(B - 1, True, True, False)
            batch(B, False, True, False)

        SLOTS = CHUNKS * BLOCKS
        PW2_AT = 1
        LN2_AT = PW2_AT + TAIL // 2
        FFN_AT = LN2_AT + 3
        BN1_AT = BLOCKS
        LN1_AT = SLOTS - 8
        SPLIT_AT = SLOTS - BLOCKS
        PIECES = ((0, 6), (6, 12), (12, CHUNK_ROWS + 2))

        def ln2_index(b):
            return 2 * b if not (isinstance(b, int) and b == B) else 2 * B - 1

        @block.sync
        def _(sp):
            for f, src in enumerate((up_filter, dn_filter)):
                sp.dma_start(filt[:, f, :, :].rearrange("p a b -> p (a b)"),
                             src.rearrange("a b -> (a b)").partition_broadcast(P)).then_inc(filt_landed, 16)
            sp.dma_start(bias_bc[:, 0, :],
                         bias.rearrange("a c h w -> (a c h w)").partition_broadcast(P)).then_inc(filt_landed, 16)

            def load(u, slot, wait):
                if wait:
                    sp.wait_ge(x_biased, u - 1)
                sp.dma_start(raw[:, slot, :, :], x_rows[:, bass.ds(u * 4, 4), :]).then_inc(x_landed[slot], 16)

            def store(u, slot):
                sp.wait_ge(y_ready, u * 2 + 2)
                sp.dma_start(l0_rows[:, bass.ds(u * 4, 4), :], y[:, slot, :, :]).then_inc(y_stored[slot], 16)

            def separable():
                AHEAD = 4
                for u in range(AHEAD + 2):
                    load(u, u % 2, u >= 2)
                    if u >= AHEAD:
                        store(u - AHEAD, u % 2)
                with sp.Fori(3, UNITS // 2) as i:
                    for k in range(2):
                        load(i * 2 + k, k, True)
                        store(i * 2 + k - AHEAD, k)
                for u in range(UNITS - AHEAD, UNITS):
                    store(u, u % 2)
                for slot in range(2):
                    sp.wait_ge(y_stored[slot], 16 * (UNITS // 2))

            def general():
                def unit(u, slot, now, before):
                    if now:
                        if not (isinstance(u, int) and u < 2):
                            sp.wait_ge(g_biased, u - 1)
                        sp.dma_start(raw2[:, slot, :, :], x_rows[:, bass.ds(u * 4, 4), :]
                                     ).then_inc(g_landed[slot], 16)
                    if before:
                        sp.wait_ge(g_y_ready, u)
                        sp.dma_start(l0_rows[:, bass.ds(u * 4 - 4, 4), :], y2[:, 1 - slot, :, :]
                                     ).then_inc(g_stored[1 - slot], 16)
                each_unit(sp, unit, True)
                for slot in range(2):
                    sp.wait_ge(g_stored[slot], 16 * (UNITS // 2))

            by_rank(sp, separable, general)

            def load_stage(b, q):
                slot = q % 2
                if not (isinstance(b, int) and b == 0 and q < 2):
                    sp.wait_ge(bn1_done, b * TAIL + q * 2 - 2)
                    sp.sem_inc(sp_waited, 1)
                for s in range(2):
                    sp.dma_start(stage[64 * s:64 * s + 64, slot, :],
                                 l0_half[s, bass.ds(b * C, C), q * 2 * N:(q + 1) * 2 * N]
                                 ).then_inc(stage_landed[slot], 16)

            def load_chunk(b, c, slot, wait=True):
                q = b * CHUNKS + c
                if wait:
                    sp.wait_ge(split_done, (q - 1) * len(PIECES))
                    sp.wait_ge(pair_top, q - 1)
                    sp.wait_ge(pair_bottom, q - 1)
                    sp.sem_inc(sp_waited, 1)
                lo = 1 if c == 0 else 0
                n = CHUNK_ROWS + 2 - lo - (1 if c == CHUNKS - 1 else 0)
                row = 0 if c == 0 else c * CHUNK_ROWS - 1
                for s in range(2):
                    sp.dma_start(rawc[64 * s:64 * s + 64, slot, lo:lo + n, :],
                                 l0_out[bass.ds(b * C, C), row:row + n, :]).then_inc(chunk_landed[slot], 16)

            def load_res(b, q):
                if not (isinstance(b, int) and b == 0):
                    sp.wait_ge(sum_ready, b * TAIL - TAIL + q * 4 + 4)
                    sp.sem_inc(sp_waited, 1)
                for s in range(2):
                    sp.dma_start(res[64 * s:64 * s + 64, q * 4 * N:(q + 1) * 4 * N],
                                 l0_half[s, bass.ds(b * C, C), q * 4 * N:(q + 1) * 4 * N]
                                 ).then_inc(res_landed[q], 16)

            def store_out(b, q):
                slot = q % 2
                sp.wait_ge(outb_ready, b * TAIL + q * 2 + 2)
                sp.sem_inc(sp_waited, 1)
                for s in range(2):
                    sp.dma_start(out_half[s, bass.ds(b * C, C), q * 2 * N:(q + 1) * 2 * N],
                                 t_out[64 * s:64 * s + 64, slot, :, :].rearrange("p a n -> p (a n)")
                                 ).then_inc(out_stored[slot], 16)

            def batch(b, conv, tail, nxt):
                for c in range(CHUNKS):
                    if conv and c + 2 < CHUNKS:
                        load_chunk(b, c + 2, c % 2)
                    elif nxt and c + 2 >= CHUNKS:
                        load_chunk(b + 1, c + 2 - CHUNKS, c % 2)
                    if nxt and c < 4:
                        load_stage(b + 1, 2 * c)
                        load_stage(b + 1, 2 * c + 1)
                    if c >= 4:
                        if tail:
                            store_out(b - 1, 2 * (c - 4))
                            store_out(b - 1, 2 * (c - 4) + 1)
                        if conv:
                            load_res(b, c - 4)

            load_stage(0, 0)
            load_stage(0, 1)
            load_chunk(0, 0, 0, False)
            load_chunk(0, 1, 1, False)
            for q in range(2, TAIL // 2):
                load_stage(0, q)
            each_batch(sp, batch)
            for slot in range(2):
                sp.wait_ge(out_stored[slot], 32 * B * (TAIL // 4))

        @block.gpsimd
        def _(pool):
            for lo, n, base, step, per_row in ((0, UP, PAD_LO + 1, -1, 2), (UP, P, PAD_LO, -2, 1),
                                               (UP + P, P, P + PAD_LO, -2, 1)):
                pool.iota(tap_of[:, lo:lo + n], [[step, n]], base=base,
                          channel_multiplier=per_row).then_inc(tap_index, 1)
            pool.iota(diag_of[:, :], [[-1, P]], base=0, channel_multiplier=1).then_inc(tap_index, 1)
            pool.iota(part_of[:, :], [[0, P]], base=0, channel_multiplier=1).then_inc(tap_index, 1)
            pool.memset(corr_o[:, :], 0.0).then_inc(tap_index, 1)
            pool.memset(wbd2[:, :], 0.0).then_inc(tap_index, 1)
            pool.memset(wbd3[:, :, :], 0.0).then_inc(tap_index, 1)
            pool.memset(wbd4[:, :], 0.0).then_inc(tap_index, 1)
            pool.wait_ge(filt_landed, 48)
            for b in range(1, B):
                pool.tensor_copy(bias_bc[:, b, :], bias_bc[:, 0, :]).then_inc(bias_spread, 1)
            if B > 1:
                pool.wait_ge(bias_spread, B - 1)
            bias_flat = bias_bc[:, :, :].rearrange("p b c -> p (b c)")

            def separable():
                def unit(u, slot, now, before):
                    pool.wait_ge(x_landed[slot], (u - slot) * 8 + 16)
                    pool.tensor_tensor(biased[:, slot, :, :], raw[:, slot, :, :],
                                       bias_flat[:, bass.ds(u * 4, 4)].unsqueeze(2).to_broadcast([P, 4, W]),
                                       ALU.add).then_inc(x_biased, 1)
                    pool.wait_ge(x_hi_ready, u + 1)
                    pool.tensor_tensor(x_lo[:, slot, :, :], biased[:, slot, :, :], x_hi[:, slot, :, :],
                                       ALU.subtract).then_inc(x_split, 1)
                each_unit(pool, unit, False)
                pool.wait_ge(s4_done, STEPS)

            def general():
                pool.memset(x_pad[:, :, :, :], 0.0).then_inc(g_zeroed, 1)
                pool.memset(z_pad[:, :, :, :, :, :], 0.0).then_inc(g_zeroed, 1)
                pool.wait_ge(g_zeroed, 2)

                def unit(u, slot, now, before):
                    pool.wait_ge(g_landed[slot], (u - slot) * 8 + 16)
                    if not (isinstance(u, int) and u < 2):
                        pool.wait_ge(g_up_done, u * 4 - 4)
                    pool.tensor_tensor(x_pad[:, slot, :, 3:3 + W], raw2[:, slot, :, :],
                                       bias_flat[:, bass.ds(u * 4, 4)].unsqueeze(2).to_broadcast([P, 4, W]),
                                       ALU.add).then_inc(g_biased, 1)
                each_unit(pool, unit, False)

            by_rank(pool, separable, general)
            pool.memset(split[:, :, :, :].bitcast(F32), 0.0).then_inc(pads_zeroed, 1)
            pool.memset(paired[:, :, :, :].bitcast(F32), 0.0).then_inc(pads_zeroed, 1)
            pool.wait_ge(pads_zeroed, 2)

            def split_lo(b, c, piece):
                slot, q = c % 2, b * CHUNKS + c
                lo, hi = PIECES[piece]
                if c == 0:
                    lo = max(lo, 1)
                if c == CHUNKS - 1:
                    hi = min(hi, CHUNK_ROWS + 1)
                if piece == 0:
                    pool.wait_ge(split_hi, q + 1)
                pool.tensor_tensor(split[C:P, slot, lo:hi, 1:W + 1], rawc[C:P, slot, lo:hi, :],
                                   split[C:P, slot, lo:hi, 1:W + 1], ALU.subtract).then_inc(split_done, 1)
                pool.wait_ge(split_done, q * len(PIECES) + piece + 1)

            def tail_lo(source, hi_ready, n, slot, done):
                pool.wait_ge(hi_ready, n + 1)
                pool.tensor_tensor(part[:, slot, 1, :], source, part[:, slot, 0, :],
                                   ALU.subtract).then_inc(done, 1)
                pool.wait_ge(done, n + 1)

            for piece in range(len(PIECES)):
                split_lo(0, 0, piece)

            def batch(b, conv, tail, nxt):
                for i in range(SLOTS):
                    if tail and i < TAIL // 2:
                        for j in (2 * i, 2 * i + 1):
                            tail_lo(gate[:, j * N:(j + 1) * N], gate_hi_ready, (b - 1) * TAIL + j, j % 4,
                                    gate_parts)
                    j = i - FFN_AT
                    if tail and 0 <= j + 1 < TAIL:
                        tail_lo(res[:, (j + 1) * N:(j + 2) * N], x2_hi_ready, (b - 1) * TAIL + j + 1,
                                (j + 1) % 2, x2_parts)
                    if conv and i % BLOCKS < len(PIECES) and i < SLOTS - BLOCKS:
                        split_lo(b, i // BLOCKS + 1, i % BLOCKS)
                    if nxt and 0 <= i - SPLIT_AT < len(PIECES):
                        split_lo(b + 1, 0, i - SPLIT_AT)
                    if tail and 0 <= j < TAIL:
                        tail_lo(gate2[:, j % 2, :], gate2_hi_ready, (b - 1) * TAIL + j, 2 + j % 2, gate2_parts)

            each_batch(pool, batch)

        @block.tensor
        def _(pe):
            def parts(t, a, lo, n):
                return t[:, a, lo:lo + n]

            def step(g, u, k, live):
                if live[2]:
                    h, kk = g - 2, (k - 2) % 4
                    slot, pos = kk // 2, 2 * (kk % 2)
                    if kk % 2 == 0:
                        pe.wait_ge(x_split, u)
                    if not (isinstance(h, int) and h < 1):
                        pe.wait_ge(s1_out, h)
                    for m in range(2):
                        for n, (xp, wp) in enumerate(((x_hi, band_lo), (x_hi, band_hi), (x_lo, band_hi))):
                            mm = nc.tensor.matmul(bank[0][:, m * UP:(m + 1) * UP], xp[:, slot, pos + m, :],
                                                  parts(wp, 0, 0, UP), start=(m == 0 and n == 0),
                                                  stop=(n == 2), skip_group_check=True)
                    mm.then_inc(s1_done, 1)
                if live[3]:
                    h, par = g - 3, (k - 3) % 2
                    pe.wait_ge(s1_out, h + 1)
                    for c in range(2):
                        if not (isinstance(h, int) and h < 1):
                            pe.wait_ge(z_ready, h * 2 - 1 + c)
                        for n, (wp, dp) in enumerate(((band_lo, s1_hi), (band_hi, s1_hi), (band_hi, s1_lo))):
                            mm = nc.tensor.matmul(bank[1 + c][:, :], parts(wp, 1, c * P, P),
                                                  dp[:, par, :, :].rearrange("p m u -> p (m u)"),
                                                  start=(n == 0), stop=(n == 2))
                        mm.then_inc(s2_done, 1)
                if live[4]:
                    h, par = g - 4, k % 2
                    pe.wait_ge(z_ready, h * 2 + 2)
                    if not (isinstance(h, int) and h < 1):
                        pe.wait_ge(s3_out, h)
                    acc = bank[3][:, :].rearrange("p (r m w) -> p r m w", r=2, m=2)
                    for n in range(8):
                        r, m, c = n // 4, n // 2 % 2, n % 2
                        mm = nc.tensor.matmul(acc[:, r, m, :], z[:, par, c, m, r * P:(r + 1) * P],
                                              parts(band, 1, UP + c * P, P),
                                              start=(n == 0), stop=(c == 1), skip_group_check=True)
                    mm.then_inc(s3_done, 1)
                if live[5]:
                    h, par = g - 5, (k - 5) % 2
                    pe.wait_ge(s3_out, h + 1)
                    if not (isinstance(h, int) and h < 1):
                        pe.wait_ge(y_ready, h)
                    for r in range(2):
                        for n, (wp, dp) in enumerate(((band_lo, s3_hi), (band_hi, s3_hi), (band_hi, s3_lo))):
                            mm = nc.tensor.matmul(bank[4][:, 0:2 * W], parts(wp, 0, UP + r * P, P),
                                                  dp[:, par, r, :], start=(r == 0 and n == 0),
                                                  stop=(r == 1 and n == 2))
                    mm.then_inc(s4_done, 1)

            for t in range(9):
                pe.wait_ge(taps_ready, t + 1)
                if t >= 1:
                    pe.wait_ge(w1_ready, t)
                nc.tensor.matmul(bank[5][:, 0:P], masked[:, t, 0:P], ident[:, :],
                                 start=True, stop=True).then_inc(pe_prep, 1)
            pe.wait_ge(corr_ready, 1)
            nc.tensor.matmul(bank[6][:, 0:P], corr_o[:, :], ident[:, :], start=True, stop=True)
            nc.tensor.matmul(bank[6][:, P:2 * P], w_nat[:, 1, :, :].rearrange("p a c -> p (a c)"),
                             ident[:, :], start=True, stop=True)
            for n, at in ((2, 2 * P), (3, 2 * P + C), (4, 3 * P)):
                mm = nc.tensor.matmul(bank[6][:, at:at + C], w_nat[0:C, n, :, :].rearrange("p a c -> p (a c)"),
                                      ident[0:C, 0:C], start=True, stop=True)
            mm.then_inc(pe_prep, 1)

            def separable():
                pe.wait_ge(bands_ready, 1)
                each_step(pe, step, 6)

            def general():
                pe.wait_ge(g_bands, 1)
                pe.wait_ge(g_zeroed, 2)

                def unit(u, slot, now, before):
                    if now:
                        pe.wait_ge(g_biased, u + 1)
                        for q in range(2):
                            for h in range(2):
                                acc = bank[2 * q + h]
                                if not (isinstance(u, int) and u < 1):
                                    pe.wait_ge(g_z_ready, u * 4 - 3 + 2 * q + h)
                                taps = range(q, PAIRS, 2)
                                for t in taps:
                                    at = 3 + (t + q - 6) // 2
                                    mm = nc.tensor.matmul(acc[:, :], band2[:, t, h * P:(h + 1) * P],
                                                          x_pad[:, slot, :, at:at + W],
                                                          start=(t == q), stop=(t == taps[-1]))
                                mm.then_inc(g_up_done, 1)
                    if before:
                        pe.wait_ge(g_z_ready, u * 4)
                        if not (isinstance(u, int) and u < 2):
                            pe.wait_ge(g_y_ready, u - 1)
                        n = 0
                        for t in range(PAIRS):
                            q = (t + 1) % 2
                            at = 3 + (t - 5 - q) // 2
                            for h in range(2):
                                mm = nc.tensor.matmul(bank[4][:, :], band2[:, t, UP + h * P:UP + (h + 1) * P],
                                                      z_pad[:, 1 - slot, q, h, :, at:at + W],
                                                      start=(n == 0), stop=(n == 2 * PAIRS - 1))
                                n += 1
                        mm.then_inc(g_down_done, 1)
                each_unit(pe, unit, True)

            by_rank(pe, separable, general)

            pe.wait_ge(consts_ready, 1)

            pe.wait_ge(pads_zeroed, 2)

            def conv_block(b, i):
                c, j = i // BLOCKS, i % BLOCKS
                slot, q, n = c % 2, b * CHUNKS + c, b * SLOTS + i
                if j == 0:
                    pe.wait_ge(split_done, (q + 1) * len(PIECES))
                    pe.wait_ge(pair_top, q + 1)
                    pe.wait_ge(pair_bottom, q + 1)
                if not (isinstance(b, int) and b == 0 and i < 3):
                    pe.wait_ge(gate_done, n - (1, 1, 4)[i] if i < 3 else n - 2)
                acc = bank[i % 3]

                def window(tile, t):
                    lo = BLOCK_ROWS * j + t // 3
                    return tile[:, slot, lo:lo + BLOCK_ROWS, t % 3:t % 3 + W]

                for t in range(3):
                    nc.tensor.matmul(acc[:, :], w_lo_pair[:, t, :], window(paired, t), start=(t == 0),
                                     stop=False, skip_group_check=True)
                    nc.tensor.matmul(acc[:, :], w_lo_last[:, t, :], window(paired, 6 + t), start=False,
                                     stop=False, skip_group_check=True)
                nc.tensor.matmul(acc[:, :].rearrange("p (r w) -> p r w", w=W)[:, :, 0:W:W - 1],
                                 corr[:, :], edge_cols[:, :, :], start=False, stop=False,
                                 skip_group_check=True)
                if i == 0:
                    nc.tensor.matmul(acc[:, 0:W], corr[:, :], edge_top[:, :], start=False,
                                     stop=False, skip_group_check=True)
                if i == SLOTS - 1:
                    nc.tensor.matmul(acc[:, N - W:N], corr[:, :], edge_bottom[:, :],
                                     start=False, stop=False, skip_group_check=True)
                for t in range(9):
                    mm = nc.tensor.matmul(acc[:, :], w_hi[:, t, :], window(split, t), start=False,
                                          stop=(t == 8), skip_group_check=True)
                mm.then_inc(conv_done, 1)

            def swap_stats(n):
                pe.wait_ge(mv_ready, n + 1)
                nc.tensor.matmul(bank[7][:, 0:2], swap[:, :], mv[:, :], start=True,
                                 stop=True).then_inc(mv_swapped, 1)

            swap_stats(0)

            def three_terms(acc, w, data):
                nc.tensor.matmul(acc[:, :], w[:, 1, :], data[:, 0, :], start=True, stop=False)
                nc.tensor.matmul(acc[:, :], w[:, 0, :], data[:, 0, :], start=False, stop=False)
                return nc.tensor.matmul(acc[:, :], w[:, 0, :], data[:, 1, :], start=False, stop=True)

            def pw2_block(b, j):
                if j >= 2:
                    pe.wait_ge(x2_ready, b * TAIL + j - 1)
                elif not (isinstance(b, int) and b == 0):
                    pe.wait_ge(sum_ready, b * TAIL - 1 + j)
                pe.wait_ge(gate_parts, b * TAIL + j + 1)
                three_terms(bank[3 + j % 2], w2_part, part[:, j % 4, :, :]).then_inc(pw2_done, 1)

            def ffn_block(b, j):
                n = b * TAIL + j
                if j >= 2:
                    pe.wait_ge(gate2_parts, n - 1)
                    if j >= 4:
                        pe.wait_ge(sum_ready, n - 3)
                    three_terms(bank[3 + j % 2], w4_part, part[:, 2 + j % 2, :, :]).then_inc(pw4_done, 1)
                if j < TAIL:
                    pe.wait_ge(x2_parts, n + 1)
                    if not (isinstance(b, int) and b == 0 and j < 1):
                        pe.wait_ge(tgate2_ready, n)
                    three_terms(bank[5], w3_part[:, :, 1, :], part[:, j % 2, :, :]).then_inc(u2_done, 1)
                    if not (isinstance(b, int) and b == 0 and j < 1):
                        pe.wait_ge(gate2_ready, n)
                    three_terms(bank[6], w3_part[:, :, 0, :], part[:, j % 2, :, :]).then_inc(u1_done, 1)

            def batch(b, conv, tail, nxt):
                for i in range(SLOTS):
                    if tail and i == LN2_AT + 2:
                        swap_stats(ln2_index(b))
                    if tail and i == FFN_AT:
                        pe.wait_ge(ln2_ready, b)
                        for o in range(2):
                            mm = nc.tensor.matmul(bank[7][:, 8 + o:9 + o], wbd3[:, o, :], ln2ab[:, 1:2],
                                                  start=True, stop=True)
                        mm.then_inc(b3_done, 1)
                    if nxt and i == LN1_AT + 2:
                        swap_stats(b * 2 + 1)
                    if conv:
                        conv_block(b, i)
                    if tail and i == 0:
                        pe.wait_ge(gtot_ready, b)
                        nc.tensor.matmul(bank[7][:, 4:5], wsca[:, :], gtot[:, :], start=True,
                                         stop=True).then_inc(sca_done, 1)
                    if tail and PW2_AT <= i < LN2_AT:
                        if i == PW2_AT:
                            pe.wait_ge(w2_ready, 3 * b)
                        for j in range(2):
                            pw2_block(b - 1, 2 * (i - PW2_AT) + j)
                    if tail and FFN_AT <= i < FFN_AT + TAIL + 2:
                        if i == FFN_AT:
                            pe.wait_ge(w3_ready, 3 * b)
                        ffn_block(b - 1, i - FFN_AT)

            each_batch(pe, batch)

        @block.scalar
        def _(act):
            def col_load(n, src, lo=0):
                for s in range(2):
                    act.dma_start(col[64 * s:64 * s + 64, n:n + 1], src[lo:lo + C, :]).then_inc(const_landed, 16)

            vec4 = "a c h w -> c (a h w)"
            col_load(LN1W, ln1_w.rearrange(vec4))
            col_load(LN1B, ln1_b.rearrange(vec4))
            col_load(SCAB, sca_b.rearrange("(c a) -> c a", a=1))
            col_load(PW2B, pw2_b.rearrange("(c a) -> c a", a=1))
            col_load(LN2W, ln2_w.rearrange(vec4))
            col_load(LN2B, ln2_b.rearrange(vec4))
            col_load(PW3B1, pw3_b.rearrange("(c a) -> c a", a=1))
            col_load(PW3B2, pw3_b.rearrange("(c a) -> c a", a=1), C)
            col_load(PW4B, pw4_b.rearrange("(c a) -> c a", a=1))
            col_load(BETA1, beta1.rearrange(vec4))
            col_load(BETA2, beta2.rearrange(vec4))
            act.dma_start(col_o[:, 0:1], dw_b.rearrange("(c a) -> c a", a=1)).then_inc(const_landed, 16)
            act.dma_start(col_o[:, 1:2], pw1_b.rearrange("(c a) -> c a", a=1)).then_inc(const_landed, 16)
            act.dma_start(dwc[:, :], dw_w.rearrange("o a h w -> o (a h w)")).then_inc(const_landed, 16)
            for n, (src, rows) in enumerate(((pw1_w, P), (pw3_w, P), (pw2_w, C), (pw4_w, C), (sca_w, C))):
                for s in range(2):
                    act.dma_start(w_nat[0:rows, n, s, :], src[:, :]).then_inc(const_landed, 16)

            def step(g, u, k, live):
                if live[0] and k % 2 == 0:
                    act.wait_ge(x_biased, u + 1)
                    if not (isinstance(u, int) and u < 2):
                        act.wait_ge(s1_done, u * 2 - 2)
                    nc.scalar.activation(x_hi[:, k // 2, :, :], biased[:, k // 2, :, :],
                                         ACT.Copy).then_inc(x_hi_ready, 1)
                if live[2]:
                    h, par = g - 2, k % 2
                    act.wait_ge(s1_done, h + 1)
                    if not (isinstance(h, int) and h < 2):
                        act.wait_ge(s2_done, h * 2 - 2)
                    nc.scalar.activation(s1_hi[:, par, :, :].rearrange("p m u -> p (m u)"), bank[0][:, :],
                                         ACT.Copy).then_inc(s1_hi_ready, 1)
                if live[3]:
                    h, par = g - 3, (k - 3) % 2
                    for c in range(2):
                        act.wait_ge(s2_done, h * 2 + 1 + c)
                        if c == 0 and not (isinstance(h, int) and h < 2):
                            act.wait_ge(s3_done, h - 1)
                        nc.scalar.activation(z[:, par, c, :, :].rearrange("p m u -> p (m u)"),
                                             bank[1 + c][:, :], ACT.Copy, scale=SLOPE).then_inc(z_scaled, 1)
                if live[4]:
                    h, par = g - 4, k % 2
                    act.wait_ge(s3_done, h + 1)
                    if not (isinstance(h, int) and h < 2):
                        act.wait_ge(s4_done, h - 1)
                    nc.scalar.activation(s3_hi[:, par, :, :].rearrange("p r n -> p (r n)"), bank[3][:, :],
                                         ACT.Copy).then_inc(s3_hi_ready, 1)

            def general():
                act.wait_ge(g_zeroed, 2)

                def unit(u, slot, now, before):
                    for n in range(4):
                        q, h = n // 2, n % 2
                        act.wait_ge(g_up_done, u * 4 + n + 1)
                        if n == 0 and not (isinstance(u, int) and u < 2):
                            act.wait_ge(g_down_done, u - 1)
                        nc.scalar.activation(z_pad[:, slot, q, h, :, 3:3 + W],
                                             bank[n][:, :].rearrange("p (m w) -> p m w", w=W),
                                             ACT.Copy, scale=SLOPE).then_inc(g_scaled, 1)
                each_unit(act, unit, False)

            by_rank(act, lambda: each_step(act, step, 6), general)

            act.wait_ge(consts_ready, 1)

            act.wait_ge(pads_zeroed, 2)

            def norm_chunk(b, c):
                slot = c % 2
                lo, hi = (1 if c == 0 else 0), CHUNK_ROWS + (1 if c == CHUNKS - 1 else 2)
                act.wait_ge(chunk_landed[slot], b * (16 * CHUNKS) + (c - slot) * 16 + 32)
                flat = rawc[:, slot, lo:hi, :].rearrange("p r w -> p (r w)")
                nc.scalar.activation(flat, flat, ACT.Identity, bias=ln1ab[:, 1:2],
                                     scale=ln1ab[:, 0:1]).then_inc(chunk_normed, 1)

            def pair_chunk(b, c):
                slot, q = c % 2, b * CHUNKS + c
                lo, hi = (1 if c == 0 else 0), CHUNK_ROWS + (1 if c == CHUNKS - 1 else 2)
                act.wait_ge(chunk_normed, q + 1)
                if not (isinstance(b, int) and b == 0 and c < 2):
                    act.wait_ge(conv_done, (q - 1) * BLOCKS)
                nc.scalar.activation(paired[0:C, slot, lo:hi, 1:W + 1], rawc[0:C, slot, lo:hi, :],
                                     ACT.Copy).then_inc(pair_top, 1)

            def gate_block(b, i):
                n = b * SLOTS + i
                act.wait_ge(conv_done, n + 1)
                if not (isinstance(b, int) and b == 0 and i < 2):
                    act.wait_ge(gate_done, n - 1)
                nc.scalar.activation(t_gate[:, i % 2, :], bank[i % 3][C:P, :], ACT.Identity,
                                     bias=col_o[C:P, 2:3]).then_inc(tgate_ready, 1)

            def sqrt_var(n):
                act.wait_ge(var_ready, n + 1)
                nc.scalar.activation(lnt[:, 4:5], lnt[:, 3:4], ACT.Sqrt).then_inc(std_ready, 1)

            def gate_hi(b, j):
                if j >= 4:
                    act.wait_ge(pw2_done, b * TAIL + j - 3)
                nc.scalar.activation(part[:, j % 4, 0, :], gate[:, j * N:(j + 1) * N],
                                     ACT.Copy).then_inc(gate_hi_ready, 1)

            def x2_hi(b, j):
                act.wait_ge(x2_ready, b * TAIL + (TAIL if j < 2 else j + 1))
                if j >= 2:
                    act.wait_ge(u1_done, b * TAIL + j - 1)
                nc.scalar.activation(part[:, j % 2, 0, :], res[:, j * N:(j + 1) * N],
                                     ACT.Copy).then_inc(x2_hi_ready, 1)

            def ffn_block(b, j):
                n = b * TAIL + j
                if j < TAIL:
                    act.wait_ge(u2_done, n + 1)
                    if not (isinstance(b, int) and b == 0 and j < 2):
                        act.wait_ge(gate2_ready, n - 1)
                    nc.scalar.activation(t_gate2[:, j % 2, :], bank[5][:, :], ACT.Identity,
                                         bias=bias3[:, 1:2]).then_inc(tgate2_ready, 1)
                if j >= 2:
                    act.wait_ge(sum_ready, n - 1)
                    o = t_out[:, (j - 2) // 2 % 2, (j - 2) % 2, :]
                    nc.scalar.activation(o, o, ACT.Identity,
                                         bias=col[:, OUTB:OUTB + 1]).then_inc(outb_ready, 1)
                if j < TAIL:
                    act.wait_ge(gate2_ready, n + 1)
                    if j >= 2:
                        act.wait_ge(pw4_done, n - 1)
                    nc.scalar.activation(part[:, 2 + j % 2, 0, :], gate2[:, j % 2, :],
                                         ACT.Copy).then_inc(gate2_hi_ready, 1)

            sqrt_var(0)
            act.wait_ge(ln1_ready, 1)
            norm_chunk(0, 0)
            pair_chunk(0, 0)

            def batch(b, conv, tail, nxt):
                for i in range(SLOTS):
                    if tail and i == 0:
                        act.wait_ge(gate_done, b * SLOTS)
                    if tail and i < TAIL // 2:
                        for j in range(2):
                            gate_hi(b - 1, 2 * i + j)
                    if tail and 0 <= i - FFN_AT + 1 < TAIL:
                        x2_hi(b - 1, i - FFN_AT + 1)
                    if conv and i % BLOCKS == 0 and i < SLOTS - BLOCKS:
                        norm_chunk(b, i // BLOCKS + 1)
                        pair_chunk(b, i // BLOCKS + 1)
                    if nxt and i == SPLIT_AT:
                        pair_chunk(b + 1, 0)
                    if conv:
                        gate_block(b, i)
                    if tail and i == 0:
                        act.wait_ge(sca_done, b)
                        nc.scalar.activation(attn[:, :], bank[7][:, 4:5], ACT.Sigmoid,
                                             bias=col[:, SCAB:SCAB + 1]).then_inc(attn_ready, 1)
                    if tail and i == LN2_AT + 1:
                        sqrt_var(ln2_index(b))
                    if tail and FFN_AT <= i < FFN_AT + TAIL + 2:
                        ffn_block(b - 1, i - FFN_AT)
                    if nxt and i == LN1_AT + 1:
                        sqrt_var(b * 2 + 1)
                    if nxt and i == LN1_AT + 2:
                        act.wait_ge(ln1_ready, b + 2)
                        norm_chunk(b + 1, 0)

            each_batch(act, batch)

        @block.vector
        def _(dve):
            made = [0]

            def prep(ins):
                made[0] += 1
                ins.then_inc(dve_prep, 1)
                dve.wait_ge(dve_prep, made[0])

            dve.wait_ge(filt_landed, 48)
            prep(nc.vector.memset(factor[:, :, :], 0.0))
            for f in range(2):
                c0 = filt[:, f, CENTRE, CENTRE:CENTRE + 1]
                prep(nc.vector.reciprocal(recip[:, f:f + 1], c0))
                prep(nc.vector.tensor_scalar(ratio[:, f, :, :], filt[:, f, :, :], recip[:, f:f + 1], None, ALU.mult))
                prep(nc.vector.tensor_tensor(
                    resid[:, f, :, :], ratio[:, f, :, CENTRE:CENTRE + 1].to_broadcast([P, TAPS, TAPS]),
                    ratio[:, f, CENTRE:CENTRE + 1, :].to_broadcast([P, TAPS, TAPS]), ALU.mult))
                prep(nc.vector.tensor_copy(factor[:, 2 * f, 1:TAPS + 1], filt[:, f, :, CENTRE]))
                prep(nc.vector.tensor_copy(factor[:, 2 * f + 1, 1:TAPS + 1], ratio[:, f, CENTRE, :]))
            prep(nc.vector.tensor_scalar(factor[:, 2, :], factor[:, 2, :], 0.5, None, ALU.mult))
            prep(nc.vector.tensor_scalar(factor[:, 3, :], factor[:, 3, :], 0.5 * GAIN, None, ALU.mult))
            prep(nc.vector.tensor_tensor(pairs[:, :, :], factor[:, :, 0:PAIRS], factor[:, :, 1:PAIRS + 1], ALU.add))
            prep(nc.vector.tensor_tensor(resid[:, :, :, :], ratio[:, :, :, :], resid[:, :, :, :], ALU.subtract))
            for t in (resid, ratio):
                prep(nc.vector.scalar_tensor_tensor(
                    out=t[:, :, :, :].rearrange("p f a b -> p (f a b)"),
                    in0=t[:, :, :, :].rearrange("p f a b -> p (f a b)"), scalar=-1.0,
                    in1=t[:, :, :, :].rearrange("p f a b -> p (f a b)"), op0=ALU.mult, op1=ALU.max))
            prep(nc.vector.scalar_tensor_tensor(
                out=resid[:, :, :, :].rearrange("p f a b -> p (f a b)"),
                in0=ratio[:, :, :, :].rearrange("p f a b -> p (f a b)"), scalar=RANK1_TOL,
                in1=resid[:, :, :, :].rearrange("p f a b -> p (f a b)"), op0=ALU.mult, op1=ALU.is_ge))
            prep(nc.vector.tensor_reduce(fits[:, 0:1], resid[:, :, :, :].rearrange("p f a b -> p (f a b)"),
                                         AX.X, ALU.min))
            prep(nc.vector.tensor_copy(is_rank1[:, :], fits[:, 0:1]))
            dve.sem_inc(rank_known, 1)
            dve.wait_ge(tap_index, 9)
            for a in range(2):
                for lo, hi, f in ((0, UP, 0), (UP, BAND, 1)):
                    for t in range(PAIRS):
                        ins = nc.vector.tensor_scalar(masked[:, t, lo:hi], tap_of[:, lo:hi], float(t),
                                                      pairs[:, 2 * f + a, t:t + 1], ALU.is_equal, ALU.mult)
                    prep(ins)
                prep(nc.vector.tensor_reduce(band[:, a, :], masked[:, :, :].rearrange("p t o -> p o t"),
                                             AX.X, ALU.add))
            prep(nc.vector.tensor_copy(band_hi[:, :, :], band[:, :, :]))
            prep(nc.vector.tensor_tensor(band_lo[:, :, :], band[:, :, :], band_hi[:, :, :], ALU.subtract))
            dve.sem_inc(bands_ready, 1)

            prep(nc.vector.tensor_scalar(ident[:, :], diag_of[:, :], 0.0, None, ALU.is_equal))
            prep(nc.vector.tensor_scalar(swap[:, :], diag_of[:, :], float(C), None, ALU.is_equal))
            prep(nc.vector.tensor_scalar(corr[:, :], diag_of[:, :], float(-C), None, ALU.is_equal))
            prep(nc.vector.tensor_tensor(swap[:, :], swap[:, :], corr[:, :], ALU.add))
            dve.wait_ge(const_landed, 16 * 35)
            for t in range(9):
                prep(nc.vector.tensor_scalar(masked[:, t, 0:P], w_nat[:, 0, :, :].rearrange("p a c -> p (a c)"),
                                             dwc[:, t:t + 1], None, ALU.mult))
                dve.sem_inc(taps_ready, 1)
            def tap_sum(n, view, negate=False):
                prep(nc.vector.tensor_reduce(colsum[:, 0:1], view, AX.X, ALU.add, negate=negate))
                prep(nc.vector.tensor_tensor(corr_o[:, n:n + 1], colsum[:, 0:1], col_o[:, 1:2], ALU.mult))

            for n, view in enumerate((dwc[:, 0:3], dwc[:, 6:9], dwc[:, 0:9:3], dwc[:, 2:9:3])):
                tap_sum(n, view)
                prep(nc.vector.tensor_scalar(corr_o[:, n:n + 1], corr_o[:, n:n + 1], -1.0, None, ALU.mult))
            for n, t in enumerate((0, 2, 6, 8)):
                tap_sum(4 + n, dwc[:, t:t + 1])
            prep(nc.vector.tensor_reduce(colsum[:, 0:1], dwc[:, :], AX.X, ALU.add))
            prep(nc.vector.scalar_tensor_tensor(out=col_o[:, 2:3], in0=colsum[:, 0:1], scalar=col_o[:, 1:2],
                                                in1=col_o[:, 0:1], op0=ALU.mult, op1=ALU.add))
            dve.sem_inc(corr_ready, 1)
            def where(dst, n):
                return nc.vector.tensor_scalar(dst, part_of[:, 0:1] if dst.shape[-1] == 1 else part_of[:, :],
                                               float(n), None, ALU.is_equal)
            prep(where(edge_top[:, :], 0))
            prep(where(edge_bottom[:, :], 1))
            for dst, corners in ((edge_top, (4, 5)), (edge_bottom, (6, 7))):
                for at, n in zip((0, W - 1), corners):
                    prep(where(colsum[:, 0:1], n))
                    prep(nc.vector.tensor_tensor(dst[:, at:at + 1], dst[:, at:at + 1], colsum[:, 0:1], ALU.add))
            for r in range(BLOCK_ROWS):
                for s in range(2):
                    prep(where(edge_cols[:, r, s:s + 1], 2 + s))
            prep(nc.vector.memset(w_lo_last[:, :, :].bitcast(F32), 0.0))
            for t in range(9):
                dve.wait_ge(pe_prep, t + 1)
                prep(nc.vector.tensor_copy(w_hi[:, t, :], bank[5][:, 0:P]))
                lanes = slice(C, P) if t // 3 == 1 else slice(0, C)
                low = w_lo_last if t // 3 == 2 else w_lo_pair
                nc.vector.tensor_tensor(low[lanes, t % 3, :], bank[5][lanes, 0:P], w_hi[lanes, t, :],
                                        ALU.subtract).then_inc(w1_ready, 1)
            dve.wait_ge(pe_prep, 10)
            prep(nc.vector.tensor_copy(corr[:, :], bank[6][:, 0:P]))
            for s in range(2):
                lanes, own = slice(64 * s, 64 * s + 64), slice(64 * s, 64 * s + 64)
                for o in range(2):
                    prep(nc.vector.tensor_copy(wbd3[lanes, o, own], bank[6][lanes, P + C * o:P + C * o + C]))
                prep(nc.vector.tensor_copy(wbd2[lanes, own], bank[6][lanes, 2 * P:2 * P + C]))
                prep(nc.vector.tensor_copy(wbd4[lanes, own], bank[6][lanes, 2 * P + C:3 * P]))
                prep(nc.vector.tensor_scalar(wsca[:, own], bank[6][:, 3 * P:3 * P + C], 1.0 / HW, None, ALU.mult))
            prep(nc.vector.tensor_copy(w4_part[:, 0, :], wbd4[:, :]))
            prep(nc.vector.tensor_tensor(w4_part[:, 1, :], wbd4[:, :], w4_part[:, 0, :], ALU.subtract))
            prep(nc.vector.tensor_tensor(colsum[:, 1:2], col[:, PW2B:PW2B + 1], col[:, BETA1:BETA1 + 1], ALU.mult))
            prep(nc.vector.scalar_tensor_tensor(out=col[:, OUTB:OUTB + 1], in0=col[:, PW4B:PW4B + 1],
                                                scalar=col[:, BETA2:BETA2 + 1], in1=colsum[:, 1:2],
                                                op0=ALU.mult, op1=ALU.add))
            dve.sem_inc(consts_ready, 1)

            def step(g, u, k, live):
                if live[2]:
                    h, par = g - 2, k % 2
                    dve.wait_ge(s1_hi_ready, h + 1)
                    nc.vector.tensor_tensor(s1_lo[:, par, :, :].rearrange("p m u -> p (m u)"), bank[0][:, :],
                                            s1_hi[:, par, :, :].rearrange("p m u -> p (m u)"),
                                            ALU.subtract).then_inc(s1_out, 1)
                if live[3]:
                    h, par = g - 3, (k - 3) % 2
                    for c in range(2):
                        dve.wait_ge(z_scaled, h * 2 + 1 + c)
                        zc = z[:, par, c, :, :].rearrange("p m u -> p (m u)")
                        nc.vector.tensor_tensor(zc, zc, bank[1 + c][:, :], ALU.max).then_inc(z_ready, 1)
                if live[4]:
                    h, par = g - 4, k % 2
                    dve.wait_ge(s3_hi_ready, h + 1)
                    nc.vector.tensor_tensor(s3_lo[:, par, :, :].rearrange("p r n -> p (r n)"), bank[3][:, :],
                                            s3_hi[:, par, :, :].rearrange("p r n -> p (r n)"),
                                            ALU.subtract).then_inc(s3_out, 1)
                if live[5]:
                    h, kk = g - 5, (k - 5) % 4
                    slot, pos = kk // 2, 2 * (kk % 2)
                    dve.wait_ge(s4_done, h + 1)
                    if kk % 2 == 0 and not (isinstance(h, int) and h < 4):
                        dve.wait_ge(y_stored[slot], (h - kk) * 4)
                    nc.vector.tensor_copy(y[:, slot, pos:pos + 2, :].rearrange("p m w -> p (m w)"),
                                          bank[4][:, 0:2 * W]).then_inc(y_ready, 1)

            def general():
                made2 = [0]

                def link(ins):
                    made2[0] += 1
                    ins.then_inc(g_chain, 1)
                    dve.wait_ge(g_chain, made2[0])

                link(nc.vector.memset(filt_pad[:, :, :, :], 0.0))
                for f in range(2):
                    link(nc.vector.tensor_copy(filt_pad[:, f, 1:TAPS + 1, 1:TAPS + 1], filt[:, f, :, :]))
                    link(nc.vector.tensor_tensor(pairs1[:, f, :, :], filt_pad[:, f, 0:PAIRS, :],
                                                 filt_pad[:, f, 1:PAIRS + 1, :], ALU.add))
                    link(nc.vector.tensor_tensor(pairs2[:, f, :, :], pairs1[:, f, :, 0:PAIRS],
                                                 pairs1[:, f, :, 1:PAIRS + 1], ALU.add))
                link(nc.vector.tensor_scalar(pairs2[:, 1, :, :], pairs2[:, 1, :, :], 0.25 * GAIN, None, ALU.mult))
                for f in range(2):
                    for s in range(PAIRS):
                        for t in range(PAIRS):
                            ins = nc.vector.tensor_scalar(masked2[:, t, :], tap_of[:, f * UP:(f + 1) * UP],
                                                          float(t), pairs2[:, f, t, s:s + 1],
                                                          ALU.is_equal, ALU.mult)
                        link(ins)
                        link(nc.vector.tensor_reduce(band2[:, s, f * UP:(f + 1) * UP],
                                                     masked2[:, :, :].rearrange("p t o -> p o t"), AX.X, ALU.add))
                dve.sem_inc(g_bands, 1)

                def unit(u, slot, now, before):
                    if now:
                        for n in range(4):
                            q, h = n // 2, n % 2
                            dve.wait_ge(g_scaled, u * 4 + n + 1)
                            zz = z_pad[:, slot, q, h, :, 3:3 + W]
                            nc.vector.tensor_tensor(zz, zz, bank[n][:, :].rearrange("p (m w) -> p m w", w=W),
                                                    ALU.max).then_inc(g_z_ready, 1)
                    if before:
                        dve.wait_ge(g_down_done, u)
                        if not (isinstance(u, int) and u < 3):
                            dve.wait_ge(g_stored[1 - slot], (u + slot) * 8 - 16)
                        nc.vector.tensor_copy(y2[:, 1 - slot, :, :].rearrange("p m w -> p (m w)"),
                                              bank[4][:, :]).then_inc(g_y_ready, 1)
                each_unit(dve, unit, True)

            by_rank(dve, lambda: each_step(dve, step, 6), general)

            CHAIN = 9

            def halves_stats(n, stats):
                dve.sem_inc(stats_made, 1)
                nc.vector.bn_aggr(mv[:, :], stats[:, :, :].rearrange("p a b -> p (a b)")).then_inc(mv_ready, 1)

            def norm_coefs(n, w, b_, ab, ready):
                count = [0]

                def link(ins):
                    count[0] += 1
                    ins.then_inc(ln_chain, 1)
                    dve.wait_ge(ln_chain, n * CHAIN + count[0])

                dve.wait_ge(mv_ready, n + 1)
                dve.wait_ge(mv_swapped, n + 1)
                link(nc.vector.tensor_tensor(lnt[:, 0:2], mv[:, :], bank[7][:, 0:2], ALU.add))
                link(nc.vector.tensor_tensor(lnt[:, 2:3], mv[:, 0:1], bank[7][:, 0:1], ALU.subtract))
                link(nc.vector.tensor_scalar(lnt[:, 2:3], lnt[:, 2:3], lnt[:, 2:3], 0.25, ALU.mult, ALU.mult))
                link(nc.vector.tensor_scalar(lnt[:, 1:2], lnt[:, 1:2], 0.5, LN_EPS, ALU.mult, ALU.add))
                nc.vector.tensor_tensor(lnt[:, 3:4], lnt[:, 1:2], lnt[:, 2:3], ALU.add).then_inc(var_ready, 1)
                dve.wait_ge(std_ready, n + 1)
                link(nc.vector.reciprocal(lnt[:, 5:6], lnt[:, 4:5]))
                link(nc.vector.tensor_tensor(ab[:, 0:1], lnt[:, 5:6], col[:, w:w + 1], ALU.mult))
                link(nc.vector.tensor_scalar(lnt[:, 6:7], lnt[:, 0:1], -0.5, None, ALU.mult))
                link(nc.vector.tensor_tensor(lnt[:, 6:7], lnt[:, 6:7], ab[:, 0:1], ALU.mult))
                link(nc.vector.tensor_tensor(ab[:, 1:2], lnt[:, 6:7], col[:, b_:b_ + 1], ALU.add))
                dve.sem_inc(ready, 1)

            def bn1(b, j):
                slot = j // 2 % 2
                if j % 2 == 0:
                    dve.wait_ge(stage_landed[slot], b * (8 * TAIL) + (j // 4 + 1) * 32)
                nc.vector.bn_stats(stats1[:, j, :], stage[:, slot, j % 2 * N:(j % 2 + 1) * N]
                                   ).then_inc(bn1_done, 1)

            def split_chunk(b, c):
                slot, q = c % 2, b * CHUNKS + c
                lo, hi = (1 if c == 0 else 0), CHUNK_ROWS + (1 if c == CHUNKS - 1 else 2)
                if not (isinstance(b, int) and b == 0 and c < 2):
                    dve.wait_ge(conv_done, (q - 1) * BLOCKS)
                if c == 0:
                    nc.vector.memset(split[:, slot, 0, :].bitcast(F32), 0.0)
                    nc.vector.memset(paired[0:C, slot, 0, :].bitcast(F32), 0.0)
                if c == CHUNKS - 1:
                    nc.vector.memset(split[:, slot, CHUNK_ROWS + 1, :].bitcast(F32), 0.0)
                    nc.vector.memset(paired[0:C, slot, CHUNK_ROWS + 1, :].bitcast(F32), 0.0)
                    nc.vector.memset(paired[C:P, slot, CHUNK_ROWS, :].bitcast(F32), 0.0)
                dve.wait_ge(chunk_normed, q + 1)
                nc.vector.tensor_copy(split[:, slot, lo:hi, 1:W + 1], rawc[:, slot, lo:hi, :]).then_inc(split_hi, 1)
                nc.vector.tensor_copy(paired[C:P, slot, 0:hi - 1, 1:W + 1],
                                      rawc[C:P, slot, 1:hi, :]).then_inc(pair_bottom, 1)

            def gate_block(b, i, tail):
                n = b * SLOTS + i
                half, at = i // TAIL, i % TAIL
                dve.wait_ge(tgate_ready, n + 1)
                if tail and half == 0:
                    dve.wait_ge(gate_parts, (b - 1) * TAIL + at + 1)
                lanes = slice(64 * half, 64 * half + 64)
                nc.vector.scalar_tensor_tensor(
                    out=gate[lanes, at * N:(at + 1) * N], in0=bank[i % 3][0:C, :], scalar=col_o[0:C, 2:3],
                    in1=t_gate[:, i % 2, :], op0=ALU.add, op1=ALU.mult,
                    accum_out=gsum[lanes, at:at + 1]).then_inc(gate_done, 1)

            def pw2_pair(b, j0):
                for j in (j0, j0 + 1):
                    n = b * TAIL + j
                    dve.wait_ge(pw2_done, n + 1)
                    if j % 4 == 0:
                        dve.wait_ge(res_landed[j // 4], b * 32 + 32)
                    xb = res[:, j * N:(j + 1) * N]
                    nc.vector.scalar_tensor_tensor(out=xb, in0=bank[3 + j % 2][:, :],
                                                   scalar=col[:, BETA1:BETA1 + 1], in1=xb,
                                                   op0=ALU.mult, op1=ALU.add).then_inc(x2_ready, 1)
                for j in (j0, j0 + 1):
                    dve.wait_ge(x2_ready, b * TAIL + j + 1)
                    nc.vector.bn_stats(stats2[:, j, :], res[:, j * N:(j + 1) * N]).then_inc(bn2_done, 1)

            def ffn_block(b, j):
                n = b * TAIL + j
                if j >= 2:
                    dve.wait_ge(pw4_done, n - 1)
                    o, slot = j - 2, (j - 2) // 2 % 2
                    if o % 2 == 0 and not (isinstance(b, int) and b == 0 and o < 4):
                        dve.wait_ge(out_stored[slot], b * (8 * TAIL) + o // 4 * 32)
                    nc.vector.scalar_tensor_tensor(out=t_out[:, slot, o % 2, :],
                                                   in0=bank[3 + j % 2][:, :],
                                                   scalar=col[:, BETA2:BETA2 + 1],
                                                   in1=res[:, o * N:(o + 1) * N],
                                                   op0=ALU.mult, op1=ALU.add).then_inc(sum_ready, 1)
                if j < TAIL:
                    dve.wait_ge(tgate2_ready, n + 1)
                    dve.wait_ge(u1_done, n + 1)
                    if not (isinstance(b, int) and b == 0 and j < 2):
                        dve.wait_ge(gate2_parts, n - 1)
                    nc.vector.scalar_tensor_tensor(out=gate2[:, j % 2, :], in0=bank[6][:, :],
                                                   scalar=bias3[:, 0:1], in1=t_gate2[:, j % 2, :],
                                                   op0=ALU.add, op1=ALU.mult).then_inc(gate2_ready, 1)

            for j in range(TAIL):
                bn1(0, j)
            dve.wait_ge(bn1_done, TAIL)
            halves_stats(0, stats1)
            norm_coefs(0, LN1W, LN1B, ln1ab, ln1_ready)
            dve.wait_ge(pads_zeroed, 2)
            split_chunk(0, 0)

            def batch(b, conv, tail, nxt):
                for i in range(SLOTS):
                    if conv and i % BLOCKS == 0 and i < SLOTS - BLOCKS:
                        split_chunk(b, i // BLOCKS + 1)
                    if nxt and i == SPLIT_AT:
                        split_chunk(b + 1, 0)
                    if tail and i == 0:
                        dve.wait_ge(attn_ready, b)
                        nc.vector.tensor_scalar(wbd2_b[:, :], wbd2[:, :], attn[:, :], None,
                                                ALU.mult).then_inc(w2_ready, 1)
                        dve.wait_ge(w2_ready, 3 * b - 2)
                        nc.vector.tensor_copy(w2_part[:, 0, :], wbd2_b[:, :]).then_inc(w2_ready, 1)
                        dve.wait_ge(w2_ready, 3 * b - 1)
                        nc.vector.tensor_tensor(w2_part[:, 1, :], wbd2_b[:, :], w2_part[:, 0, :],
                                                ALU.subtract).then_inc(w2_ready, 1)
                    if conv:
                        gate_block(b, i, tail)
                    if nxt and BN1_AT <= i < BN1_AT + TAIL:
                        bn1(b + 1, i - BN1_AT)
                    if tail and PW2_AT <= i < LN2_AT:
                        pw2_pair(b - 1, 2 * (i - PW2_AT))
                    if tail and i == LN2_AT:
                        dve.wait_ge(bn2_done, b * TAIL)
                        halves_stats(ln2_index(b), stats2)
                    if tail and i == LN2_AT + 1:
                        norm_coefs(ln2_index(b), LN2W, LN2B, ln2ab, ln2_ready)
                    if tail and i == LN2_AT + 2:
                        for o in range(2):
                            nc.vector.tensor_scalar(wbd3_b[:, o, :], wbd3[:, o, :], ln2ab[:, 0:1], None, ALU.mult)
                        dve.wait_ge(b3_done, b)
                        nc.vector.tensor_tensor(bias3[:, :], bank[7][:, 8:10], col[:, PW3B1:PW3B2 + 1],
                                                ALU.add).then_inc(w3_ready, 1)
                        dve.wait_ge(w3_ready, 3 * b - 2)
                        nc.vector.tensor_copy(w3_part[:, 0, :, :], wbd3_b[:, :, :]).then_inc(w3_ready, 1)
                        dve.wait_ge(w3_ready, 3 * b - 1)
                        nc.vector.tensor_tensor(w3_part[:, 1, :, :], wbd3_b[:, :, :], w3_part[:, 0, :, :],
                                                ALU.subtract).then_inc(w3_ready, 1)
                    if tail and FFN_AT <= i < FFN_AT + TAIL + 2:
                        ffn_block(b - 1, i - FFN_AT)
                    if nxt and i == LN1_AT:
                        dve.wait_ge(bn1_done, (b + 2) * TAIL)
                        halves_stats(b * 2 + 1, stats1)
                    if nxt and i == LN1_AT + 1:
                        norm_coefs(b * 2 + 1, LN1W, LN1B, ln1ab, ln1_ready)
                if conv:
                    dve.wait_ge(gate_done, (b + 1) * SLOTS)
                    nc.vector.tensor_reduce(gtot[:, :], gsum[:, :], AX.X, ALU.add).then_inc(gtot_ready, 1)

            each_batch(dve, batch)


NAMES = ["x", "L0_conv_bias", "L0_conv_up_filter", "L0_conv_dn_filter", "L1_conv_ln1_w", "L1_conv_ln1_b",
         "L1_conv_pw1_w", "L1_conv_pw1_b", "L1_conv_dw_w", "L1_conv_dw_b", "L1_conv_sca_w", "L1_conv_sca_b",
         "L1_conv_pw2_w", "L1_conv_pw2_b", "L1_conv_ln2_w", "L1_conv_ln2_b", "L1_conv_pw3_w",
         "L1_conv_pw3_b", "L1_conv_pw4_w", "L1_conv_pw4_b", "L1_conv_beta1", "L1_conv_beta2"]


def kernel(**inputs):
    import numpy as np
    import concourse.bacc as bacc
    from concourse.bass_utils import run_bass_kernel_spmd

    nc = bacc.Bacc("TRN2", target_bir_lowering=False, num_devices=1)
    arrays, args = {}, []
    for name in NAMES:
        a = np.ascontiguousarray(inputs[name])
        arrays[f"in_{name}"] = a
        args.append(nc.dram_tensor(f"in_{name}", a.shape, mybir.dt.from_np(a.dtype), kind="ExternalInput").ap())
    shape = inputs["x"].shape
    args.append(nc.dram_tensor("out_y", shape, F32, kind="ExternalOutput").ap())
    build(nc, *args)
    results = run_bass_kernel_spmd(nc, [arrays], core_ids=[0])
    return results.results[0]["out_y"]
```

```python
from contextlib import ExitStack

import concourse.bass as bass
from concourse import mybir

F32 = mybir.dt.float32
F32R = mybir.dt.float32r
BF16 = mybir.dt.bfloat16
I32 = mybir.dt.int32
ALU = mybir.AluOpType
ACT = mybir.ActivationFunctionType
AX = mybir.AxisListType

P = 128
UP = 2 * P
TAPS = 12
PAD_LO = (TAPS - 1) // 2
PAIRS = TAPS + 1
CENTRE = TAPS // 2 - 1
SLOPE = 0.2
GAIN = float(2.0 ** 0.5)
RANK1_TOL = 2.0 ** -21
LN_EPS = 1e-6


def build(nc, x, bias, up_filter, dn_filter, ln1_w, ln1_b, pw1_w, pw1_b, dw_w, dw_b, sca_w, sca_b,
          pw2_w, pw2_b, ln2_w, ln2_b, pw3_w, pw3_b, pw4_w, pw4_b, beta1, beta2, out):
    B, C, H, W = x.shape
    assert (C, H, W) == (64, P, P) and tuple(up_filter.shape) == (TAPS, TAPS)
    IMGS = B * C
    STEPS = IMGS // 2
    HW = H * W
    HALF = HW // 2
    CHUNK_ROWS = 16
    CHUNKS = H // CHUNK_ROWS
    BLOCK_ROWS = 4
    BLOCKS = CHUNK_ROWS // BLOCK_ROWS
    N = BLOCK_ROWS * W
    TAIL = HALF // N

    l0_out = nc.dram_tensor("l0_out", [IMGS, H, W], F32, kind="Internal").ap()
    x_rows = x.rearrange("b c h w -> h (b c) w")
    l0_rows = l0_out.rearrange("n h w -> h n w")
    l0_half = l0_out.rearrange("n (s r) w -> s n (r w)", s=2)
    out_half = out.rearrange("b c (s r) w -> s (b c) (r w)", s=2)

    with ExitStack() as ctx:
        def sb(name, shape, dt=F32):
            return ctx.enter_context(nc.sbuf_tensor(name, shape, dt))

        def sem(name):
            return ctx.enter_context(nc.semaphore(name))

        bank = [ctx.enter_context(nc.psum_tensor(f"bank{i}", [P, 512], F32)) for i in range(8)]

        stage = sb("stage", [P, 2, 2 * N])
        stage_home = stage[:, :, :].rearrange("p s n -> p (s n)")
        taken = [0]

        def prep_only(pattern, **dims):
            n = 1
            for d in dims.values():
                n *= d
            taken[0] += n
            assert taken[0] <= stage_home.shape[-1]
            return stage_home[:, taken[0] - n:taken[0]].rearrange(pattern, **dims)

        filt = prep_only("p (f a b) -> p f a b", f=2, a=TAPS, b=TAPS)
        ratio = prep_only("p (f a b) -> p f a b", f=2, a=TAPS, b=TAPS)
        resid = prep_only("p (f a b) -> p f a b", f=2, a=TAPS, b=TAPS)
        recip = sb("recip", [P, 2])
        factor = sb("factor", [P, 4, TAPS + 2])
        pairs = sb("pairs", [P, 4, PAIRS])
        fits = sb("fits", [P, 4])
        is_rank1 = sb("is_rank1", [P, 1], I32)
        BAND = 2 * UP
        tap_of = sb("tap_of", [P, BAND], I32)

        res = sb("res", [P, HALF])
        gate = sb("gate", [P, HALF])
        split = sb("split", [P, 2, CHUNK_ROWS + 2, W + 2], F32R)
        paired = sb("paired", [P, 2, CHUNK_ROWS + 2, W + 2], F32R)
        masked = gate[:, 0:PAIRS * BAND].rearrange("p (t o) -> p t o", t=PAIRS)

        t_out = sb("t_out", [P, 2, 2, N])
        part = sb("part", [P, 4, 2, N], F32R)

        tapped = gate[:, PAIRS * BAND:PAIRS * BAND + 9 * P].rearrange("p (t o) -> p t o", t=9)
        col_pair = sb("col_pair", [P, 2, CHUNK_ROWS, W], F32R)

        band = t_out[:, :, :, :].rearrange("p a b n -> p (a b n)")[:, 0:2 * BAND].rearrange(
            "p (a o) -> p a o", a=2)
        band_hi, band_lo = (part[:, s, :, :].rearrange("p h n -> p (h n)").rearrange("p (a o) -> p a o", a=2)
                            for s in range(2))
        used = {}

        def work(home, pattern, **dims):
            n = 1
            for d in dims.values():
                n *= d
            at = used.get(id(home), 0)
            used[id(home)] = at + n
            assert at + n <= home.shape[-1]
            return home[:, at:at + n].rearrange(pattern, **dims)

        res_home = res[:, :]
        split_home = split[:, :, :, :].rearrange("p s r w -> p (s r w)")
        paired_home = paired[:, :, :, :].rearrange("p s r w -> p (s r w)")
        raw = work(res_home, "p (s m w) -> p s m w", s=2, m=4, w=W)
        biased = work(res_home, "p (s m w) -> p s m w", s=2, m=4, w=W)
        z = work(res_home, "p (s c m u) -> p s c m u", s=2, c=2, m=2, u=UP)
        y = work(res_home, "p (s m w) -> p s m w", s=2, m=4, w=W)
        x_hi, x_lo = (work(split_home, "p (s m w) -> p s m w", s=2, m=4, w=W) for _ in range(2))
        s1_hi, s1_lo = (work(split_home, "p (s m u) -> p s m u", s=2, m=2, u=UP) for _ in range(2))
        s3_hi, s3_lo = (work(paired_home, "p (s r n) -> p s r n", s=2, r=2, n=2 * W) for _ in range(2))

        filt_pad = sb("filt_pad", [P, 2, TAPS + 2, TAPS + 2])
        pairs2 = sb("pairs2", [P, 2, PAIRS, PAIRS])
        pairs1 = sb("pairs1", [P, 2, PAIRS, TAPS + 2])
        band2 = gate[:, 0:PAIRS * 2 * UP].rearrange("p (s o) -> p s o", s=PAIRS)
        used.clear()
        PADW = W + 6
        raw2 = work(res_home, "p (s m w) -> p s m w", s=2, m=4, w=W)
        x_pad = work(res_home, "p (s m w) -> p s m w", s=2, m=4, w=PADW)
        z_pad = work(res_home, "p (s q r m w) -> p s q r m w", s=2, q=2, r=2, m=4, w=PADW)
        y2 = work(res_home, "p (s m w) -> p s m w", s=2, m=4, w=W)

        rawc = sb("rawc", [P, 2, CHUNK_ROWS + 2, W])
        masked2 = rawc[:, :, :, :].rearrange("p s r w -> p (s r w)")[:, 0:PAIRS * UP].rearrange(
            "p (t o) -> p t o", t=PAIRS)
        bias_bc = rawc[:, :, :, :].rearrange("p s r w -> p (s r w)")[:, PAIRS * UP:PAIRS * UP + IMGS].rearrange(
            "p (b c) -> p b c", b=B)
        w_hi = sb("w_hi", [P, 9, P], F32R)
        w_lo_pair = sb("w_lo_pair", [P, 3, P], F32R)
        w_lo_col = sb("w_lo_col", [P, P], F32R)
        w_lo_last = sb("w_lo_last", [P, P], F32R)
        t_gate = sb("t_gate", [C, 2, N])
        t_gate2 = sb("t_gate2", [P, 2, N])
        gate2 = sb("gate2", [P, 2, N])
        ident = prep_only("p (a b) -> p (a b)", a=1, b=P)
        swap = sb("swap", [P, P])
        diag_of = sb("diag_of", [P, P], I32)
        part_of = sb("part_of", [P, P], I32)
        w_nat = prep_only("p (n a c) -> p n a c", n=5, a=2, c=C)
        dwc = sb("dwc", [P, 9])
        colsum = sb("colsum", [P, 8])
        corr_o = prep_only("p (a b) -> p (a b)", a=1, b=P)
        corr = sb("corr", [P, P])
        corr_part = sb("corr_part", [P, P], BF16)
        edge_cols = sb("edge_cols", [P, BLOCK_ROWS, 2], BF16)
        edge_top = sb("edge_top", [P, W], BF16)
        edge_bottom = sb("edge_bottom", [P, W], BF16)
        wbd2 = sb("wbd2", [P, P])
        wbd2_b = sb("wbd2_b", [P, P])
        wbd3 = sb("wbd3", [P, 2, P])
        wbd3_b = sb("wbd3_b", [P, 2, P])
        wbd4 = sb("wbd4", [P, P])
        wsca = sb("wsca", [P, P])
        w2_part = sb("w2_part", [P, 2, P], F32R)
        w3_part = sb("w3_part", [P, 2, 2, P], F32R)
        w4_part = sb("w4_part", [P, 2, P], F32R)
        col = sb("col", [P, 16])
        LN1W, LN1B, SCAB, PW2B, LN2W, LN2B, PW3B1, PW3B2, PW4B, BETA1, BETA2, OUTB = range(12)
        col_o = sb("col_o", [P, 4])
        stats1 = sb("stats1", [P, TAIL, 6])
        stats2 = sb("stats2", [P, TAIL, 6])
        mv = sb("mv", [P, 2])
        lnt = sb("lnt", [P, 8])
        ln1ab = sb("ln1ab", [P, 2])
        ln2ab = sb("ln2ab", [P, 2])
        bias3 = sb("bias3", [P, 2])
        gsum = sb("gsum", [P, CHUNKS * BLOCKS // 2])
        gtot = sb("gtot", [P, 1])
        attn = sb("attn", [P, 1])

        filt_landed = sem("filt_landed")
        const_landed = sem("const_landed")
        vector_landed = sem("vector_landed")
        tap_index = sem("tap_index")
        dve_prep = sem("dve_prep")
        pool_prep = sem("pool_prep")
        taps_ready = sem("taps_ready")
        corr_ready = sem("corr_ready")
        consts_ready = sem("consts_ready")
        bias_spread = sem("bias_spread")
        bands_ready = sem("bands_ready")
        x_landed = [sem(f"x_landed{i}") for i in range(2)]
        x_biased = sem("x_biased")
        x_hi_ready = sem("x_hi_ready")
        x_split = sem("x_split")
        s1_done = sem("s1_done")
        s1_hi_ready = sem("s1_hi_ready")
        s1_out = sem("s1_out")
        s2_done = sem("s2_done")
        z_scaled = sem("z_scaled")
        z_ready = sem("z_ready")
        s3_done = sem("s3_done")
        s3_hi_ready = sem("s3_hi_ready")
        s3_out = sem("s3_out")
        s4_done = sem("s4_done")
        y_ready = sem("y_ready")
        y_stored = [sem(f"y_stored{i}") for i in range(2)]
        rank_known = sem("rank_known")
        g_bands = sem("g_bands")
        g_chain = sem("g_chain")
        g_landed = [sem(f"g_landed{i}") for i in range(2)]
        g_zeroed = sem("g_zeroed")
        g_biased = sem("g_biased")
        g_up_done = sem("g_up_done")
        g_scaled = sem("g_scaled")
        g_z_ready = sem("g_z_ready")
        g_down_done = sem("g_down_done")
        g_y_ready = sem("g_y_ready")
        g_stored = [sem(f"g_stored{i}") for i in range(2)]
        pe_prep = sem("pe_prep")
        res_landed = [sem(f"res_landed{i}") for i in range(4)]
        stage_landed = [sem(f"stage_landed{i}") for i in range(2)]
        pads_zeroed = sem("pads_zeroed")
        pair_top = sem("pair_top")
        pair_bottom = sem("pair_bottom")
        col_lower = sem("col_lower")
        col_upper = sem("col_upper")
        first_landed = sem("first_landed")
        chunk_landed = [sem(f"chunk_landed{i}") for i in range(2)]
        chunk_normed = sem("chunk_normed")
        split_hi = sem("split_hi")
        split_done = sem("split_done")
        conv_done = sem("conv_done")
        tgate_ready = sem("tgate_ready")
        gate_done = sem("gate_done")
        bn1_done = sem("bn1_done")
        ln_chain = sem("ln_chain")
        stats_made = sem("stats_made")
        sp_waited = sem("sp_waited")
        mv_ready = sem("mv_ready")
        mv_swapped = sem("mv_swapped")
        var_ready = sem("var_ready")
        std_ready = sem("std_ready")
        ln1_ready = sem("ln1_ready")
        ln2_ready = sem("ln2_ready")
        gtot_ready = sem("gtot_ready")
        sca_done = sem("sca_done")
        attn_ready = sem("attn_ready")
        w2_ready = sem("w2_ready")
        gate_hi_ready = sem("gate_hi_ready")
        gate_parts = sem("gate_parts")
        x2_hi_ready = sem("x2_hi_ready")
        x2_parts = sem("x2_parts")
        gate2_hi_ready = sem("gate2_hi_ready")
        gate2_parts = sem("gate2_parts")
        pw2_done = sem("pw2_done")
        x2_ready = sem("x2_ready")
        bn2_done = sem("bn2_done")
        b3_done = sem("b3_done")
        w3_ready = sem("w3_ready")
        u2_done = sem("u2_done")
        u1_done = sem("u1_done")
        tgate2_ready = sem("tgate2_ready")
        gate2_ready = sem("gate2_ready")
        pw4_done = sem("pw4_done")
        sum_ready = sem("sum_ready")
        outb_ready = sem("outb_ready")
        out_stored = [sem(f"out_stored{i}") for i in range(2)]

        block = ctx.enter_context(nc.Block())

        def tap_bank(t):
            return bank[5 + t // 4][:, t % 4 * P:t % 4 * P + P]

        def each_step(eng, step, lags):
            def live(g):
                return [0 <= g - lag < STEPS for lag in range(lags)]
            for g in range(8):
                step(g, g // 2, g % 4, live(g))
            with eng.Fori(2, STEPS // 4) as i:
                for k in range(4):
                    step(i * 4 + k, i * 2 + k // 2, k, [True] * lags)
            for g in range(STEPS, STEPS + lags - 1):
                step(g, g // 2, g % 4, live(g))

        UNITS = IMGS // 4

        def each_unit(eng, unit, lag):
            for u in range(4):
                unit(u, u % 2, True, u >= 1)
            with eng.Fori(2, UNITS // 2) as i:
                for k in range(2):
                    unit(i * 2 + k, k, True, True)
            if lag:
                unit(UNITS, 0, False, True)

        def by_rank(eng, separable, general):
            eng.wait_ge(rank_known, 1)
            flag = eng.value_load(is_rank1[0:1, 0:1], min_val=0, max_val=1)
            with eng.If(flag > 0):
                separable()
            with eng.Else():
                general()

        def each_batch(eng, batch):
            batch(0, True, False, B > 1)
            if B > 2:
                batch(1, True, True, True)
            if B > 3:
                with eng.Fori(0, B - 3) as i:
                    batch(i + 2, True, True, True)
            if B > 1:
                batch(B - 1, True, True, False)
            batch(B, False, True, False)

        SLOTS = CHUNKS * BLOCKS
        PW2_AT = 2
        LN2_AT = PW2_AT + TAIL // 2
        FFN_AT = LN2_AT + 3
        BN1_AT = LN2_AT - 1
        LN1_AT = BN1_AT + TAIL
        SPLIT_AT = SLOTS - BLOCKS
        PIECES = ((0, 6), (6, 12), (12, CHUNK_ROWS + 2))
        PIECE_AT = ((0,), (1,), (2,), ())

        def ln2_index(b):
            return 2 * b if not (isinstance(b, int) and b == B) else 2 * B - 1

        @block.sync
        def _(sp):
            for f, src in enumerate((up_filter, dn_filter)):
                sp.dma_start(filt[:, f, :, :].rearrange("p a b -> p (a b)"),
                             src.rearrange("a b -> (a b)").partition_broadcast(P)).then_inc(filt_landed, 16)
            sp.dma_start(bias_bc[:, 0, :],
                         bias.rearrange("a c h w -> (a c h w)").partition_broadcast(P)).then_inc(filt_landed, 16)

            def load(u, slot, wait):
                if wait:
                    sp.wait_ge(x_biased, u - 1)
                sp.dma_start(raw[:, slot, :, :], x_rows[:, bass.ds(u * 4, 4), :]).then_inc(x_landed[slot], 16)

            def store(u, slot):
                sp.wait_ge(y_ready, u * 2 + 2)
                sp.dma_start(l0_rows[:, bass.ds(u * 4, 4), :], y[:, slot, :, :]).then_inc(y_stored[slot], 16)

            def load_chunk(b, c, slot, wait=True):
                q = b * CHUNKS + c
                if wait:
                    sp.wait_ge(split_done, (q - 1) * len(PIECES))
                    sp.wait_ge(pair_top, q - 1)
                    sp.wait_ge(pair_bottom, q - 1)
                    sp.wait_ge(col_lower, q - 1)
                    sp.wait_ge(col_upper, q - 1)
                    sp.sem_inc(sp_waited, 1)
                lo = 1 if c == 0 else 0
                n = CHUNK_ROWS + 2 - lo - (1 if c == CHUNKS - 1 else 0)
                row = 0 if c == 0 else c * CHUNK_ROWS - 1
                for s in range(2):
                    sp.dma_start(rawc[64 * s:64 * s + 64, slot, lo:lo + n, :],
                                 l0_out[bass.ds(b * C, C), row:row + n, :]).then_inc(chunk_landed[slot], 16)

            def load_first(biased_count, early):
                if early:
                    for slot in range(2):
                        sp.wait_ge(y_stored[slot], 16 * (C // 8))
                for s in range(2):
                    sp.dma_start(gate[64 * s:64 * s + 64, :], l0_half[s, 0:C, :]).then_inc(first_landed, 16)
                load_chunk(0, 0, 0, False)
                sp.wait_ge(biased_count, UNITS)
                load_chunk(0, 1, 1, False)

            def separable():
                AHEAD = 4
                for u in range(AHEAD + 2):
                    load(u, u % 2, u >= 2)
                    if u >= AHEAD:
                        store(u - AHEAD, u % 2)
                with sp.Fori(3, UNITS // 2) as i:
                    for k in range(2):
                        load(i * 2 + k, k, True)
                        store(i * 2 + k - AHEAD, k)
                load_first(x_biased, True)
                for u in range(UNITS - AHEAD, UNITS):
                    store(u, u % 2)
                for slot in range(2):
                    sp.wait_ge(y_stored[slot], 16 * (UNITS // 2))

            def general():
                def unit(u, slot, now, before):
                    if now:
                        if not (isinstance(u, int) and u < 2):
                            sp.wait_ge(g_biased, u - 1)
                        sp.dma_start(raw2[:, slot, :, :], x_rows[:, bass.ds(u * 4, 4), :]
                                     ).then_inc(g_landed[slot], 16)
                    if before:
                        sp.wait_ge(g_y_ready, u)
                        sp.dma_start(l0_rows[:, bass.ds(u * 4 - 4, 4), :], y2[:, 1 - slot, :, :]
                                     ).then_inc(g_stored[1 - slot], 16)
                each_unit(sp, unit, True)
                for slot in range(2):
                    sp.wait_ge(g_stored[slot], 16 * (UNITS // 2))
                load_first(g_biased, False)

            by_rank(sp, separable, general)

            def load_stage(b, q):
                slot = q % 2
                sp.wait_ge(bn1_done, b * TAIL + q * 2 - 2)
                sp.sem_inc(sp_waited, 1)
                for s in range(2):
                    sp.dma_start(stage[64 * s:64 * s + 64, slot, :],
                                 l0_half[s, bass.ds(b * C, C), q * 2 * N:(q + 1) * 2 * N]
                                 ).then_inc(stage_landed[slot], 16)

            def load_res(b, q):
                if not (isinstance(b, int) and b == 0):
                    sp.wait_ge(sum_ready, b * TAIL - TAIL + q * 4 + 4)
                    sp.sem_inc(sp_waited, 1)
                for s in range(2):
                    sp.dma_start(res[64 * s:64 * s + 64, q * 4 * N:(q + 1) * 4 * N],
                                 l0_half[s, bass.ds(b * C, C), q * 4 * N:(q + 1) * 4 * N]
                                 ).then_inc(res_landed[q], 16)

            def store_out(b, q):
                slot = q % 2
                sp.wait_ge(outb_ready, b * TAIL + q * 2 + 2)
                sp.sem_inc(sp_waited, 1)
                for s in range(2):
                    sp.dma_start(out_half[s, bass.ds(b * C, C), q * 2 * N:(q + 1) * 2 * N],
                                 t_out[64 * s:64 * s + 64, slot, :, :].rearrange("p a n -> p (a n)")
                                 ).then_inc(out_stored[slot], 16)

            def batch(b, conv, tail, nxt):
                def stages(*parts):
                    for q in parts if nxt else ():
                        load_stage(b + 1, q)

                def stores(*parts):
                    for q in parts if tail else ():
                        store_out(b - 1, q)

                def residuals(*parts):
                    for q in parts if conv else ():
                        load_res(b, q)

                for c in range(CHUNKS):
                    if conv and c + 2 < CHUNKS:
                        load_chunk(b, c + 2, c % 2)
                    elif nxt and c + 2 >= CHUNKS:
                        load_chunk(b + 1, c + 2 - CHUNKS, c % 2)
                    if c == 1:
                        stages(0, 1)
                    if c == 2:
                        stages(2)
                    if c == 3:
                        stages(3, 4)
                    if c == 4:
                        stages(5)
                        stores(0)
                        stages(6)
                    if c == 5:
                        stores(1)
                        stages(7)
                        stores(2)
                        residuals(0)
                    if c == 6:
                        stores(3, 4)
                        residuals(1)
                    if c == 7:
                        stores(5, 6)
                        residuals(2)
                stores(7)
                residuals(3)

            each_batch(sp, batch)
            for slot in range(2):
                sp.wait_ge(out_stored[slot], 32 * B * (TAIL // 4))

        @block.gpsimd
        def _(pool):
            for lo, n, base, step, per_row in ((0, UP, PAD_LO + 1, -1, 2), (UP, P, PAD_LO, -2, 1),
                                               (UP + P, P, P + PAD_LO, -2, 1)):
                pool.iota(tap_of[:, lo:lo + n], [[step, n]], base=base,
                          channel_multiplier=per_row).then_inc(tap_index, 1)
            pool.iota(diag_of[:, :], [[-1, P]], base=0, channel_multiplier=1).then_inc(tap_index, 1)
            for n, at in enumerate(range(0, P, 32)):
                pool.wait_ge(tap_index, 4 + n)
                pool.iota(part_of[at:at + 32, :], [[0, P]], base=0, channel_multiplier=1).then_inc(tap_index, 1)
            pool.wait_ge(tap_index, 8)
            pool.memset(col_pair[:, :, :, 0:1].bitcast(F32), 0.0).then_inc(tap_index, 1)
            pool.memset(corr_o[:, :], 0.0).then_inc(tap_index, 1)
            pool.memset(wbd2[:, :], 0.0).then_inc(tap_index, 1)
            pool.memset(wbd3[:, :, :], 0.0).then_inc(tap_index, 1)
            pool.memset(wbd4[:, :], 0.0).then_inc(tap_index, 1)
            made = [0]

            def prep(ins):
                made[0] += 1
                ins.then_inc(pool_prep, 1)
                pool.wait_ge(pool_prep, made[0])

            pool.wait_ge(tap_index, 13)
            prep(nc.gpsimd.tensor_scalar(ident[:, :], diag_of[:, :], 0.0, None, ALU.is_equal))
            prep(nc.gpsimd.tensor_scalar(swap[:, :], diag_of[:, :], float(C), None, ALU.is_equal))
            prep(nc.gpsimd.tensor_scalar(corr[:, :], diag_of[:, :], float(-C), None, ALU.is_equal))
            prep(nc.gpsimd.tensor_tensor(swap[:, :], swap[:, :], corr[:, :], ALU.add))
            pool.wait_ge(const_landed, 16 * 13)
            for t in range(9):
                prep(nc.gpsimd.tensor_scalar(tapped[:, t, :], w_nat[:, 0, :, :].rearrange("p a c -> p (a c)"),
                                             dwc[:, t:t + 1], None, ALU.mult))
            pool.sem_inc(taps_ready, 1)
            def sum_taps(taps):
                prep(nc.gpsimd.tensor_copy(colsum[:, 0:1], dwc[:, taps[0]:taps[0] + 1]))
                for t in taps[1:]:
                    prep(nc.gpsimd.tensor_tensor(colsum[:, 0:1], colsum[:, 0:1], dwc[:, t:t + 1], ALU.add))

            for n, taps in enumerate(((0, 1, 2), (6, 7, 8), (0, 3, 6), (2, 5, 8), (0,), (2,), (6,), (8,))):
                sum_taps(taps)
                prep(nc.gpsimd.tensor_tensor(corr_o[:, n:n + 1], colsum[:, 0:1], col_o[:, 1:2], ALU.mult))
            prep(nc.gpsimd.tensor_scalar(corr_o[:, 0:4], corr_o[:, 0:4], -1.0, None, ALU.mult))
            for at in (32, 64):
                prep(nc.gpsimd.tensor_copy(corr_o[:, at:at + 8], corr_o[:, 0:8]))
            sum_taps(range(9))
            prep(nc.gpsimd.tensor_tensor(col_o[:, 2:3], colsum[:, 0:1], col_o[:, 1:2], ALU.mult))
            prep(nc.gpsimd.tensor_tensor(col_o[:, 2:3], col_o[:, 2:3], col_o[:, 0:1], ALU.add))
            pool.sem_inc(corr_ready, 1)
            def where(dst, n):
                return nc.gpsimd.tensor_scalar(dst, part_of[:, 0:1] if dst.shape[-1] == 1 else part_of[:, :],
                                               float(n), None, ALU.is_equal)
            prep(where(edge_top[:, :], 0))
            prep(where(edge_bottom[:, :], 1))
            for dst, corners in ((edge_top, (4, 5)), (edge_bottom, (6, 7))):
                for at, n in zip((0, W - 1), corners):
                    prep(where(colsum[:, 0:1], n))
                    prep(nc.gpsimd.tensor_tensor(dst[:, at:at + 1], dst[:, at:at + 1], colsum[:, 0:1], ALU.add))
            for r in range(BLOCK_ROWS):
                for s in range(2):
                    prep(where(edge_cols[:, r, s:s + 1], 2 + s))
            pool.wait_ge(filt_landed, 48)
            for b in range(1, B):
                pool.tensor_copy(bias_bc[:, b, :], bias_bc[:, 0, :]).then_inc(bias_spread, 1)
            if B > 1:
                pool.wait_ge(bias_spread, B - 1)
            bias_flat = bias_bc[:, :, :].rearrange("p b c -> p (b c)")

            def separable():
                def unit(u, slot, now, before):
                    pool.wait_ge(x_landed[slot], (u - slot) * 8 + 16)
                    pool.tensor_tensor(biased[:, slot, :, :], raw[:, slot, :, :],
                                       bias_flat[:, bass.ds(u * 4, 4)].unsqueeze(2).to_broadcast([P, 4, W]),
                                       ALU.add).then_inc(x_biased, 1)
                    pool.wait_ge(x_hi_ready, u + 1)
                    pool.tensor_tensor(x_lo[:, slot, :, :], biased[:, slot, :, :], x_hi[:, slot, :, :],
                                       ALU.subtract).then_inc(x_split, 1)
                each_unit(pool, unit, False)
                pool.wait_ge(s4_done, STEPS)

            def general():
                pool.memset(x_pad[:, :, :, :], 0.0).then_inc(g_zeroed, 1)
                pool.memset(z_pad[:, :, :, :, :, :], 0.0).then_inc(g_zeroed, 1)
                pool.wait_ge(g_zeroed, 2)

                def unit(u, slot, now, before):
                    pool.wait_ge(g_landed[slot], (u - slot) * 8 + 16)
                    if not (isinstance(u, int) and u < 2):
                        pool.wait_ge(g_up_done, u * 4 - 4)
                    pool.tensor_tensor(x_pad[:, slot, :, 3:3 + W], raw2[:, slot, :, :],
                                       bias_flat[:, bass.ds(u * 4, 4)].unsqueeze(2).to_broadcast([P, 4, W]),
                                       ALU.add).then_inc(g_biased, 1)
                each_unit(pool, unit, False)

            by_rank(pool, separable, general)
            pool.memset(split[:, :, :, 0:W + 2:W + 1].bitcast(F32), 0.0).then_inc(pads_zeroed, 1)
            pool.memset(paired[:, :, :, 0:W + 2:W + 1].bitcast(F32), 0.0).then_inc(pads_zeroed, 1)
            pool.wait_ge(pads_zeroed, 2)
            pool.memset(paired[C:P, :, CHUNK_ROWS + 1, :].bitcast(F32), 0.0).then_inc(pads_zeroed, 1)
            pool.wait_ge(pads_zeroed, 3)

            def split_lo(b, c, piece):
                slot, q = c % 2, b * CHUNKS + c
                lo, hi = PIECES[piece]
                if c == 0:
                    lo = max(lo, 1)
                if c == CHUNKS - 1:
                    hi = min(hi, CHUNK_ROWS + 1)
                if piece == 0:
                    pool.wait_ge(split_hi, q + 1)
                pool.tensor_tensor(split[C:P, slot, lo:hi, 1:W + 1], rawc[C:P, slot, lo:hi, :],
                                   split[C:P, slot, lo:hi, 1:W + 1], ALU.subtract).then_inc(split_done, 1)
                pool.wait_ge(split_done, q * len(PIECES) + piece + 1)

            def tail_lo(source, hi_ready, n, slot, done):
                pool.wait_ge(hi_ready, n + 1)
                pool.tensor_tensor(part[:, slot, 1, :], source, part[:, slot, 0, :],
                                   ALU.subtract).then_inc(done, 1)
                pool.wait_ge(done, n + 1)

            for piece in range(len(PIECES)):
                split_lo(0, 0, piece)

            def batch(b, conv, tail, nxt):
                for i in range(SLOTS):
                    k = i - PW2_AT
                    if tail and k < TAIL // 2 - 2:
                        for j in (2 * k + 4, 2 * k + 5):
                            tail_lo(gate[:, j * N:(j + 1) * N], gate_hi_ready, (b - 1) * TAIL + j, j % 4,
                                    gate_parts)
                    j = i - FFN_AT
                    if tail and 0 <= j + 1 < TAIL:
                        tail_lo(res[:, (j + 1) * N:(j + 2) * N], x2_hi_ready, (b - 1) * TAIL + j + 1,
                                (j + 1) % 2, x2_parts)
                    following = (b, i // BLOCKS + 1) if i < SPLIT_AT else (b + 1, 0)
                    if conv and i < SPLIT_AT or nxt and i >= SPLIT_AT:
                        for piece in PIECE_AT[i % BLOCKS]:
                            split_lo(*following, piece)
                    if tail and conv and 0 <= j - 1 < TAIL:
                        tail_lo(gate2[:, (j - 1) % 2, :], gate2_hi_ready, (b - 1) * TAIL + j - 1,
                                2 + (j - 1) % 2, gate2_parts)

            each_batch(pool, batch)

        @block.tensor
        def _(pe):
            def parts(t, a, lo, n):
                return t[:, a, lo:lo + n]

            def step(g, u, k, live):
                if live[2]:
                    h, kk = g - 2, (k - 2) % 4
                    slot, pos = kk // 2, 2 * (kk % 2)
                    if kk % 2 == 0:
                        pe.wait_ge(x_split, u)
                    if not (isinstance(h, int) and h < 1):
                        pe.wait_ge(s1_out, h)
                    for m in range(2):
                        for n, (xp, wp) in enumerate(((x_hi, band_lo), (x_hi, band_hi), (x_lo, band_hi))):
                            mm = nc.tensor.matmul(bank[0][:, m * UP:(m + 1) * UP], xp[:, slot, pos + m, :],
                                                  parts(wp, 0, 0, UP), start=(m == 0 and n == 0),
                                                  stop=(n == 2), skip_group_check=True)
                    mm.then_inc(s1_done, 1)
                if live[3]:
                    h, par = g - 3, (k - 3) % 2
                    pe.wait_ge(s1_out, h + 1)
                    for c in range(2):
                        if not (isinstance(h, int) and h < 1):
                            pe.wait_ge(z_ready, h * 2 - 1 + c)
                        for n, (wp, dp) in enumerate(((band_lo, s1_hi), (band_hi, s1_hi), (band_hi, s1_lo))):
                            mm = nc.tensor.matmul(bank[1 + c][:, :], parts(wp, 1, c * P, P),
                                                  dp[:, par, :, :].rearrange("p m u -> p (m u)"),
                                                  start=(n == 0), stop=(n == 2))
                        mm.then_inc(s2_done, 1)
                if live[4]:
                    h, par = g - 4, k % 2
                    pe.wait_ge(z_ready, h * 2 + 2)
                    if not (isinstance(h, int) and h < 1):
                        pe.wait_ge(s3_out, h)
                    acc = bank[3][:, :].rearrange("p (r m w) -> p r m w", r=2, m=2)
                    for n in range(8):
                        r, m, c = n // 4, n // 2 % 2, n % 2
                        mm = nc.tensor.matmul(acc[:, r, m, :], z[:, par, c, m, r * P:(r + 1) * P],
                                              parts(band, 1, UP + c * P, P),
                                              start=(n == 0), stop=(c == 1), skip_group_check=True)
                    mm.then_inc(s3_done, 1)
                if live[5]:
                    h, par = g - 5, (k - 5) % 2
                    pe.wait_ge(s3_out, h + 1)
                    if not (isinstance(h, int) and h < 1):
                        pe.wait_ge(y_ready, h)
                    for r in range(2):
                        for n, (wp, dp) in enumerate(((band_lo, s3_hi), (band_hi, s3_hi), (band_hi, s3_lo))):
                            mm = nc.tensor.matmul(bank[4][:, 0:2 * W], parts(wp, 0, UP + r * P, P),
                                                  dp[:, par, r, :], start=(r == 0 and n == 0),
                                                  stop=(r == 1 and n == 2))
                    mm.then_inc(s4_done, 1)

            pe.wait_ge(taps_ready, 1)
            for t in range(9):
                nc.tensor.matmul(tap_bank(t), tapped[:, t, :], ident[:, :],
                                 start=True, stop=True).then_inc(pe_prep, 1)
            pe.wait_ge(corr_ready, 1)
            nc.tensor.matmul(bank[7][:, P:2 * P], corr_o[:, :], ident[:, :], start=True, stop=True)
            nc.tensor.matmul(bank[7][:, 2 * P:3 * P], w_nat[:, 1, :, :].rearrange("p a c -> p (a c)"),
                             ident[:, :], start=True, stop=True)
            for n, dst in ((2, bank[7][:, 3 * P:3 * P + C]), (3, bank[7][:, 3 * P + C:4 * P]), (4, bank[4][:, 0:C])):
                mm = nc.tensor.matmul(dst, w_nat[0:C, n, :, :].rearrange("p a c -> p (a c)"),
                                      ident[0:C, 0:C], start=True, stop=True)
            mm.then_inc(pe_prep, 1)

            def separable():
                pe.wait_ge(bands_ready, 1)
                each_step(pe, step, 6)

            def general():
                pe.wait_ge(g_bands, 1)
                pe.wait_ge(g_zeroed, 2)

                def unit(u, slot, now, before):
                    if now:
                        pe.wait_ge(g_biased, u + 1)
                        for q in range(2):
                            for h in range(2):
                                acc = bank[2 * q + h]
                                if not (isinstance(u, int) and u < 1):
                                    pe.wait_ge(g_z_ready, u * 4 - 3 + 2 * q + h)
                                taps = range(q, PAIRS, 2)
                                for t in taps:
                                    at = 3 + (t + q - 6) // 2
                                    mm = nc.tensor.matmul(acc[:, :], band2[:, t, h * P:(h + 1) * P],
                                                          x_pad[:, slot, :, at:at + W],
                                                          start=(t == q), stop=(t == taps[-1]))
                                mm.then_inc(g_up_done, 1)
                    if before:
                        pe.wait_ge(g_z_ready, u * 4)
                        if not (isinstance(u, int) and u < 2):
                            pe.wait_ge(g_y_ready, u - 1)
                        n = 0
                        for t in range(PAIRS):
                            q = (t + 1) % 2
                            at = 3 + (t - 5 - q) // 2
                            for h in range(2):
                                mm = nc.tensor.matmul(bank[4][:, :], band2[:, t, UP + h * P:UP + (h + 1) * P],
                                                      z_pad[:, 1 - slot, q, h, :, at:at + W],
                                                      start=(n == 0), stop=(n == 2 * PAIRS - 1))
                                n += 1
                        mm.then_inc(g_down_done, 1)
                each_unit(pe, unit, True)

            by_rank(pe, separable, general)

            def conv_block(b, i):
                c, j = i // BLOCKS, i % BLOCKS
                slot, q, n = c % 2, b * CHUNKS + c, b * SLOTS + i
                if j == 0:
                    pe.wait_ge(split_done, (q + 1) * len(PIECES))
                    pe.wait_ge(pair_top, q + 1)
                    pe.wait_ge(pair_bottom, q + 1)
                    pe.wait_ge(col_lower, q + 1)
                    pe.wait_ge(col_upper, q + 1)
                if not (isinstance(b, int) and b == 0 and i < 3):
                    pe.wait_ge(gate_done, n - (1, 1, 4)[i] if i < 3 else n - 2)
                acc = bank[i % 3]

                def window(tile, t):
                    lo = BLOCK_ROWS * j + t // 3
                    return tile[:, slot, lo:lo + BLOCK_ROWS, t % 3:t % 3 + W]

                for t in range(3):
                    nc.tensor.matmul(acc[:, :], w_lo_pair[:, t, :], window(paired, t), start=(t == 0),
                                     stop=False, skip_group_check=True)
                nc.tensor.matmul(acc[:, :], w_lo_col[:, :], col_pair[:, slot, BLOCK_ROWS * j:BLOCK_ROWS * (j + 1), :],
                                 start=False, stop=False, skip_group_check=True)
                nc.tensor.matmul(acc[:, :], w_lo_last[:, :], window(paired, 8), start=False,
                                 stop=False, skip_group_check=True)
                nc.tensor.matmul(acc[:, :].rearrange("p (r w) -> p r w", w=W)[:, :, 0:W:W - 1],
                                 corr_part[:, :], edge_cols[:, :, :], start=False, stop=False,
                                 skip_group_check=True)
                if i == 0:
                    nc.tensor.matmul(acc[:, 0:W], corr_part[:, :], edge_top[:, :], start=False,
                                     stop=False, skip_group_check=True)
                if i == SLOTS - 1:
                    nc.tensor.matmul(acc[:, N - W:N], corr_part[:, :], edge_bottom[:, :],
                                     start=False, stop=False, skip_group_check=True)
                for t in range(9):
                    mm = nc.tensor.matmul(acc[:, :], w_hi[:, t, :], window(split, t), start=False,
                                          stop=(t == 8), skip_group_check=True)
                mm.then_inc(conv_done, 1)

            def swap_stats(n):
                pe.wait_ge(mv_ready, n + 1)
                nc.tensor.matmul(bank[7][:, 0:2], swap[:, :], mv[:, :], start=True,
                                 stop=True).then_inc(mv_swapped, 1)

            swap_stats(0)
            pe.wait_ge(consts_ready, 1)
            pe.wait_ge(pads_zeroed, 3)

            def three_terms(acc, w, data):
                nc.tensor.matmul(acc[:, :], w[:, 1, :], data[:, 0, :], start=True, stop=False)
                nc.tensor.matmul(acc[:, :], w[:, 0, :], data[:, 0, :], start=False, stop=False)
                return nc.tensor.matmul(acc[:, :], w[:, 0, :], data[:, 1, :], start=False, stop=True)

            def pw2_block(b, j):
                if j >= 2:
                    pe.wait_ge(x2_ready, b * TAIL + j - 1)
                elif not (isinstance(b, int) and b == 0):
                    pe.wait_ge(sum_ready, b * TAIL - 1 + j)
                pe.wait_ge(gate_parts, b * TAIL + j + 1)
                three_terms(bank[3 + j % 2], w2_part, part[:, j % 4, :, :]).then_inc(pw2_done, 1)

            def ffn_block(b, j):
                n = b * TAIL + j
                if j >= 2:
                    pe.wait_ge(gate2_parts, n - 1)
                    if j >= 4:
                        pe.wait_ge(sum_ready, n - 3)
                    three_terms(bank[3 + j % 2], w4_part, part[:, 2 + j % 2, :, :]).then_inc(pw4_done, 1)
                if j < TAIL:
                    pe.wait_ge(x2_parts, n + 1)
                    if not (isinstance(b, int) and b == 0 and j < 1):
                        pe.wait_ge(tgate2_ready, n)
                    three_terms(bank[5], w3_part[:, :, 1, :], part[:, j % 2, :, :]).then_inc(u2_done, 1)
                    if not (isinstance(b, int) and b == 0 and j < 1):
                        pe.wait_ge(gate2_ready, n)
                    three_terms(bank[6], w3_part[:, :, 0, :], part[:, j % 2, :, :]).then_inc(u1_done, 1)

            def batch(b, conv, tail, nxt):
                for i in range(SLOTS):
                    if tail and i == LN2_AT + 2:
                        swap_stats(ln2_index(b))
                    if tail and i == FFN_AT:
                        pe.wait_ge(ln2_ready, b)
                        for o in range(2):
                            mm = nc.tensor.matmul(bank[7][:, 8 + o:9 + o], wbd3[:, o, :], ln2ab[:, 1:2],
                                                  start=True, stop=True)
                        mm.then_inc(b3_done, 1)
                    if nxt and i == LN1_AT + 2:
                        swap_stats(b * 2 + 1)
                    if conv:
                        conv_block(b, i)
                    if tail and i == 0:
                        pe.wait_ge(gtot_ready, b)
                        nc.tensor.matmul(bank[7][:, 4:5], wsca[:, :], gtot[:, :], start=True,
                                         stop=True).then_inc(sca_done, 1)
                    if tail and PW2_AT <= i < LN2_AT:
                        if i == PW2_AT:
                            pe.wait_ge(w2_ready, 3 * b)
                        for j in range(2):
                            pw2_block(b - 1, 2 * (i - PW2_AT) + j)
                    if tail and FFN_AT <= i < FFN_AT + TAIL + 2:
                        if i == FFN_AT:
                            pe.wait_ge(w3_ready, 3 * b)
                        ffn_block(b - 1, i - FFN_AT)

            each_batch(pe, batch)

        @block.scalar
        def _(act):
            act.dma_start(col_o[:, 0:1], dw_b.rearrange("(c a) -> c a", a=1)).then_inc(const_landed, 16)
            act.dma_start(col_o[:, 1:2], pw1_b.rearrange("(c a) -> c a", a=1)).then_inc(const_landed, 16)
            act.dma_start(dwc[:, :], dw_w.rearrange("o a h w -> o (a h w)")).then_inc(const_landed, 16)
            for n, (src, rows) in enumerate(((pw1_w, P), (pw3_w, P), (pw2_w, C), (pw4_w, C), (sca_w, C))):
                for s in range(2):
                    act.dma_start(w_nat[0:rows, n, s, :], src[:, :]).then_inc(const_landed, 16)
            def col_load(n, src, lo=0):
                for s in range(2):
                    act.dma_start(col[64 * s:64 * s + 64, n:n + 1], src[lo:lo + C, :]).then_inc(vector_landed, 16)

            vec4 = "a c h w -> c (a h w)"
            col_load(LN1W, ln1_w.rearrange(vec4))
            col_load(LN1B, ln1_b.rearrange(vec4))
            col_load(SCAB, sca_b.rearrange("(c a) -> c a", a=1))
            col_load(PW2B, pw2_b.rearrange("(c a) -> c a", a=1))
            col_load(LN2W, ln2_w.rearrange(vec4))
            col_load(LN2B, ln2_b.rearrange(vec4))
            col_load(PW3B1, pw3_b.rearrange("(c a) -> c a", a=1))
            col_load(PW3B2, pw3_b.rearrange("(c a) -> c a", a=1), C)
            col_load(PW4B, pw4_b.rearrange("(c a) -> c a", a=1))
            col_load(BETA1, beta1.rearrange(vec4))
            col_load(BETA2, beta2.rearrange(vec4))

            def step(g, u, k, live):
                if live[0] and k % 2 == 0:
                    act.wait_ge(x_biased, u + 1)
                    if not (isinstance(u, int) and u < 2):
                        act.wait_ge(s1_done, u * 2 - 2)
                    nc.scalar.activation(x_hi[:, k // 2, :, :], biased[:, k // 2, :, :],
                                         ACT.Copy).then_inc(x_hi_ready, 1)
                if live[2]:
                    h, par = g - 2, k % 2
                    act.wait_ge(s1_done, h + 1)
                    if not (isinstance(h, int) and h < 2):
                        act.wait_ge(s2_done, h * 2 - 2)
                    nc.scalar.activation(s1_hi[:, par, :, :].rearrange("p m u -> p (m u)"), bank[0][:, :],
                                         ACT.Copy).then_inc(s1_hi_ready, 1)
                if live[3]:
                    h, par = g - 3, (k - 3) % 2
                    for c in range(2):
                        act.wait_ge(s2_done, h * 2 + 1 + c)
                        if c == 0 and not (isinstance(h, int) and h < 2):
                            act.wait_ge(s3_done, h - 1)
                        nc.scalar.activation(z[:, par, c, :, :].rearrange("p m u -> p (m u)"),
                                             bank[1 + c][:, :], ACT.Copy, scale=SLOPE).then_inc(z_scaled, 1)
                if live[4]:
                    h, par = g - 4, k % 2
                    act.wait_ge(s3_done, h + 1)
                    if not (isinstance(h, int) and h < 2):
                        act.wait_ge(s4_done, h - 1)
                    nc.scalar.activation(s3_hi[:, par, :, :].rearrange("p r n -> p (r n)"), bank[3][:, :],
                                         ACT.Copy).then_inc(s3_hi_ready, 1)

            def general():
                act.wait_ge(g_zeroed, 2)

                def unit(u, slot, now, before):
                    for n in range(4):
                        q, h = n // 2, n % 2
                        act.wait_ge(g_up_done, u * 4 + n + 1)
                        if n == 0 and not (isinstance(u, int) and u < 2):
                            act.wait_ge(g_down_done, u - 1)
                        nc.scalar.activation(z_pad[:, slot, q, h, :, 3:3 + W],
                                             bank[n][:, :].rearrange("p (m w) -> p m w", w=W),
                                             ACT.Copy, scale=SLOPE).then_inc(g_scaled, 1)
                each_unit(act, unit, False)

            by_rank(act, lambda: each_step(act, step, 6), general)

            act.wait_ge(consts_ready, 1)

            def norm_chunk(b, c):
                slot = c % 2
                lo, hi = (1 if c == 0 else 0), CHUNK_ROWS + (1 if c == CHUNKS - 1 else 2)
                act.wait_ge(chunk_landed[slot], b * (16 * CHUNKS) + (c - slot) * 16 + 32)
                flat = rawc[:, slot, lo:hi, :].rearrange("p r w -> p (r w)")
                nc.scalar.activation(flat, flat, ACT.Identity, bias=ln1ab[:, 1:2],
                                     scale=ln1ab[:, 0:1]).then_inc(chunk_normed, 1)

            def pair_chunk(b, c):
                slot, q = c % 2, b * CHUNKS + c
                lo, hi = (1 if c == 0 else 0), CHUNK_ROWS + (1 if c == CHUNKS - 1 else 2)
                act.wait_ge(chunk_normed, q + 1)
                if not (isinstance(b, int) and b == 0 and c < 2):
                    act.wait_ge(conv_done, (q - 1) * BLOCKS)
                nc.scalar.activation(paired[0:C, slot, lo:hi, 1:W + 1], rawc[0:C, slot, lo:hi, :],
                                     ACT.Copy).then_inc(pair_top, 1)

            def col_chunk(b, c):
                slot = c % 2
                rows = CHUNK_ROWS - (1 if c == CHUNKS - 1 else 0)
                nc.scalar.activation(col_pair[0:C, slot, 0:rows, 1:W], rawc[0:C, slot, 2:2 + rows, 0:W - 1],
                                     ACT.Copy).then_inc(col_lower, 1)

            def gate_block(b, i):
                n = b * SLOTS + i
                act.wait_ge(conv_done, n + 1)
                if not (isinstance(b, int) and b == 0 and i < 2):
                    act.wait_ge(gate_done, n - 1)
                nc.scalar.activation(t_gate[:, i % 2, :], bank[i % 3][C:P, :], ACT.Identity,
                                     bias=col_o[C:P, 2:3]).then_inc(tgate_ready, 1)

            def sqrt_var(n):
                act.wait_ge(var_ready, n + 1)
                nc.scalar.activation(lnt[:, 4:5], lnt[:, 3:4], ACT.Sqrt).then_inc(std_ready, 1)

            def gate_hi(b, j):
                if j >= 4:
                    act.wait_ge(pw2_done, b * TAIL + j - 3)
                nc.scalar.activation(part[:, j % 4, 0, :], gate[:, j * N:(j + 1) * N],
                                     ACT.Copy).then_inc(gate_hi_ready, 1)

            def x2_hi(b, j):
                act.wait_ge(x2_ready, b * TAIL + (TAIL if j < 2 else j + 1))
                if j >= 2:
                    act.wait_ge(u1_done, b * TAIL + j - 1)
                nc.scalar.activation(part[:, j % 2, 0, :], res[:, j * N:(j + 1) * N],
                                     ACT.Copy).then_inc(x2_hi_ready, 1)

            def ffn_block(b, j):
                n = b * TAIL + j
                if 1 <= j <= TAIL:
                    act.wait_ge(gate2_ready, n)
                    if j >= 3:
                        act.wait_ge(pw4_done, n - 2)
                    nc.scalar.activation(part[:, 2 + (j - 1) % 2, 0, :], gate2[:, (j - 1) % 2, :],
                                         ACT.Copy).then_inc(gate2_hi_ready, 1)
                if j < TAIL:
                    act.wait_ge(u2_done, n + 1)
                    if not (isinstance(b, int) and b == 0 and j < 2):
                        act.wait_ge(gate2_ready, n - 1)
                    nc.scalar.activation(t_gate2[:, j % 2, :], bank[5][:, :], ACT.Identity,
                                         bias=bias3[:, 1:2]).then_inc(tgate2_ready, 1)
                if j >= 3:
                    o = j - 3
                    act.wait_ge(sum_ready, n - 2)
                    nc.scalar.activation(t_out[:, o // 2 % 2, o % 2, :], t_out[:, o // 2 % 2, o % 2, :],
                                         ACT.Identity, bias=col[:, OUTB:OUTB + 1]).then_inc(outb_ready, 1)

            sqrt_var(0)
            act.wait_ge(ln1_ready, 1)
            norm_chunk(0, 0)
            act.wait_ge(pads_zeroed, 3)
            pair_chunk(0, 0)
            col_chunk(0, 0)
            norm_chunk(0, 1)

            def batch(b, conv, tail, nxt):
                for i in range(SLOTS):
                    if tail and i == 0:
                        act.wait_ge(gate_done, b * SLOTS)
                    if tail and i == 0:
                        for j in range(2):
                            gate_hi(b - 1, j)
                    if tail and i == 1:
                        for j in range(2, 4):
                            gate_hi(b - 1, j)
                    if tail and 0 <= i - FFN_AT + 1 < TAIL:
                        x2_hi(b - 1, i - FFN_AT + 1)
                    following = (b, i // BLOCKS + 1) if i < SPLIT_AT else (b + 1, 0)
                    if conv and i < SPLIT_AT or nxt and i >= SPLIT_AT:
                        if i % BLOCKS == 0:
                            pair_chunk(*following)
                        if i % BLOCKS == 1:
                            col_chunk(*following)
                    if nxt and i == LN1_AT + 2:
                        act.wait_ge(ln1_ready, b + 2)
                        norm_chunk(b + 1, 0)
                    if conv:
                        gate_block(b, i)
                    if tail and PW2_AT <= i < PW2_AT + TAIL // 2 - 2:
                        for j in range(2):
                            gate_hi(b - 1, 2 * (i - PW2_AT) + 4 + j)
                    if tail and i == 0:
                        act.wait_ge(sca_done, b)
                        nc.scalar.activation(attn[:, :], bank[7][:, 4:5], ACT.Sigmoid,
                                             bias=col[:, SCAB:SCAB + 1]).then_inc(attn_ready, 1)
                    if tail and i == LN2_AT + 1:
                        sqrt_var(ln2_index(b))
                    if tail and FFN_AT <= i < FFN_AT + TAIL + 3:
                        ffn_block(b - 1, i - FFN_AT)
                    c = i // BLOCKS + 2
                    if conv and i % BLOCKS == 2 and c < CHUNKS:
                        norm_chunk(b, c)
                    if nxt and i == LN1_AT + 1:
                        sqrt_var(b * 2 + 1)
                    if nxt and i == SPLIT_AT + 2:
                        norm_chunk(b + 1, 1)

            each_batch(act, batch)

        @block.vector
        def _(dve):
            made = [0]

            def prep(ins):
                made[0] += 1
                ins.then_inc(dve_prep, 1)
                dve.wait_ge(dve_prep, made[0])

            dve.wait_ge(filt_landed, 48)
            prep(nc.vector.memset(factor[:, :, :], 0.0))
            for f in range(2):
                c0 = filt[:, f, CENTRE, CENTRE:CENTRE + 1]
                prep(nc.vector.reciprocal(recip[:, f:f + 1], c0))
                prep(nc.vector.tensor_scalar(ratio[:, f, :, :], filt[:, f, :, :], recip[:, f:f + 1], None, ALU.mult))
                prep(nc.vector.tensor_tensor(
                    resid[:, f, :, :], ratio[:, f, :, CENTRE:CENTRE + 1].to_broadcast([P, TAPS, TAPS]),
                    ratio[:, f, CENTRE:CENTRE + 1, :].to_broadcast([P, TAPS, TAPS]), ALU.mult))
                prep(nc.vector.tensor_copy(factor[:, 2 * f, 1:TAPS + 1], filt[:, f, :, CENTRE]))
                prep(nc.vector.tensor_copy(factor[:, 2 * f + 1, 1:TAPS + 1], ratio[:, f, CENTRE, :]))
            prep(nc.vector.tensor_scalar(factor[:, 2, :], factor[:, 2, :], 0.5, None, ALU.mult))
            prep(nc.vector.tensor_scalar(factor[:, 3, :], factor[:, 3, :], 0.5 * GAIN, None, ALU.mult))
            prep(nc.vector.tensor_tensor(pairs[:, :, :], factor[:, :, 0:PAIRS], factor[:, :, 1:PAIRS + 1], ALU.add))
            prep(nc.vector.tensor_tensor(resid[:, :, :, :], ratio[:, :, :, :], resid[:, :, :, :], ALU.subtract))
            for t in (resid, ratio):
                prep(nc.vector.scalar_tensor_tensor(
                    out=t[:, :, :, :].rearrange("p f a b -> p (f a b)"),
                    in0=t[:, :, :, :].rearrange("p f a b -> p (f a b)"), scalar=-1.0,
                    in1=t[:, :, :, :].rearrange("p f a b -> p (f a b)"), op0=ALU.mult, op1=ALU.max))
            prep(nc.vector.scalar_tensor_tensor(
                out=resid[:, :, :, :].rearrange("p f a b -> p (f a b)"),
                in0=ratio[:, :, :, :].rearrange("p f a b -> p (f a b)"), scalar=RANK1_TOL,
                in1=resid[:, :, :, :].rearrange("p f a b -> p (f a b)"), op0=ALU.mult, op1=ALU.is_ge))
            prep(nc.vector.tensor_reduce(fits[:, 0:1], resid[:, :, :, :].rearrange("p f a b -> p (f a b)"),
                                         AX.X, ALU.min))
            prep(nc.vector.tensor_copy(is_rank1[:, :], fits[:, 0:1]))
            dve.sem_inc(rank_known, 1)
            dve.wait_ge(tap_index, 13)
            for a in range(2):
                for lo, hi, f in ((0, UP, 0), (UP, BAND, 1)):
                    for t in range(PAIRS):
                        ins = nc.vector.tensor_scalar(masked[:, t, lo:hi], tap_of[:, lo:hi], float(t),
                                                      pairs[:, 2 * f + a, t:t + 1], ALU.is_equal, ALU.mult)
                    prep(ins)
                prep(nc.vector.tensor_reduce(band[:, a, :], masked[:, :, :].rearrange("p t o -> p o t"),
                                             AX.X, ALU.add))
            prep(nc.vector.tensor_copy(band_hi[:, :, :], band[:, :, :]))
            prep(nc.vector.tensor_tensor(band_lo[:, :, :], band[:, :, :], band_hi[:, :, :], ALU.subtract))
            dve.sem_inc(bands_ready, 1)

            dve.wait_ge(pe_prep, 10)
            for s in range(2):
                own = slice(64 * s, 64 * s + 64)
                prep(nc.vector.tensor_scalar(wsca[:, own], bank[4][:, 0:C], 1.0 / HW, None, ALU.mult))
            before_paths = made[0]
            OUT_PARTS = 6

            def weights_out(n):
                if n == 0:
                    prep(nc.vector.memset(w_lo_last[:, :].bitcast(F32), 0.0))
                for t in (2 * n, 2 * n + 1):
                    if t < 9:
                        prep(nc.vector.tensor_copy(w_hi[:, t, :], tap_bank(t)))
                        lanes = slice(C, P) if t in (3, 4, 5, 7) else slice(0, C)
                        low = (w_lo_pair[lanes, t % 3, :] if t < 6 else w_lo_col[lanes, :] if t < 8
                               else w_lo_last[lanes, :])
                        prep(nc.vector.tensor_tensor(low, tap_bank(t)[lanes, :], w_hi[lanes, t, :], ALU.subtract))
                if n == 4:
                    prep(nc.vector.tensor_copy(corr[:, :], bank[7][:, P:2 * P]))
                    prep(nc.vector.tensor_copy(corr_part[:, :], corr[:, :]))
                    for first in (32, 64):
                        for at in range(first, 96, 32):
                            lanes = slice(at, at + 32)
                            prep(nc.vector.tensor_tensor(corr[lanes, :], corr[lanes, :], corr_part[lanes, :],
                                                         ALU.subtract))
                            prep(nc.vector.tensor_copy(corr_part[lanes, :], corr[lanes, :]))
                if n == 5:
                    for s in range(2):
                        lanes, own = slice(64 * s, 64 * s + 64), slice(64 * s, 64 * s + 64)
                        for o in range(2):
                            prep(nc.vector.tensor_copy(wbd3[lanes, o, own],
                                                       bank[7][lanes, 2 * P + C * o:2 * P + C * o + C]))
                        prep(nc.vector.tensor_copy(wbd2[lanes, own], bank[7][lanes, 3 * P:3 * P + C]))
                        prep(nc.vector.tensor_copy(wbd4[lanes, own], bank[7][lanes, 3 * P + C:4 * P]))
                    prep(nc.vector.tensor_copy(w4_part[:, 0, :], wbd4[:, :]))
                    prep(nc.vector.tensor_tensor(w4_part[:, 1, :], wbd4[:, :], w4_part[:, 0, :], ALU.subtract))
                    dve.wait_ge(vector_landed, 16 * 22)
                    prep(nc.vector.tensor_tensor(colsum[:, 1:2], col[:, PW2B:PW2B + 1], col[:, BETA1:BETA1 + 1],
                                                 ALU.mult))
                    prep(nc.vector.scalar_tensor_tensor(out=col[:, OUTB:OUTB + 1], in0=col[:, PW4B:PW4B + 1],
                                                        scalar=col[:, BETA2:BETA2 + 1], in1=colsum[:, 1:2],
                                                        op0=ALU.mult, op1=ALU.add))
                    dve.sem_inc(consts_ready, 1)

            def step(g, u, k, live):
                if live[2]:
                    h, par = g - 2, k % 2
                    dve.wait_ge(s1_hi_ready, h + 1)
                    nc.vector.tensor_tensor(s1_lo[:, par, :, :].rearrange("p m u -> p (m u)"), bank[0][:, :],
                                            s1_hi[:, par, :, :].rearrange("p m u -> p (m u)"),
                                            ALU.subtract).then_inc(s1_out, 1)
                if live[3]:
                    h, par = g - 3, (k - 3) % 2
                    for c in range(2):
                        dve.wait_ge(z_scaled, h * 2 + 1 + c)
                        zc = z[:, par, c, :, :].rearrange("p m u -> p (m u)")
                        nc.vector.tensor_tensor(zc, zc, bank[1 + c][:, :], ALU.max).then_inc(z_ready, 1)
                if live[4]:
                    h, par = g - 4, k % 2
                    dve.wait_ge(s3_hi_ready, h + 1)
                    nc.vector.tensor_tensor(s3_lo[:, par, :, :].rearrange("p r n -> p (r n)"), bank[3][:, :],
                                            s3_hi[:, par, :, :].rearrange("p r n -> p (r n)"),
                                            ALU.subtract).then_inc(s3_out, 1)
                if live[5]:
                    h, kk = g - 5, (k - 5) % 4
                    slot, pos = kk // 2, 2 * (kk % 2)
                    dve.wait_ge(s4_done, h + 1)
                    if kk % 2 == 0 and not (isinstance(h, int) and h < 4):
                        dve.wait_ge(y_stored[slot], (h - kk) * 4)
                    nc.vector.tensor_copy(y[:, slot, pos:pos + 2, :].rearrange("p m w -> p (m w)"),
                                          bank[4][:, 0:2 * W]).then_inc(y_ready, 1)

            def general():
                made2 = [0]

                def link(ins):
                    made2[0] += 1
                    ins.then_inc(g_chain, 1)
                    dve.wait_ge(g_chain, made2[0])

                link(nc.vector.memset(filt_pad[:, :, :, :], 0.0))
                for f in range(2):
                    link(nc.vector.tensor_copy(filt_pad[:, f, 1:TAPS + 1, 1:TAPS + 1], filt[:, f, :, :]))
                    link(nc.vector.tensor_tensor(pairs1[:, f, :, :], filt_pad[:, f, 0:PAIRS, :],
                                                 filt_pad[:, f, 1:PAIRS + 1, :], ALU.add))
                    link(nc.vector.tensor_tensor(pairs2[:, f, :, :], pairs1[:, f, :, 0:PAIRS],
                                                 pairs1[:, f, :, 1:PAIRS + 1], ALU.add))
                link(nc.vector.tensor_scalar(pairs2[:, 1, :, :], pairs2[:, 1, :, :], 0.25 * GAIN, None, ALU.mult))
                for f in range(2):
                    for s in range(PAIRS):
                        for t in range(PAIRS):
                            ins = nc.vector.tensor_scalar(masked2[:, t, :], tap_of[:, f * UP:(f + 1) * UP],
                                                          float(t), pairs2[:, f, t, s:s + 1],
                                                          ALU.is_equal, ALU.mult)
                        link(ins)
                        link(nc.vector.tensor_reduce(band2[:, s, f * UP:(f + 1) * UP],
                                                     masked2[:, :, :].rearrange("p t o -> p o t"), AX.X, ALU.add))
                dve.sem_inc(g_bands, 1)

                def unit(u, slot, now, before):
                    if now:
                        for n in range(4):
                            q, h = n // 2, n % 2
                            dve.wait_ge(g_scaled, u * 4 + n + 1)
                            zz = z_pad[:, slot, q, h, :, 3:3 + W]
                            nc.vector.tensor_tensor(zz, zz, bank[n][:, :].rearrange("p (m w) -> p m w", w=W),
                                                    ALU.max).then_inc(g_z_ready, 1)
                    if before:
                        dve.wait_ge(g_down_done, u)
                        if not (isinstance(u, int) and u < 3):
                            dve.wait_ge(g_stored[1 - slot], (u + slot) * 8 - 16)
                        nc.vector.tensor_copy(y2[:, 1 - slot, :, :].rearrange("p m w -> p (m w)"),
                                              bank[4][:, :]).then_inc(g_y_ready, 1)
                each_unit(dve, unit, True)

            def bn_first(j):
                if j == 0:
                    dve.wait_ge(first_landed, 32)
                nc.vector.bn_stats(stats1[:, j, :], gate[:, j * N:(j + 1) * N]).then_inc(bn1_done, 1)

            def separable():
                def step_and_stats(g, u, k, live):
                    step(g, u, k, live)
                    if isinstance(g, int) and 2 <= g < 2 + OUT_PARTS:
                        weights_out(g - 2)
                    if isinstance(g, int) and g >= STEPS:
                        for j in range(4 * (g - STEPS), min(4 * (g - STEPS) + 4, TAIL)):
                            bn_first(j)
                each_step(dve, step_and_stats, 6)

            def general_and_stats():
                made[0] = before_paths
                for n in range(OUT_PARTS):
                    weights_out(n)
                general()
                for j in range(TAIL):
                    bn_first(j)

            by_rank(dve, separable, general_and_stats)

            CHAIN = 9

            def halves_stats(n, stats):
                dve.sem_inc(stats_made, 1)
                nc.vector.bn_aggr(mv[:, :], stats[:, :, :].rearrange("p a b -> p (a b)")).then_inc(mv_ready, 1)

            def norm_coefs(n, w, b_, ab, ready):
                count = [0]

                def link(ins):
                    count[0] += 1
                    ins.then_inc(ln_chain, 1)
                    dve.wait_ge(ln_chain, n * CHAIN + count[0])

                dve.wait_ge(mv_ready, n + 1)
                dve.wait_ge(mv_swapped, n + 1)
                link(nc.vector.tensor_tensor(lnt[:, 0:2], mv[:, :], bank[7][:, 0:2], ALU.add))
                link(nc.vector.tensor_tensor(lnt[:, 2:3], mv[:, 0:1], bank[7][:, 0:1], ALU.subtract))
                link(nc.vector.tensor_scalar(lnt[:, 2:3], lnt[:, 2:3], lnt[:, 2:3], 0.25, ALU.mult, ALU.mult))
                link(nc.vector.tensor_scalar(lnt[:, 1:2], lnt[:, 1:2], 0.5, LN_EPS, ALU.mult, ALU.add))
                nc.vector.tensor_tensor(lnt[:, 3:4], lnt[:, 1:2], lnt[:, 2:3], ALU.add).then_inc(var_ready, 1)
                dve.wait_ge(std_ready, n + 1)
                link(nc.vector.reciprocal(lnt[:, 5:6], lnt[:, 4:5]))
                link(nc.vector.tensor_tensor(ab[:, 0:1], lnt[:, 5:6], col[:, w:w + 1], ALU.mult))
                link(nc.vector.tensor_scalar(lnt[:, 6:7], lnt[:, 0:1], -0.5, None, ALU.mult))
                link(nc.vector.tensor_tensor(lnt[:, 6:7], lnt[:, 6:7], ab[:, 0:1], ALU.mult))
                link(nc.vector.tensor_tensor(ab[:, 1:2], lnt[:, 6:7], col[:, b_:b_ + 1], ALU.add))
                dve.sem_inc(ready, 1)

            def bn1(b, j):
                slot = j // 2 % 2
                if j % 2 == 0:
                    dve.wait_ge(stage_landed[slot], (b - 1) * (8 * TAIL) + (j // 4 + 1) * 32)
                nc.vector.bn_stats(stats1[:, j, :], stage[:, slot, j % 2 * N:(j % 2 + 1) * N]
                                   ).then_inc(bn1_done, 1)

            def split_chunk(b, c):
                slot, q = c % 2, b * CHUNKS + c
                lo, hi = (1 if c == 0 else 0), CHUNK_ROWS + (1 if c == CHUNKS - 1 else 2)
                if not (isinstance(b, int) and b == 0 and c < 2):
                    dve.wait_ge(conv_done, (q - 1) * BLOCKS)
                if c == 0:
                    nc.vector.memset(split[:, slot, 0, :].bitcast(F32), 0.0)
                    nc.vector.memset(paired[0:C, slot, 0, :].bitcast(F32), 0.0)
                if c == CHUNKS - 1:
                    nc.vector.memset(split[:, slot, CHUNK_ROWS + 1, :].bitcast(F32), 0.0)
                    nc.vector.memset(paired[0:C, slot, CHUNK_ROWS + 1, :].bitcast(F32), 0.0)
                    nc.vector.memset(paired[C:P, slot, CHUNK_ROWS, :].bitcast(F32), 0.0)
                    nc.vector.memset(col_pair[:, slot, CHUNK_ROWS - 1, :].bitcast(F32), 0.0)
                dve.wait_ge(chunk_normed, q + 1)
                nc.vector.tensor_copy(split[:, slot, lo:hi, 1:W + 1], rawc[:, slot, lo:hi, :]).then_inc(split_hi, 1)

            def pair_chunk(b, c):
                slot, q = c % 2, b * CHUNKS + c
                hi = CHUNK_ROWS + (1 if c == CHUNKS - 1 else 2)
                nc.vector.tensor_copy(paired[C:P, slot, 0:hi - 1, 1:W + 1],
                                      rawc[C:P, slot, 1:hi, :]).then_inc(pair_bottom, 1)
                rows = CHUNK_ROWS - (1 if c == CHUNKS - 1 else 0)
                nc.vector.tensor_copy(col_pair[C:P, slot, 0:rows, :],
                                      rawc[C:P, slot, 2:2 + rows, :]).then_inc(col_upper, 1)

            def gate_block(b, i, tail):
                n = b * SLOTS + i
                half, at = i // TAIL, i % TAIL
                dve.wait_ge(tgate_ready, n + 1)
                if tail and half == 0:
                    dve.wait_ge(gate_parts, (b - 1) * TAIL + at + 1)
                lanes = slice(64 * half, 64 * half + 64)
                nc.vector.scalar_tensor_tensor(
                    out=gate[lanes, at * N:(at + 1) * N], in0=bank[i % 3][0:C, :], scalar=col_o[0:C, 2:3],
                    in1=t_gate[:, i % 2, :], op0=ALU.add, op1=ALU.mult,
                    accum_out=gsum[lanes, at:at + 1]).then_inc(gate_done, 1)

            def pw2_pair(b, j0):
                for j in (j0, j0 + 1):
                    n = b * TAIL + j
                    dve.wait_ge(pw2_done, n + 1)
                    if j % 4 == 0:
                        dve.wait_ge(res_landed[j // 4], b * 32 + 32)
                    xb = res[:, j * N:(j + 1) * N]
                    nc.vector.scalar_tensor_tensor(out=xb, in0=bank[3 + j % 2][:, :],
                                                   scalar=col[:, BETA1:BETA1 + 1], in1=xb,
                                                   op0=ALU.mult, op1=ALU.add).then_inc(x2_ready, 1)
                for j in (j0, j0 + 1):
                    dve.wait_ge(x2_ready, b * TAIL + j + 1)
                    nc.vector.bn_stats(stats2[:, j, :], res[:, j * N:(j + 1) * N]).then_inc(bn2_done, 1)

            def gate_ffn(b, j):
                n = b * TAIL + j
                dve.wait_ge(tgate2_ready, n + 1)
                dve.wait_ge(u1_done, n + 1)
                if not (isinstance(b, int) and b == 0 and j < 2):
                    dve.wait_ge(gate2_parts, n - 1)
                nc.vector.scalar_tensor_tensor(out=gate2[:, j % 2, :], in0=bank[6][:, :],
                                               scalar=bias3[:, 0:1], in1=t_gate2[:, j % 2, :],
                                               op0=ALU.add, op1=ALU.mult).then_inc(gate2_ready, 1)

            def gate_ffn_lo(b, j):
                dve.wait_ge(gate2_hi_ready, b * TAIL + j + 1)
                nc.vector.tensor_tensor(part[:, 2 + j % 2, 1, :], gate2[:, j % 2, :],
                                        part[:, 2 + j % 2, 0, :], ALU.subtract).then_inc(gate2_parts, 1)

            def add_ffn(b, o):
                slot = o // 2 % 2
                dve.wait_ge(pw4_done, b * TAIL + o + 1)
                if o % 2 == 0 and not (isinstance(b, int) and b == 0 and o < 4):
                    dve.wait_ge(out_stored[slot], b * (8 * TAIL) + o // 4 * 32)
                nc.vector.scalar_tensor_tensor(out=t_out[:, slot, o % 2, :], in0=bank[3 + o % 2][:, :],
                                               scalar=col[:, BETA2:BETA2 + 1],
                                               in1=res[:, o * N:(o + 1) * N],
                                               op0=ALU.mult, op1=ALU.add).then_inc(sum_ready, 1)

            dve.wait_ge(bn1_done, TAIL)
            halves_stats(0, stats1)
            norm_coefs(0, LN1W, LN1B, ln1ab, ln1_ready)
            dve.wait_ge(pads_zeroed, 3)
            split_chunk(0, 0)
            pair_chunk(0, 0)

            def batch(b, conv, tail, nxt):
                for i in range(SLOTS):
                    if tail and 0 <= i - FFN_AT - 1 < TAIL:
                        gate_ffn(b - 1, i - FFN_AT - 1)
                    following = (b, i // BLOCKS + 1) if i < SPLIT_AT else (b + 1, 0)
                    if conv and i < SPLIT_AT or nxt and i >= SPLIT_AT:
                        if i % BLOCKS == 0:
                            split_chunk(*following)
                        if i % BLOCKS == 1:
                            pair_chunk(*following)
                    if tail and i == 0:
                        dve.wait_ge(attn_ready, b)
                        nc.vector.tensor_scalar(wbd2_b[:, :], wbd2[:, :], attn[:, :], None,
                                                ALU.mult).then_inc(w2_ready, 1)
                        dve.wait_ge(w2_ready, 3 * b - 2)
                        nc.vector.tensor_copy(w2_part[:, 0, :], wbd2_b[:, :]).then_inc(w2_ready, 1)
                        dve.wait_ge(w2_ready, 3 * b - 1)
                        nc.vector.tensor_tensor(w2_part[:, 1, :], wbd2_b[:, :], w2_part[:, 0, :],
                                                ALU.subtract).then_inc(w2_ready, 1)
                    if conv:
                        gate_block(b, i, tail)
                    if nxt and BN1_AT <= i < BN1_AT + TAIL:
                        bn1(b + 1, i - BN1_AT)
                    if tail and PW2_AT <= i < LN2_AT:
                        pw2_pair(b - 1, 2 * (i - PW2_AT))
                    if tail and i == LN2_AT:
                        dve.wait_ge(bn2_done, b * TAIL)
                        halves_stats(ln2_index(b), stats2)
                    if tail and i == LN2_AT + 1:
                        norm_coefs(ln2_index(b), LN2W, LN2B, ln2ab, ln2_ready)
                    if tail and i == LN2_AT + 2:
                        for o in range(2):
                            nc.vector.tensor_scalar(wbd3_b[:, o, :], wbd3[:, o, :], ln2ab[:, 0:1], None, ALU.mult)
                        dve.wait_ge(b3_done, b)
                        nc.vector.tensor_tensor(bias3[:, :], bank[7][:, 8:10], col[:, PW3B1:PW3B2 + 1],
                                                ALU.add).then_inc(w3_ready, 1)
                        dve.wait_ge(w3_ready, 3 * b - 2)
                        nc.vector.tensor_copy(w3_part[:, 0, :, :], wbd3_b[:, :, :]).then_inc(w3_ready, 1)
                        dve.wait_ge(w3_ready, 3 * b - 1)
                        nc.vector.tensor_tensor(w3_part[:, 1, :, :], wbd3_b[:, :, :], w3_part[:, 0, :, :],
                                                ALU.subtract).then_inc(w3_ready, 1)
                    if tail and 0 <= i - FFN_AT - 2 < TAIL:
                        add_ffn(b - 1, i - FFN_AT - 2)
                    if tail and not conv and 0 <= i - FFN_AT - 1 < TAIL:
                        gate_ffn_lo(b - 1, i - FFN_AT - 1)
                    if nxt and i == LN1_AT:
                        dve.wait_ge(bn1_done, (b + 2) * TAIL)
                        halves_stats(b * 2 + 1, stats1)
                    if nxt and i == LN1_AT + 1:
                        norm_coefs(b * 2 + 1, LN1W, LN1B, ln1ab, ln1_ready)
                if conv:
                    dve.wait_ge(gate_done, (b + 1) * SLOTS)
                    nc.vector.tensor_reduce(gtot[:, :], gsum[:, :], AX.X, ALU.add).then_inc(gtot_ready, 1)

            each_batch(dve, batch)


NAMES = ["x", "L0_conv_bias", "L0_conv_up_filter", "L0_conv_dn_filter", "L1_conv_ln1_w", "L1_conv_ln1_b",
         "L1_conv_pw1_w", "L1_conv_pw1_b", "L1_conv_dw_w", "L1_conv_dw_b", "L1_conv_sca_w", "L1_conv_sca_b",
         "L1_conv_pw2_w", "L1_conv_pw2_b", "L1_conv_ln2_w", "L1_conv_ln2_b", "L1_conv_pw3_w",
         "L1_conv_pw3_b", "L1_conv_pw4_w", "L1_conv_pw4_b", "L1_conv_beta1", "L1_conv_beta2"]


def kernel(**inputs):
    import numpy as np
    import concourse.bacc as bacc
    from concourse.bass_utils import run_bass_kernel_spmd

    nc = bacc.Bacc("TRN2", target_bir_lowering=False, num_devices=1)
    arrays, args = {}, []
    for name in NAMES:
        a = np.ascontiguousarray(inputs[name])
        arrays[f"in_{name}"] = a
        args.append(nc.dram_tensor(f"in_{name}", a.shape, mybir.dt.from_np(a.dtype), kind="ExternalInput").ap())
    shape = inputs["x"].shape
    args.append(nc.dram_tensor("out_y", shape, F32, kind="ExternalOutput").ap())
    build(nc, *args)
    results = run_bass_kernel_spmd(nc, [arrays], core_ids=[0])
    return results.results[0]["out_y"]
```
